# Optimizing a Trainium2 kernel written in Bass

```python
import numpy as np
import jax
import jax.numpy as jnp

def _softmax(x, axis=-1):
    return jax.nn.softmax(x, axis=axis)

def _gelu(x):
    return jax.nn.gelu(x, approximate=True)

def _silu(x):
    return jax.nn.silu(x)

def _sigmoid(x):
    return jax.nn.sigmoid(x)

def _layernorm(x, axis=-1, eps=1e-05):
    m = jnp.mean(x, axis=axis, keepdims=True)
    v = jnp.var(x, axis=axis, keepdims=True)
    return (x - m) / jnp.sqrt(v + eps)

def _scatter_add(tgt, idx, src, axis=0):
    return tgt.at[idx].add(src)

def _segment_sum(src, seg, n):
    return jax.ops.segment_sum(src, seg, n)
kernel_name = 'mk_adaln_d2_jaxref_r4_2e361e'

def setup_inputs(seed: int=0):
    np.random.seed(seed)
    _w = jnp.asarray

    def _L0_attn_setup():
        import jax, jax.numpy as jnp
        import numpy as np
        EPS = 1.1920929e-07
        NUM_HEADS = 16
        SOFTCAP = 50.0

        def rms_norm(x):
            return x * jax.lax.rsqrt(jnp.mean(x * x, axis=-1, keepdims=True) + EPS)
        key = jax.random.key(seed)
        ks = jax.random.split(key, 5)
        B, S, D = (2, 512, 256)
        x = jax.random.normal(ks[0], (B, S, D), dtype=jnp.float32)
        w_q = jax.random.normal(ks[1], (D, D), dtype=jnp.float32) * 0.02
        w_k = jax.random.normal(ks[2], (D, D), dtype=jnp.float32) * 0.02
        w_v = jax.random.normal(ks[3], (D, D), dtype=jnp.float32) * 0.02
        w_o = jax.random.normal(ks[4], (D, D), dtype=jnp.float32) * 0.02
        return {'x': x, 'w_q': w_q, 'w_k': w_k, 'w_v': w_v, 'w_o': w_o}
    _L0_attn_in = _L0_attn_setup()

    def _L0_ffn_setup():
        import math
        import jax, jax.numpy as jnp
        import numpy as np
        B, T, D = (4, 1024, 256)
        H = 16
        HD = D // H
        CAP = int(1024 * 0.125)
        DFF = int(D * 4 * 2 / 3)
        EPS = 1e-06

        def rmsnorm(x, g):
            return x * jax.lax.rsqrt(jnp.mean(x * x, axis=-1, keepdims=True) + EPS) * g
        key = jax.random.key(seed)
        ks = jax.random.split(key, 9)
        s = lambda k, shape: jax.random.normal(k, shape, jnp.float32) * 0.02
        return {'x': jax.random.normal(ks[0], (B, T, D), jnp.float32), 'w_router': s(ks[1], (D,)), 'W_qkv': s(ks[2], (3 * D, D)), 'W_out': s(ks[3], (D, D)), 'g1': jnp.ones((D,), jnp.float32), 'g2': jnp.ones((D,), jnp.float32), 'W1': s(ks[4], (DFF, D)), 'W2': s(ks[5], (DFF, D)), 'W3': s(ks[6], (D, DFF))}
    _L0_ffn_in = _L0_ffn_setup()
    _L0_c = _w((lambda *s: np.random.randn(*s).astype(np.float32) * 0.05)(8, 256))
    _L0_wmod = _w((lambda *s: np.random.randn(*s).astype(np.float32) * 0.05)(256, 6 * 256) * 256 ** (-0.5))

    def _L1_attn_setup():
        import jax, jax.numpy as jnp
        import numpy as np
        import math
        B, T, C, D = (8, 512, 256, 256)
        N_LAYER, LAYER_ID = (24, 12)

        def _wkv(time_decay, time_first, k, v):
            ew = jnp.exp(-jnp.exp(time_decay))
            eu = jnp.exp(time_first)
            ek = jnp.exp(k)
            ekv = ek * v

            def step(carry, inp):
                a, b = carry
                ekt, ekvt = inp
                out = (eu * ekvt + a) / (eu * ekt + b)
                return ((ew * a + ekvt, ew * b + ekt), out)
            init = (jnp.zeros_like(ek[:, 0]), jnp.zeros_like(ek[:, 0]))
            xs = (jnp.swapaxes(ek, 0, 1), jnp.swapaxes(ekv, 0, 1))
            _, out = jax.lax.scan(step, init, xs)
            return jnp.swapaxes(out, 0, 1)
        key = jax.random.key(seed)
        ks = jax.random.split(key, 5)
        r01 = LAYER_ID / (N_LAYER - 1)
        r10 = 1.0 - LAYER_ID / N_LAYER
        ddd = np.arange(C, dtype=np.float64) / C
        h = np.arange(D, dtype=np.float64)
        decay_speed = -5 + 8 * (h / (D - 1)) ** (0.7 + 1.3 * r01)
        zigzag = ((np.arange(D) + 1) % 3 - 1) * 0.5
        time_first = np.log(0.3) + zigzag
        scale = C ** (-0.5)
        return {'x': jax.random.normal(ks[0], (B, T, C), jnp.float32), 'time_decay': jnp.asarray(decay_speed, jnp.float32), 'time_first': jnp.asarray(time_first, jnp.float32), 'time_mix_k': jnp.asarray(ddd ** r10, jnp.float32), 'time_mix_v': jnp.asarray(ddd ** r10 + 0.3 * r01, jnp.float32), 'time_mix_r': jnp.asarray(ddd ** (0.5 * r10), jnp.float32), 'Wk': jax.random.normal(ks[1], (D, C), jnp.float32) * scale, 'Wv': jax.random.normal(ks[2], (D, C), jnp.float32) * scale, 'Wr': jax.random.normal(ks[3], (D, C), jnp.float32) * scale, 'Wo': jax.random.normal(ks[4], (C, D), jnp.float32) * scale}
    _L1_attn_in = _L1_attn_setup()

    def _L1_ffn_setup():
        import jax, jax.numpy as jnp
        import numpy as np
        HIDDEN = 256
        NUM_EXPERTS = 8
        CAPACITY_FACTOR = 1.25
        key = jax.random.key(seed)
        k_tok, k_g, k_w1, k_b1, k_w2, k_b2 = jax.random.split(key, 6)
        B, S, H, E = (4, 512, HIDDEN, NUM_EXPERTS)
        tokens = jax.random.normal(k_tok, (B, S, H), dtype=jnp.float32)
        gate_w = jax.random.normal(k_g, (E, H), dtype=jnp.float32) * 0.02
        W1 = jax.random.normal(k_w1, (E, H, H), dtype=jnp.float32) * 0.02
        b1 = jax.random.normal(k_b1, (E, H), dtype=jnp.float32) * 0.02
        W2 = jax.random.normal(k_w2, (E, H, H), dtype=jnp.float32) * 0.02
        b2 = jax.random.normal(k_b2, (E, H), dtype=jnp.float32) * 0.02
        return {'tokens': tokens, 'gate_w': gate_w, 'W1': W1, 'b1': b1, 'W2': W2, 'b2': b2}
    _L1_ffn_in = _L1_ffn_setup()
    _L1_c = _w((lambda *s: np.random.randn(*s).astype(np.float32) * 0.05)(8, 256))
    _L1_wmod = _w((lambda *s: np.random.randn(*s).astype(np.float32) * 0.05)(256, 6 * 256) * 256 ** (-0.5))
    _d = {'L0_attn_x': _L0_attn_in['x'], 'L0_attn_w_q': _L0_attn_in['w_q'], 'L0_attn_w_k': _L0_attn_in['w_k'], 'L0_attn_w_v': _L0_attn_in['w_v'], 'L0_attn_w_o': _L0_attn_in['w_o'], 'L0_ffn_w_router': _L0_ffn_in['w_router'], 'L0_ffn_W_qkv': _L0_ffn_in['W_qkv'], 'L0_ffn_W_out': _L0_ffn_in['W_out'], 'L0_ffn_g1': _L0_ffn_in['g1'], 'L0_ffn_g2': _L0_ffn_in['g2'], 'L0_ffn_W1': _L0_ffn_in['W1'], 'L0_ffn_W2': _L0_ffn_in['W2'], 'L0_ffn_W3': _L0_ffn_in['W3'], 'L0_c': _L0_c, 'L0_wmod': _L0_wmod, 'L1_attn_time_decay': _L1_attn_in['time_decay'], 'L1_attn_time_first': _L1_attn_in['time_first'], 'L1_attn_time_mix_k': _L1_attn_in['time_mix_k'], 'L1_attn_time_mix_v': _L1_attn_in['time_mix_v'], 'L1_attn_time_mix_r': _L1_attn_in['time_mix_r'], 'L1_attn_Wk': _L1_attn_in['Wk'], 'L1_attn_Wv': _L1_attn_in['Wv'], 'L1_attn_Wr': _L1_attn_in['Wr'], 'L1_attn_Wo': _L1_attn_in['Wo'], 'L1_ffn_gate_w': _L1_ffn_in['gate_w'], 'L1_ffn_W1': _L1_ffn_in['W1'], 'L1_ffn_b1': _L1_ffn_in['b1'], 'L1_ffn_W2': _L1_ffn_in['W2'], 'L1_ffn_b2': _L1_ffn_in['b2'], 'L1_c': _L1_c, 'L1_wmod': _L1_wmod}
    _x0 = _d['L0_attn_x']
    _d['L0_attn_x'] = jax.random.normal(jax.random.fold_in(jax.random.key(seed), 1), (8, 1024, 256), dtype=_x0.dtype)
    del _x0
    return _d

def reference(L0_attn_x, L0_attn_w_q, L0_attn_w_k, L0_attn_w_v, L0_attn_w_o, L0_ffn_w_router, L0_ffn_W_qkv, L0_ffn_W_out, L0_ffn_g1, L0_ffn_g2, L0_ffn_W1, L0_ffn_W2, L0_ffn_W3, L0_c, L0_wmod, L1_attn_time_decay, L1_attn_time_first, L1_attn_time_mix_k, L1_attn_time_mix_v, L1_attn_time_mix_r, L1_attn_Wk, L1_attn_Wv, L1_attn_Wr, L1_attn_Wo, L1_ffn_gate_w, L1_ffn_W1, L1_ffn_b1, L1_ffn_W2, L1_ffn_b2, L1_c, L1_wmod):

    def _L0_attn_ref(x, w_q, w_k, w_v, w_o):
        import jax, jax.numpy as jnp
        import numpy as np
        EPS = 1.1920929e-07
        NUM_HEADS = 16
        SOFTCAP = 50.0

        def rms_norm(x):
            return x * jax.lax.rsqrt(jnp.mean(x * x, axis=-1, keepdims=True) + EPS)
        B, S, D = x.shape
        H = NUM_HEADS
        dk = D // H

        def split_heads(y):
            return y.reshape(B, S, H, dk).transpose(0, 2, 1, 3)
        q = split_heads(x @ w_q.T)
        k = split_heads(x @ w_k.T)
        v = split_heads(x @ w_v.T)
        q = rms_norm(q)
        k = rms_norm(k)
        scores = jnp.einsum('bhqd,bhkd->bhqk', q, k) / jnp.sqrt(jnp.float32(dk))
        scores = jnp.tanh(scores / SOFTCAP) * SOFTCAP
        causal = jnp.tril(jnp.ones((S, S), dtype=bool))
        scores = jnp.where(causal[None, None], scores, -jnp.inf)
        probs = jax.nn.softmax(scores, axis=-1)
        y = jnp.einsum('bhqk,bhkd->bhqd', probs, v)
        y = y.transpose(0, 2, 1, 3).reshape(B, S, D)
        return y @ w_o.T

    def _L0_ffn_ref(x, w_router, W_qkv, W_out, g1, g2, W1, W2, W3):
        import math
        import jax, jax.numpy as jnp
        import numpy as np
        B, T, D = (4, 1024, 256)
        H = 16
        HD = D // H
        CAP = int(1024 * 0.125)
        DFF = int(D * 4 * 2 / 3)
        EPS = 1e-06

        def rmsnorm(x, g):
            return x * jax.lax.rsqrt(jnp.mean(x * x, axis=-1, keepdims=True) + EPS) * g
        Bq, Tq, Dq = x.shape
        scores = x @ w_router
        _, idx = jax.lax.top_k(scores, CAP)
        x_sel = jnp.take_along_axis(x, idx[:, :, None], axis=1)
        h = rmsnorm(x_sel, g1)
        qkv = (h @ W_qkv.T).reshape(Bq, CAP, 3, H, HD)
        q, k, v = jnp.moveaxis(qkv, 2, 0)
        att = jnp.einsum('bqhd,bkhd->bhqk', q, k) / math.sqrt(HD)
        mask = jnp.triu(jnp.ones((CAP, CAP), bool), 1)
        att = jnp.where(mask, -jnp.inf, att)
        att = jax.nn.softmax(att, axis=-1)
        o = jnp.einsum('bhqk,bkhd->bqhd', att, v).reshape(Bq, CAP, Dq)
        x_attn = o @ W_out.T
        h2 = rmsnorm(x_sel + x_attn, g2)
        x_ff = jax.nn.silu(h2 @ W1.T) * (h2 @ W2.T) @ W3.T
        x_proc = x_sel + x_attn + x_ff
        out = x.at[jnp.arange(Bq)[:, None], idx].set(x_proc)
        return out

    def _L1_attn_ref(x, time_decay, time_first, time_mix_k, time_mix_v, time_mix_r, Wk, Wv, Wr, Wo):
        import jax, jax.numpy as jnp
        import numpy as np
        import math
        B, T, C, D = (8, 512, 256, 256)
        N_LAYER, LAYER_ID = (24, 12)

        def _wkv(time_decay, time_first, k, v):
            ew = jnp.exp(-jnp.exp(time_decay))
            eu = jnp.exp(time_first)
            ek = jnp.exp(k)
            ekv = ek * v

            def step(carry, inp):
                a, b = carry
                ekt, ekvt = inp
                out = (eu * ekvt + a) / (eu * ekt + b)
                return ((ew * a + ekvt, ew * b + ekt), out)
            init = (jnp.zeros_like(ek[:, 0]), jnp.zeros_like(ek[:, 0]))
            xs = (jnp.swapaxes(ek, 0, 1), jnp.swapaxes(ekv, 0, 1))
            _, out = jax.lax.scan(step, init, xs)
            return jnp.swapaxes(out, 0, 1)
        xx = jnp.pad(x, ((0, 0), (1, 0), (0, 0)))[:, :-1]
        xk = x * time_mix_k + xx * (1 - time_mix_k)
        xv = x * time_mix_v + xx * (1 - time_mix_v)
        xr = x * time_mix_r + xx * (1 - time_mix_r)
        k = jnp.einsum('btc,dc->btd', xk, Wk)
        v = jnp.einsum('btc,dc->btd', xv, Wv)
        sr = jax.nn.sigmoid(jnp.einsum('btc,dc->btd', xr, Wr))
        rwkv = sr * _wkv(time_decay, time_first, k, v)
        return jnp.einsum('btd,cd->btc', rwkv, Wo)

    def _L1_ffn_ref(tokens, gate_w, W1, b1, W2, b2):
        import jax, jax.numpy as jnp
        import numpy as np
        HIDDEN = 256
        NUM_EXPERTS = 8
        CAPACITY_FACTOR = 1.25
        B, S, H = tokens.shape
        E = gate_w.shape[0]
        T = B * S
        x = tokens.reshape(T, H)
        logits = x @ gate_w.T
        probs = jax.nn.softmax(logits, axis=-1)
        top2_w, top2_idx = jax.lax.top_k(probs, 2)
        cap = int(CAPACITY_FACTOR * T / E)
        counts = jnp.bincount(top2_idx.reshape(-1), length=E)
        keep = (counts <= cap).astype(x.dtype)
        comb = jnp.zeros((T, E), dtype=x.dtype).at[jnp.arange(T)[:, None], top2_idx].add(top2_w)
        comb = comb * keep[None, :]
        h = jax.nn.relu(jnp.einsum('th,ehf->tef', x, W1) + b1[None, :, :])
        y = jnp.einsum('teh,ehf->tef', h, W2) + b2[None, :, :]
        out = jnp.einsum('te,tef->tf', comb, y)
        return out.reshape(B, S, H)
    x = L0_attn_x
    mod = (_silu(L0_c) @ L0_wmod).reshape(L0_c.shape[0], 6, 1, -1)
    sa, ca, ga, sb, cb, gb = (mod[:, 0], mod[:, 1], mod[:, 2], mod[:, 3], mod[:, 4], mod[:, 5])
    ga = (2 * (ga >= 0) - 1) * jnp.maximum(jnp.abs(ga), 0.25)
    gb = (2 * (gb >= 0) - 1) * jnp.maximum(jnp.abs(gb), 0.25)
    h = _layernorm(x, axis=-1) * (1 + ca) + sa
    x = x + ga * _L0_attn_ref(h, L0_attn_w_q, L0_attn_w_k, L0_attn_w_v, L0_attn_w_o)
    h = _layernorm(x, axis=-1) * (1 + cb) + sb
    x = x + gb * _L0_ffn_ref(h, L0_ffn_w_router, L0_ffn_W_qkv, L0_ffn_W_out, L0_ffn_g1, L0_ffn_g2, L0_ffn_W1, L0_ffn_W2, L0_ffn_W3)
    mod = (_silu(L1_c) @ L1_wmod).reshape(L1_c.shape[0], 6, 1, -1)
    sa, ca, ga, sb, cb, gb = (mod[:, 0], mod[:, 1], mod[:, 2], mod[:, 3], mod[:, 4], mod[:, 5])
    ga = (2 * (ga >= 0) - 1) * jnp.maximum(jnp.abs(ga), 0.25)
    gb = (2 * (gb >= 0) - 1) * jnp.maximum(jnp.abs(gb), 0.25)
    h = _layernorm(x, axis=-1) * (1 + ca) + sa
    x = x + ga * _L1_attn_ref(h, L1_attn_time_decay, L1_attn_time_first, L1_attn_time_mix_k, L1_attn_time_mix_v, L1_attn_time_mix_r, L1_attn_Wk, L1_attn_Wv, L1_attn_Wr, L1_attn_Wo)
    h = _layernorm(x, axis=-1) * (1 + cb) + sb
    x = x + gb * _L1_ffn_ref(h, L1_ffn_gate_w, L1_ffn_W1, L1_ffn_b1, L1_ffn_W2, L1_ffn_b2)
    return x

_drawn_inputs = setup_inputs


def setup_inputs(seed=0):
    import zlib

    import numpy as np

    out = dict(_drawn_inputs(seed))
    spreads = {'L0_ffn_g1': (1.0, 0.6), 'L0_ffn_g2': (1.0, 0.6)}
    factors = {'L0_attn_w_q': 8.0,
     'L0_attn_w_k': 8.0,
     'L0_attn_w_v': 8.0,
     'L0_attn_w_o': 8.0,
     'L0_ffn_w_router': 8.0,
     'L0_ffn_W_qkv': 8.0,
     'L0_ffn_W_out': 8.0,
     'L0_ffn_W1': 8.0,
     'L0_ffn_W2': 8.0,
     'L0_ffn_W3': 8.0,
     'L1_attn_time_first': 7.47,
     'L1_attn_time_mix_k': 4.254,
     'L1_attn_time_mix_v': 2.787,
     'L1_attn_time_mix_r': 8.0}
    for name, (base, spread) in spreads.items():
        noise = np.random.default_rng([zlib.crc32(name.encode()), seed]).standard_normal(out[name].shape)
        drawn = base * np.exp(spread * noise) if base else spread * noise
        out[name] = jnp.asarray(drawn.astype(out[name].dtype))
    for name, factor in factors.items():
        out[name] = (out[name] * factor).astype(out[name].dtype)
    return out
```

```python
import concourse.bass as bass
from concourse import mybir
from contextlib import ExitStack

F32 = mybir.dt.float32
F16 = mybir.dt.float16
BF16 = mybir.dt.bfloat16
I32 = mybir.dt.int32
ALU = mybir.AluOpType
ACT = mybir.ActivationFunctionType
AX = mybir.AxisListType

P = 128
B, T, D = 8, 1024, 256
NT = T // P
NH, DK = 16, 16
CAP = T // 8
DFF = 682
NE = 8
EXPERT_CAP = int(1.25 * B * T / NE)
RSQRT_MAGIC = 1597463007.0
SA, CA, GA, SB, CB, GB = range(6)


def rsqrt(dve, nc, link, x, y, t):
    link(nc.vector.tensor_scalar(y.bitcast(I32), x.bitcast(I32), -0.5, RSQRT_MAGIC, ALU.mult, ALU.add))
    for _ in range(3):
        link(nc.vector.scalar_tensor_tensor(out=t, in0=x, scalar=-0.5, in1=y, op0=ALU.mult, op1=ALU.mult))
        link(nc.vector.tensor_tensor(t, t, y, ALU.mult))
        link(nc.vector.scalar_tensor_tensor(out=y, in0=t, scalar=1.5, in1=y, op0=ALU.add, op1=ALU.mult))


RSQRT_LINKS = 10


def wait_apart(eng, sem, value):
    eng.wait_ge(sem, value)
    if not isinstance(value, int):
        eng.nop(nofuse=True)


def bcast(ap, n):
    return ap.unsqueeze(len(ap.shape)).to_broadcast(list(ap.shape) + [n])


class Linker:

    def __init__(self, eng, sem, batch, steps):
        self.eng, self.sem, self.before, self.steps, self.k = eng, sem, batch * steps, steps, 0

    def __call__(self, ins):
        ins.then_inc(self.sem, 1)
        self.k += 1
        self.eng.wait_ge(self.sem, self.before + self.k)

    def done(self):
        assert self.k == self.steps, (self.k, self.steps)


def modulation(nc, sem, g, cs, wmods):
    with ExitStack() as st:
        c_nat = st.enter_context(nc.sbuf_tensor("c_nat", [B, 2, D], F32))
        c_tanh = st.enter_context(nc.sbuf_tensor("c_tanh", [B, 2, D], F32))
        c_silu = st.enter_context(nc.sbuf_tensor("c_silu", [B, 2, D], F32))
        cT = st.enter_context(nc.sbuf_tensor("cT", [P, 2, 2, B], F32))
        wmod = st.enter_context(nc.sbuf_tensor("wmod", [P, 2, 2, 6 * D], F32))
        gate = st.enter_context(nc.sbuf_tensor("gate", [P, 2, 2, 2, 2, B], F32))
        ps_c = st.enter_context(nc.psum_tensor("ps_c", [P, 2, 2, B], F32))
        ps_m = st.enter_context(nc.psum_tensor("ps_m", [P, 2, 12, B], F32))
        mod_rows = st.enter_context(nc.sbuf_tensor("mod_rows", [12 * B, 2, P], F32))
        ps_r = st.enter_context(nc.psum_tensor("ps_r", [12 * B, 2, P], F32))
        s_ld, s_wm = sem("mod_c_loaded"), sem("mod_w_loaded")
        s_done, s_rt, s_rows, s_st = sem("mod_done"), sem("mod_rows_transposed"), sem("mod_rows"), sem("mod_stored")
        s_id, s_th, s_silu, s_ct, s_cte, s_mm = (sem("mod_" + n) for n in
            ("identity", "tanh", "silu", "c_transposed", "cT", "product"))
        s_dve = sem("mod_dve_chain")
        ident, MOD = g["ident"], g["MOD"]
        with nc.Block() as block:
            @block.sync
            def _(sp):
                for l in range(2):
                    sp.dma_start(c_nat[:, l, :], cs[l]).then_inc(s_ld, 16)
                for l in range(2):
                    sp.dma_start(wmod[:, l, :, :], wmods[l].rearrange("(h p) n -> p h n", p=P)).then_inc(s_wm, 16)
                sp.wait_ge(s_rows, 1)
                for l in range(2):
                    sp.dma_start(g["mod_dram"][l].rearrange("v b c -> (v b) c"), mod_rows[:, l, :]).then_inc(s_st, 16)
                sp.wait_ge(s_st, 32)

            @block.gpsimd
            def _(pool):
                nc.gpsimd.memset(ident[:], 0.0).then_inc(s_id, 1)
                pool.wait_ge(s_id, 1)
                nc.gpsimd.affine_select(out=ident[:], in_=ident[:], compare_op=ALU.not_equal, fill=1.0, base=0,
                                        pattern=[[-1, P]], channel_multiplier=1).then_inc(s_id, 1)

            @block.scalar
            def _(act):
                act.wait_ge(s_ld, 32)
                nc.scalar.activation(c_tanh[:], c_nat[:], ACT.Tanh, scale=0.5).then_inc(s_th, 1)

            @block.vector
            def _(dve):
                link = Linker(dve, s_dve, 0, 5)
                dve.wait_ge(s_th, 1)
                dve.wait_ge(s_id, 2)
                link(nc.vector.scalar_tensor_tensor(out=c_silu[:], in0=c_tanh[:], scalar=1.0, in1=c_nat[:],
                                                    op0=ALU.add, op1=ALU.mult))
                nc.vector.tensor_scalar(c_silu[:], c_silu[:], 0.5, None, ALU.mult).then_inc(s_silu, 1)
                dve.wait_ge(s_ct, 1)
                nc.vector.tensor_copy(cT[:], ps_c[:]).then_inc(s_cte, 1)
                dve.wait_ge(s_mm, 1)
                link(nc.vector.tensor_copy(MOD[:], ps_m[:]))
                v = MOD[:].rearrange("p l (a b h) n -> p l a b h n", a=2, b=3)
                for l in range(2):
                    for a in range(2):
                        nc.vector.tensor_scalar(gate[:, 0, l, a], v[:, l, a, 2], 0.0, 2.0, ALU.is_ge, ALU.mult)
                        last = nc.vector.scalar_tensor_tensor(out=gate[:, 1, l, a], in0=v[:, l, a, 2], scalar=-1.0,
                                                              in1=v[:, l, a, 2], op0=ALU.mult, op1=ALU.max)
                link(last)
                link(nc.vector.tensor_scalar(gate[:, 1], gate[:, 1], 0.25, None, ALU.max))
                for l in range(2):
                    for a in range(2):
                        nc.vector.tensor_scalar(v[:, l, a, 1], v[:, l, a, 1], 1.0, None, ALU.add)
                        last = nc.vector.scalar_tensor_tensor(out=v[:, l, a, 2], in0=gate[:, 0, l, a], scalar=-1.0,
                                                              in1=gate[:, 1, l, a], op0=ALU.add, op1=ALU.mult)
                link(last)
                nc.vector.tensor_copy(g["ident16"][:], ident[:]).then_inc(s_done, 1)
                link.done()
                dve.wait_ge(s_rt, 1)
                nc.vector.tensor_copy(mod_rows[:], ps_r[:]).then_inc(s_rows, 1)

            @block.tensor
            def _(pe):
                pe.wait_ge(s_id, 2)
                pe.wait_ge(s_silu, 1)
                for l in range(2):
                    for h in range(2):
                        last = nc.tensor.transpose(ps_c[:, l, h, :], c_silu[:, l, h * P:(h + 1) * P], ident[0:B, 0:B])
                last.then_inc(s_ct, 1)
                pe.wait_ge(s_cte, 1)
                pe.wait_ge(s_wm, 32)
                for l in range(2):
                    for m in range(12):
                        for h in range(2):
                            last = nc.tensor.matmul(ps_m[:, l, m, :], wmod[:, l, h, m * P:(m + 1) * P], cT[:, l, h, :],
                                                    start=(h == 0), stop=(h == 1))
                last.then_inc(s_mm, 1)
                pe.wait_ge(s_done, 1)
                for l in range(2):
                    last = nc.tensor.transpose(ps_r[:, l, :], MOD[:, l].rearrange("p v b -> p (v b)"), ident[:])
                last.then_inc(s_rt, 1)


def softcap_attention(nc, sem, g, x, w_q, w_k, w_v, w_o):
    QC = 512
    NQC = T // QC
    UNITS = [(q, c, i) for q in range(4) for c in range(NQC) for i in range((c + 1) * QC // P)]
    NU = len(UNITS)
    NTP = 3
    assert NU % NTP == 0
    N_DIAG = 4 * NT
    EPS = 1.1920929e-07
    SPLIT_SCALE = 2.0 ** 12

    def span(c, i):
        n0 = max(i * P, c * QC)
        return n0, (c + 1) * QC - n0

    EXTRA = {u: [] for u in range(NU)}
    EXTRA[0] += [("heads_out", 7)]
    EXTRA[1] += [("gated_wo", 0), ("gated_wo", 1)]
    for n in range(4):
        EXTRA[2 + n].append(("yT", n))
        EXTRA[6 + n].append(("project_out", n))
        EXTRA[10 + n] += [("qkT_half1", 2 * n), ("qkT_half1", 2 * n + 1)]
        EXTRA[17 + n].append(("hT", n))
        EXTRA[38 + n] += [("qkT_half0", 2 * n), ("qkT_half0", 2 * n + 1)]
    for n in range(12):
        EXTRA[21 + n + 2 * (n // 6)].append(("qkv", n))
    for m in range(7):
        EXTRA[9 if m == 0 else 4 + 12 * (m // 2) + 8 * (m % 2)].append(("heads_out", m))
    LN_AT = 14
    ORDER = [e for u in range(NU) for e in EXTRA[u]]

    def of_before(e):
        return e[0] in ("gated_wo", "yT", "project_out") or e == ("heads_out", 7)

    def of_next(e):
        return e[0] in ("hT", "qkv", "qkT_half0")

    BEFORES, NEXTS = list(filter(of_before, ORDER)), list(filter(of_next, ORDER))
    IN_LAST = [e for e in ORDER if not of_next(e)]
    assert ORDER[:len(BEFORES)] == BEFORES and len(ORDER) % 2 == 0

    def uses(stage, n, b):
        e = (stage, n)
        base = len(NEXTS) - len(BEFORES)
        fixed = isinstance(b, int)
        if of_next(e):
            at = NEXTS.index(e) + 1 if fixed and b == 0 else base + len(ORDER) * (b - 1) + ORDER.index(e) + 1
            odd = (NEXTS.index(e) if fixed and b == 0 else base + ORDER.index(e)) % 2
        elif of_before(e):
            cut = len(NEXTS) if fixed and b == B - 1 else 0
            at = base - cut + len(ORDER) * (b + 1) + ORDER.index(e) + 1
            odd = (base - cut + ORDER.index(e)) % 2
        else:
            order = IN_LAST if fixed and b == B - 1 else ORDER
            at = base + len(ORDER) * b + order.index(e) + 1
            odd = (base + order.index(e)) % 2
        return at, odd

    def batch_of(e, b, first, last):
        if of_before(e):
            return None if first else b - 1
        if of_next(e):
            return None if last else b + 1
        return b

    with ExitStack() as st:
        def sb(name, shape):
            return st.enter_context(nc.sbuf_tensor("a_" + name, shape, F32))

        def sb16(name, shape):
            return st.enter_context(nc.sbuf_tensor("a_" + name, shape, F16))

        KT = sb16("KT", [P, NH // 2, T])
        QT = sb16("QT", [P, NH // 2, T])
        QKS = sb16("QKS", [P, 2, NT, NH, 4, DK])
        VA = sb("VA", [P, NT, NH, DK + 1])
        VR = sb("VR", [P, NT, D // 2])
        Z = sb("Z", [P, NT, D])
        HT = sb("HT", [P, 2, T])
        QK = Z[:].rearrange("p (m i) c -> p m i c", m=2)
        TP = sb("TP", [P, NTP, 4, QC])
        OS = sb("OS", [P, 2, QC])
        Y = sb("Y", [P, NT, D])
        YT = HT
        WOG = sb("WOG", [P, 2, D])
        WS = Z[:, 0:2, :]
        WO = sb("WO", [P, 2, D])
        WQKV = sb("WQKV", [P, 2, 3 * D])
        STATS = sb("STATS", [P, NT, 6])
        MV = sb("MV", [P, NT, 2])
        LV, LR, LT = sb("LV", [P, NT]), sb("LR", [P, NT]), sb("LT", [P, NT])
        SS, RS, RT = (sb(n, [P, NT // 2 * 32]) for n in ("SS", "RS", "RT"))
        RC = sb("RC", [P, 4, 4])
        SC = st.enter_context(nc.psum_tensor("SC", [P, 4, QC], F32))
        OB = [st.enter_context(nc.psum_tensor(f"OB{i}", [P, QC], F32)) for i in range(2)]
        AUX = [st.enter_context(nc.psum_tensor(f"AUX{i}", [P, 512], F32)) for i in range(2)]
        X, ident, MOD = g["X"], g["ident"], g["MOD"]
        ident16 = g["ident16"]

        WN = Z[:].rearrange("p (m h) c -> p m h c", h=2)

        def square_of(i):
            return QKS[:, 0, i].rearrange("p h s d -> p (h s d)").bitcast(F32)

        s_w, s_wo_ld, s_x = sem("a_w_loaded"), sem("a_wo_loaded"), sem("a_x_loaded")
        s_ones, s_wt, s_wte = sem("a_ones"), sem("a_w_transposed"), sem("a_wT")
        s_aux, s_auxf = sem("a_ring_filled"), sem("a_ring_emptied")
        s_z, s_sq, s_ssr, s_qkn = sem("a_z"), sem("a_qk_squared"), sem("a_squares_summed"), sem("a_qk_normed")
        s_va1, s_zero = sem("a_v_half1"), sem("a_strips_zero")
        s_sc, s_th, s_ex, s_mk, s_pv = (sem("a_" + n) for n in ("scores", "tanh", "exp", "masked", "pv"))
        s_os, s_ws = sem("a_strips_copied"), sem("a_wo_scaled")
        c_ln, c_norm, c_rc = sem("a_ln_chain"), sem("a_norm_chain"), sem("a_reciprocal_chain")

        with nc.Block() as block:
            @block.sync
            def _(sp):
                for m, w in enumerate((w_q, w_k, w_v)):
                    sp.dma_start(WN[:, m], w.rearrange("(h p) c -> p h c", p=P)).then_inc(s_w, 16)
                sp.dma_start(WO[:], w_o.rearrange("(h p) c -> p h c", p=P)).then_inc(s_wo_ld, 16)
                xv = x.rearrange("b (i p) c -> p (b i) c", p=P)
                sp.dma_start(X[:, 0:NT, :], xv[:, 0:NT, :]).then_inc(s_x, 16)
                with sp.Fori(1, B) as b:
                    sp.wait_ge(s_x, 16 * b)
                    sp.dma_start(X[:, bass.ds(b * NT, NT), :], xv[:, bass.ds(b * NT, NT), :]).then_inc(s_x, 16)

            @block.gpsimd
            def _(pool):
                nc.gpsimd.memset(VA[:, :, :, DK], 1.0).then_inc(s_ones, 1)

                def square(b, i):
                    pool.wait_ge(s_auxf, uses("qkv", 3 * (i // 2) + i % 2, b)[0])
                    nc.gpsimd.tensor_tensor(square_of(i).rearrange("p (m c) -> p m c", m=2), QK[:, :, i % 4],
                                            QK[:, :, i % 4], ALU.mult).then_inc(s_sq, 1)

                def v_copy(b):
                    wait_apart(pool, s_auxf, uses("qkv", 11, b)[0])
                    nc.gpsimd.tensor_copy(VA[:, :, NH // 2:, 0:DK],
                                          VR[:].rearrange("p i (h d) -> p i h d", d=DK)).then_inc(s_va1, 1)

                def units(b, first, last):
                    n_diag = 0
                    for u, (q, c, i) in enumerate(UNITS):
                        if i >= c * QC // P:
                            wait_apart(pool, s_ex, NU * b + u + 1)
                            n_diag += 1
                            t = TP[:, u % NTP, :, 0:P]
                            nc.gpsimd.affine_select(out=t, in_=t, compare_op=ALU.is_ge, fill=0.0, base=0,
                                                    pattern=[[0, 4], [1, P]], channel_multiplier=-1).then_inc(s_mk, 1)
                        for stage, n in EXTRA[u - 1] if u and not last else []:
                            if stage == "qkv" and n % 3 < 2:
                                square(b + 1, 2 * (n // 3) + n % 3)
                        if u == 10:
                            if not first:
                                pool.wait_ge(s_pv, NU * b)
                            v_copy(b)
                    assert n_diag == N_DIAG

                for i in range(NT):
                    square(0, i)
                units(0, True, False)
                with pool.Fori(1, B - 1) as b:
                    units(b, False, False)
                units(B - 1, False, True)

            @block.scalar
            def _(act):
                def tanh(b, u):
                    q, c, i = UNITS[u]
                    _, n = span(c, i)
                    act.wait_ge(s_sc, NU * b + u + 1)
                    if not (isinstance(b, int) and NU * b + u < NTP):
                        act.wait_ge(s_pv, NU * b + u - NTP + 1)
                    nc.scalar.activation(TP[:, u % NTP, :, 0:n], SC[:, :, 0:n], ACT.Tanh,
                                         scale=1.0 / (50.0 * DK ** 0.5 * SPLIT_SCALE ** 2)).then_inc(s_th, 1)

                def exp(b, u):
                    q, c, i = UNITS[u]
                    _, n = span(c, i)
                    act.wait_ge(s_th, NU * b + u + 1)
                    t = TP[:, u % NTP, :, 0:n]
                    nc.scalar.activation(t, t, ACT.Exp, scale=50.0).then_inc(s_ex, 1)

                def units(b, last):
                    for u in range(NU):
                        if u + 1 < NU:
                            tanh(b, u + 1)
                        elif not last:
                            tanh(b + 1, 0)
                        exp(b, u)

                tanh(0, 0)
                units(0, False)
                with act.Fori(1, B - 1) as b:
                    units(b, False)
                units(B - 1, True)

            @block.tensor
            def _(pe):
                pe.wait_ge(s_w, 48)
                for m in range(3):
                    if m >= 2:
                        pe.wait_ge(s_wte, m - 1)
                    for h in range(2):
                        for o in range(2):
                            last = nc.tensor.transpose(AUX[m % 2][:, h * D + o * P:h * D + o * P + P],
                                                       WN[:, m, o, h * P:h * P + P], ident[:])
                    last.then_inc(s_wt, 1)
                pe.wait_ge(s_wte, 3)

                def tiles_T(aux, src, g4, col):
                    for t in range(4):
                        last = nc.tensor.transpose(aux[:, t * P:(t + 1) * P], src[:, 4 * g4 + t, col:col + P], ident[:])
                    return last

                def extra(stage, n, b):
                    at, odd = uses(stage, n, b)
                    if not (isinstance(at, int) and at <= 2):
                        pe.wait_ge(s_auxf, at - 2)
                    aux = AUX[odd]
                    if stage == "hT":
                        pe.wait_ge(s_z, NT * b + 4 * (n // 2) + 4)
                        last = tiles_T(aux, Z, n // 2, P * (n % 2))
                    elif stage == "qkv":
                        p, what = n // 3, n % 3
                        if n == 0:
                            pe.wait_ge(s_auxf, uses("hT", 3, b)[0])
                        if what < 2:
                            i = 2 * p + what
                            for h in range(2):
                                last = nc.tensor.matmul(aux[:, :], HT[:, h, i * P:(i + 1) * P], WQKV[:, h, 0:2 * D],
                                                        start=(h == 0), stop=(h == 1))
                        else:
                            for i in range(2):
                                for h in range(2):
                                    last = nc.tensor.matmul(aux[:, i * D:(i + 1) * D],
                                                            HT[:, h, (2 * p + i) * P:(2 * p + i + 1) * P],
                                                            WQKV[:, h, 2 * D:3 * D], start=(h == 0), stop=(h == 1))
                    elif stage in ("qkT_half0", "qkT_half1"):
                        pe.wait_ge(s_qkn, 2 * b + 2)
                        aux16 = aux[:, :].bitcast(F16)
                        pair, kind = 4 * int(stage[-1]) + n // 2, 1 - n % 2
                        for i in range(NT):
                            src = QKS[:, kind, i, 2 * pair:2 * pair + 2].rearrange("p h s d -> p (h s d)")
                            last = nc.tensor.transpose(aux16[:, i * P:(i + 1) * P], src, ident16[:])
                    elif stage == "heads_out":
                        pe.wait_ge(s_os, 8 * b + n + 1)
                        for t in range(4):
                            last = nc.tensor.transpose(aux[:, t * P:(t + 1) * P], OS[:, n % 2, t * P:(t + 1) * P], ident[:])
                    elif stage == "gated_wo":
                        pe.wait_ge(s_ws, b + 1)
                        for h in range(2):
                            last = nc.tensor.transpose(aux[:, h * P:(h + 1) * P], WS[:, h, n * P:(n + 1) * P], ident[:])
                    elif stage == "yT":
                        pe.wait_ge(s_auxf, uses("heads_out", 7, b)[0])
                        last = tiles_T(aux, Y, n // 2, P * (n % 2))
                    elif stage == "project_out":
                        pe.wait_ge(s_auxf, uses("yT", 3, b)[0])
                        for t in range(2):
                            for h in range(2):
                                last = nc.tensor.matmul(aux[:, t * D:(t + 1) * D],
                                                        YT[:, h, (2 * n + t) * P:(2 * n + t + 1) * P], WOG[:, h, :],
                                                        start=(h == 0), stop=(h == 1))
                    last.then_inc(s_aux, 1)

                def scores(b, u):
                    q, c, i = UNITS[u]
                    n0, n = span(c, i)
                    if u == 0:
                        pe.wait_ge(s_auxf, uses("qkT_half0", 7, b)[0])
                    if u == NU // 2:
                        pe.wait_ge(s_auxf, uses("qkT_half1", 7, b)[0])
                    if not (isinstance(b, int) and NU * b + u == 0):
                        pe.wait_ge(s_th, NU * b + u)
                    for j in range(4):
                        pair, rows = 2 * q + j // 2, slice(64 * (j % 2), 64 * (j % 2) + 64)
                        last = nc.tensor.matmul(SC[:, j, 0:n], KT[rows, pair, i * P:(i + 1) * P],
                                                QT[rows, pair, n0:n0 + n], start=True, stop=True)
                    last.then_inc(s_sc, 1)

                def values(b, u, n_diag):
                    q, c, i = UNITS[u]
                    n0, n = span(c, i)
                    m = NQC * q + c
                    if u == 0:
                        pe.wait_ge(s_auxf, uses("qkv", 11, b)[0])
                        pe.wait_ge(s_ones, 1)
                        pe.wait_ge(s_zero, 1)
                    if u == NU // 2:
                        pe.wait_ge(s_va1, b + 1)
                    if i == 0 and not (isinstance(b, int) and 8 * b + m < 2):
                        pe.wait_ge(s_os, 8 * b + m - 1)
                    pe.wait_ge(s_ex, NU * b + u + 1)
                    if i >= c * QC // P:
                        n_diag += 1
                        pe.wait_ge(s_mk, N_DIAG * b + n_diag)
                    for j in range(4):
                        last = nc.tensor.matmul(OB[m % 2][32 * j:32 * j + DK + 1, n0 - c * QC:n0 - c * QC + n],
                                                VA[:, i, 4 * q + j, :], TP[:, u % NTP, j, 0:n],
                                                start=(i == 0), stop=(i == (c + 1) * QC // P - 1))
                    last.then_inc(s_pv, 1)
                    return n_diag

                def units(b, first, last):
                    n_diag = 0
                    for u in range(NU):
                        if u + 2 < NU:
                            scores(b, u + 2)
                        elif not last:
                            scores(b + 1, u + 2 - NU)
                        n_diag = values(b, u, n_diag)
                        for e in EXTRA[u]:
                            bb = batch_of(e, b, first, last)
                            if bb is not None:
                                extra(*e, bb)

                for e in NEXTS:
                    extra(*e, 0)
                scores(0, 0)
                scores(0, 1)
                units(0, True, False)
                with pe.Fori(1, B - 1) as b:
                    units(b, False, False)
                units(B - 1, False, True)
                for e in BEFORES:
                    extra(*e, B - 1)

            @block.vector
            def _(dve):
                for m in range(3):
                    dve.wait_ge(s_wt, m + 1)
                    nc.vector.tensor_copy(WQKV[:, :, m * D:(m + 1) * D],
                                          AUX[m % 2][:, :].rearrange("p (h o) -> p h o", h=2)).then_inc(s_wte, 1)
                dve.wait_ge(s_wo_ld, 16)
                nc.vector.memset(OB[0][:, :], 0.0)
                nc.vector.memset(OB[1][:, :], 0.0).then_inc(s_zero, 1)

                def layer_norm(b):
                    link = Linker(dve, c_ln, b, 3 + RSQRT_LINKS)
                    dve.wait_ge(s_x, 16 * b + 16)
                    for i in range(NT):
                        last = nc.vector.bn_stats(STATS[:, i, :], X[:, b * NT + i, :])
                    last.then_inc(c_ln, 1)
                    link.k += 1
                    wait_apart(dve, c_ln, link.before + link.k)
                    for i in range(NT):
                        last = nc.vector.bn_aggr(MV[:, i, :], STATS[:, i, :])
                    link(last)
                    link(nc.vector.tensor_scalar(LV[:], MV[:, :, 1], 1e-5, None, ALU.add))
                    rsqrt(dve, nc, link, LV[:], LR[:], LT[:])
                    link.done()
                    if not (isinstance(b, int) and b == 0):
                        dve.wait_ge(s_qkn, 2 * b)
                    for i in range(NT):
                        nc.vector.tensor_scalar(Z[:, i, :], X[:, b * NT + i, :], MV[:, i, 0:1], LR[:, i:i + 1],
                                                ALU.subtract, ALU.mult).then_inc(s_z, 1)

                def sum_squares(b, i):
                    dve.wait_ge(s_sq, NT * b + i + 1)
                    nc.vector.tensor_reduce(SS[:].rearrange("p (m i h) -> p m i h", m=2, i=4)[:, :, i % 4],
                                            square_of(i).rearrange("p (m h d) -> p m h d", m=2, d=DK), AX.X,
                                            ALU.add).then_inc(s_ssr, 1)

                def norm_qk(b, g4):
                    sum_squares(b, 4 * g4 + 3)
                    link = Linker(dve, c_norm, 2 * b + g4, 3 + RSQRT_LINKS)
                    dve.wait_ge(s_ssr, NT * b + 4 * g4 + 4)
                    link(nc.vector.tensor_scalar(SS[:], SS[:], 1.0 / DK / SPLIT_SCALE ** 2, EPS / SPLIT_SCALE ** 2,
                                                 ALU.mult, ALU.add))
                    rsqrt(dve, nc, link, SS[:], RS[:], RT[:])
                    qv = QK[:].rearrange("p m i (h d) -> p (m i h) d", d=DK)
                    link(nc.vector.tensor_tensor(qv, qv, bcast(RS[:], DK), ALU.mult))

                    def both(ap):
                        return ap.unsqueeze(2).to_broadcast([P, 4 * NH, 2, DK])

                    tiles = slice(4 * g4, 4 * g4 + 4)
                    q, k = (QK[:, m].rearrange("p i (h d) -> p (i h) d", d=DK) for m in range(2))
                    qs, ks = (QKS[:, m, tiles].rearrange("p i h s d -> p (i h) s d") for m in range(2))
                    nc.vector.tensor_copy(qs[:, :, 0:2], both(q))
                    link(nc.vector.tensor_copy(ks[:, :, 0::2], both(k)))
                    nc.vector.tensor_tensor(qs[:, :, 2:4], both(q), qs[:, :, 0:2], ALU.subtract)
                    nc.vector.tensor_tensor(ks[:, :, 1::2], both(k), ks[:, :, 0::2], ALU.subtract).then_inc(s_qkn, 1)
                    link.done()

                def scale_wo(b):
                    dve.wait_ge(s_qkn, 2 * B if isinstance(b, int) and b == B - 1 else 2 * b + 4)
                    for h in range(2):
                        last = nc.vector.tensor_scalar(WS[:, h, :], WO[:, h, :], MOD[:, 0, 2 * GA + h, bass.ds(b, 1)],
                                                       None, ALU.mult)
                    last.then_inc(s_ws, 1)

                def extra(stage, n, b):
                    zero = isinstance(b, int) and b == 0
                    at, odd = uses(stage, n, b)
                    aux = AUX[odd]
                    dve.wait_ge(s_aux, at)
                    if stage == "hT":
                        h, g4 = n % 2, n // 2
                        last = nc.vector.tensor_scalar(HT[:, h, g4 * 512:(g4 + 1) * 512], aux[:, :],
                                                       MOD[:, 0, 2 * CA + h, bass.ds(b, 1)],
                                                       MOD[:, 0, 2 * SA + h, bass.ds(b, 1)], ALU.mult, ALU.add)
                    elif stage == "qkv" and n % 3 < 2:
                        if n == 6:
                            dve.wait_ge(s_qkn, 2 * b + 1)
                        last = nc.vector.tensor_copy(QK[:, :, (2 * (n // 3) + n % 3) % 4],
                                                     aux[:, :].rearrange("p (m c) -> p m c", m=2))
                    elif stage == "qkv":
                        if not zero:
                            dve.wait_ge(s_va1, b)
                        if not zero and n == 2:
                            dve.wait_ge(s_pv, NU * (b - 1) + NU // 2)
                        tiles, v = slice(2 * (n // 3), 2 * (n // 3) + 2), aux[:, :].rearrange("p (i c) -> p i c", i=2)
                        nc.vector.tensor_copy(VA[:, tiles, 0:NH // 2, 0:DK],
                                              v[:, :, 0:P].rearrange("p i (h d) -> p i h d", d=DK))
                        last = nc.vector.tensor_copy(VR[:, tiles, :], v[:, :, P:])
                    elif stage in ("qkT_half0", "qkT_half1"):
                        half = int(stage[-1])
                        if n == 0 and not zero:
                            dve.wait_ge(s_sc, NU * (b - 1) + (NU if half else NU // 2))
                        last = nc.vector.tensor_copy((QT if n % 2 else KT)[:, 4 * half + n // 2, :], aux[:, :].bitcast(F16))
                    elif stage == "heads_out":
                        link = Linker(dve, c_rc, 8 * b + n, 1)
                        av = aux[:, :].rearrange("p (t j e) -> p t j e", t=4, j=4)
                        link(nc.vector.reciprocal(RC[:], av[:, :, :, DK]))
                        yv = Y[:].rearrange("p i (q j d) -> p i q j d", q=4, d=DK)
                        last = nc.vector.tensor_tensor(yv[:, 4 * (n % 2):4 * (n % 2) + 4, n // 2], av[:, :, :, 0:DK],
                                                       bcast(RC[:], DK), ALU.mult)
                    elif stage == "gated_wo":
                        last = nc.vector.tensor_copy(WOG[:, n, :], aux[:, 0:D])
                    elif stage == "yT":
                        last = nc.vector.tensor_copy(YT[:, n % 2, n // 2 * 512:n // 2 * 512 + 512], aux[:, :])
                    elif stage == "project_out":
                        xt = X[:, bass.ds(b * NT + 2 * n, 2), :]
                        last = nc.vector.tensor_tensor(xt, aux[:, :].rearrange("p (t c) -> p t c", t=2), xt, ALU.add)
                    last.then_inc(s_auxf, 1)
                    if stage == "qkv" and n % 3 < 2 and n % 6:
                        sum_squares(b, 2 * (n // 3) + n % 3 - 1)
                    if stage == "qkv" and n % 6 == 5:
                        norm_qk(b, n // 6)

                def units(b, first, last):
                    for u, (q, c, i) in enumerate(UNITS):
                        if i == (c + 1) * QC // P - 1:
                            m = NQC * q + c
                            dve.wait_ge(s_pv, NU * b + u + 1)
                            nc.vector.tensor_copy(OS[:, m % 2, :], OB[m % 2][:, :]).then_inc(s_os, 1)
                        for e in EXTRA[u]:
                            bb = batch_of(e, b, first, last)
                            if bb is not None:
                                extra(*e, bb)
                        if u == 0 and not first:
                            scale_wo(b - 1)
                        if u == LN_AT and not last:
                            layer_norm(b + 1)

                layer_norm(0)
                for e in NEXTS:
                    extra(*e, 0)
                units(0, True, False)
                with dve.Fori(1, B - 1) as b:
                    units(b, False, False)
                units(B - 1, False, True)
                scale_wo(B - 1)
                for e in BEFORES:
                    extra(*e, B - 1)


def transpose_weights(nc, sem, g, name, jobs, loads, zeroed=()):
    def place(n):
        return ring[n % 4][0:jobs[n][0].shape[1], 0:jobs[n][0].shape[0]]

    with ExitStack() as st:
        ring = [st.enter_context(nc.psum_tensor(f"{name}_ring{i}", [P, P], F32)) for i in range(4)]
        s_ld = sem(name + "_loaded")
        if zeroed:
            s_zero = sem(name + "_zeroed")
        s_t = sem(name + "_transposed")
        s_out = [sem(name + "_out_vector"), sem(name + "_out_scalar")]
        with nc.Block() as block:
            @block.sync
            def _(sp):
                for d, s in loads:
                    sp.dma_start(d, s, allow_slow_non_contiguous=(len(s.shape) == 2 and s.shape[1] == 2)).then_inc(s_ld, 16)

            @block.gpsimd
            def _(pool):
                for z in zeroed:
                    nc.gpsimd.memset(z, 0.0).then_inc(s_zero, 1)

            @block.tensor
            def _(pe):
                pe.wait_ge(s_ld, 16 * len(loads))
                for n, (src, dst, scale) in enumerate(jobs):
                    if n >= 4:
                        pe.wait_ge(s_out[n % 2], (n - 4) // 2 + 1)
                    nc.tensor.transpose(place(n), src, g["ident"][0:src.shape[0], 0:src.shape[0]]).then_inc(s_t, 1)

            @block.vector
            def _(dve):
                dve.wait_ge(s_ld, 16 * len(loads))
                if zeroed:
                    dve.wait_ge(s_zero, len(zeroed))
                for n, (src, dst, scale) in enumerate(jobs):
                    if n % 2 == 0:
                        dve.wait_ge(s_t, n + 1)
                        nc.vector.tensor_scalar(dst, _like(place(n), dst), scale, None,
                                                ALU.mult).then_inc(s_out[0], 1)

            @block.scalar
            def _(act):
                act.wait_ge(s_ld, 16 * len(loads))
                if zeroed:
                    act.wait_ge(s_zero, len(zeroed))
                for n, (src, dst, scale) in enumerate(jobs):
                    if n % 2:
                        act.wait_ge(s_t, n + 1)
                        nc.scalar.activation(dst, _like(place(n), dst), ACT.Copy if isinstance(scale, float)
                                             else ACT.Identity, scale=scale).then_inc(s_out[1], 1)


def _like(src, dst):
    if len(dst.shape) == 2:
        return src
    if len(dst.shape) == 3:
        return src.rearrange("p (a b) -> p a b", a=dst.shape[1])
    return src.rearrange("p (a b c) -> p a b c", a=dst.shape[1], b=dst.shape[2])


def routed_block(nc, sem, g, w):
    NF = -(-DFF // P)
    G4 = NH // 4
    with ExitStack() as st:
        def sb(name, shape, dtype=F32):
            return st.enter_context(nc.sbuf_tensor("r_" + name, shape, dtype))

        WQK = sb("WQK", [P, 2, 2, G4, 4, 2 * DK])
        WV = sb("WV", [P, 2, D])
        WOUT = sb("WOUT", [P, 2, D])
        W1 = sb("W1", [P, 2, NF * P])
        W2 = sb("W2", [P, 2, NF * P])
        W3 = sb("W3", [P, NF, D])
        WR = sb("WR", [P, D])
        with ExitStack() as tmp:
            def tb(name, shape):
                return tmp.enter_context(nc.sbuf_tensor("r_" + name, shape, F32))
            G = tb("G", [P, 2, 2])
            NQ, N1, N2 = tb("NQ", [P, 6, D]), tb("N1", [P, NF, D]), tb("N2", [P, NF, D])
            N3, NO = tb("N3", [P, 2, DFF]), tb("NO", [P, 2, D])
            full, rest = DFF // P, DFF % P
            loads = [(G[:, m, :], w["g%d" % (m + 1)].rearrange("(h p) -> p h", p=P)) for m in range(2)]
            loads += [(NQ[:], w["W_qkv"].rearrange("(m p) c -> p m c", p=P)),
                      (NO[:], w["W_out"].rearrange("(m p) c -> p m c", p=P)),
                      (N3[:], w["W3"].rearrange("(m p) c -> p m c", p=P)),
                      (WR[:], w["w_router"].unsqueeze(0).to_broadcast([P, D]))]
            for n, t in ((N1, "W1"), (N2, "W2")):
                loads += [(n[:, 0:full, :], w[t][0:full * P].rearrange("(m p) c -> p m c", p=P)),
                          (n[0:rest, full, :], w[t][full * P:DFF])]
            jobs = []
            for h in range(2):
                cols = slice(h * P, (h + 1) * P)
                for m in range(4):
                    dst = WQK[:, h, m // 2, 2 * (m % 2):2 * (m % 2) + 2, :, 0:DK]
                    jobs.append((NQ[:, m, cols], dst, G[:, 0, h:h + 1]))
                for m in range(2):
                    jobs.append((NQ[:, 4 + m, cols], WV[:, h, m * P:(m + 1) * P], G[:, 0, h:h + 1]))
                    jobs.append((NO[:, m, cols], WOUT[:, h, m * P:(m + 1) * P], 1.0))
                for m in range(NF):
                    rows = min(P, DFF - m * P)
                    for n, d in ((N1, W1), (N2, W2)):
                        jobs.append((n[0:rows, m, cols], d[:, h, m * P:m * P + rows], G[:, 1, h:h + 1]))
            for m in range(NF):
                rows = min(P, DFF - m * P)
                for c in range(2):
                    jobs.append((N3[:, c, m * P:m * P + rows], W3[0:rows, m, c * P:(c + 1) * P], 0.5))
            transpose_weights(nc, sem, g, "r_weights", jobs, loads, zeroed=(WQK[:], W1[:], W2[:], W3[:, full, :]))

        LOW = sb("LOW", [P, P])
        RANKS = sb("RANKS", [P, P])
        ONES = sb("ONES", [P, P])
        NEG = sb("NEG", [P, 4, P], BF16)
        identb = sb("identb", [P, P], BF16)
        ROWS = [sb(f"ROWS{s}", [P, 3, D]) for s in range(2)]
        H = [sb(f"H{s}", [P, NT, D]) for s in range(2)]
        JUNK = [sb(f"JUNK{s}", [P, 2, 9 * P], BF16) for s in range(2)]
        ST, MV = [sb(f"ST{s}", [P, NT, 6]) for s in range(2)], [sb(f"MV{s}", [P, NT, 2]) for s in range(2)]
        RL = [sb(f"RL{s}", [P, 4, NT]) for s in range(2)]
        SCR = [sb(f"SCR{s}", [P, NT]) for s in range(2)]
        CNT = [sb(f"CNT{s}", [P, NT, 5]) for s in range(2)]
        RANK = [sb(f"RANK{s}", [P, NT]) for s in range(2)]
        DG = [sb(f"DG{s}", [P, NT, P]) for s in range(2)]
        PM = [DG[s] for s in range(2)]
        PT = [sb(f"PT{s}", [P, NT, P]) for s in range(2)]
        SEL = [sb(f"SEL{s}", [P, D]) for s in range(2)]
        XA = [sb(f"XA{s}", [P, D]) for s in range(2)]
        U = [sb(f"U{s}", [P, D]) for s in range(2)]
        UT = [sb(f"UT{s}", [P, 2, P]) for s in range(2)]
        OT = [sb(f"OT{s}", [P, 2, P]) for s in range(2)]
        QKT = [sb(f"QKT{s}", [P, 2, G4, P]) for s in range(2)]
        V = [sb(f"V{s}", [P, NH, DK + 1]) for s in range(2)]
        EX = [sb(f"EX{s}", [P, NH, P]) for s in range(2)]
        ET = [sb(f"ET{s}", [P, NH, P]) for s in range(2)]
        TH = [EX[s][:].rearrange("p h k -> p (h k)")[:, 0:NF * P] for s in range(2)]
        GH = [ET[s][:].rearrange("p h k -> p (h k)")[:, 0:NF * P] for s in range(2)]
        MX = [sb(f"MX{s}", [P, 2, NH]) for s in range(2)]
        SM = [sb(f"SM{s}", [P, 2, 4]) for s in range(2)]
        BK = [[st.enter_context(nc.psum_tensor(f"r_BK{s}{n}", [P, 512], F32)) for n in range(4)] for s in range(2)]
        X, ident = g["X"], g["ident"]
        names = ["filled", "constants", "rows0", "rows1", "free", "mean", "z", "h", "diagonals", "score_rows", "one_hot", "gathered",
                 "pt", "sum1", "u1", "u1T", "u1T_out", "qkv", "qkT_out", "v_out", "scores", "max", "exp",
                 "expT", "expT_out_a", "expT_out_v", "heads", "heads_out", "headsT", "headsT_out", "attended", "xa",
                 "sum2", "u2", "u2T", "u2T_out", "hidden", "tanh", "gated", "processed", "delta", "scattered"]
        s = {n: sem("r_" + n) for n in names}
        c_ln, c_h, c_rank, c_u1, c_max, c_heads, c_u2, c_gate, c_x = (sem("r_chain_" + n) for n in
            ("ln", "h", "rank", "u1", "max", "heads", "u2", "gate", "x"))
        rows_dram = g["mod_dram"]

        def both(step, j):
            for n in range(2):
                step(n, 2 * j + n)

        with nc.Block() as block:
            @block.sync
            def _(sp):
                with sp.Fori(0, B // 2) as j:
                    for n in range(2):
                        sp.wait_ge(s["free"], 2 * j + n + 1)
                        sp.dma_start(ROWS[n][:].rearrange("p v (h c) -> p (v h) c", h=2),
                                     rows_dram[0, 2 * SB:2 * GB + 2, bass.ds(2 * j + n, 1), :].rearrange(
                                         "v b c -> b v c").to_broadcast([P, 6, P])).then_inc(s["rows%d" % n], 16)

            @block.gpsimd
            def _(pool):
                c = s["constants"]
                nc.gpsimd.memset(LOW[:], 1.0).then_inc(s["filled"], 1)
                nc.gpsimd.memset(NEG[:], 0.0).then_inc(s["filled"], 1)
                pool.wait_ge(s["filled"], 2)
                nc.gpsimd.affine_select(out=LOW[:], in_=LOW[:], compare_op=ALU.is_gt, fill=0.0, base=0,
                                        pattern=[[-1, P]], channel_multiplier=1).then_inc(c, 1)
                nc.gpsimd.affine_select(out=NEG[:], in_=NEG[:], compare_op=ALU.is_ge, fill=-1e30, base=0,
                                        pattern=[[0, 4], [-1, P]], channel_multiplier=1).then_inc(c, 1)
                nc.gpsimd.iota(RANKS[:], pattern=[[1, P]], base=0, channel_multiplier=0,
                               allow_small_or_imprecise_dtypes=True).then_inc(c, 1)
                nc.gpsimd.memset(ONES[:], 1.0).then_inc(c, 1)
                for n in range(2):
                    nc.gpsimd.memset(V[n][:, :, DK], 1.0).then_inc(c, 1)

            @block.tensor
            def _(pe):
                pe.wait_ge(s["constants"], 7)

                def score_rows(n, b):
                    pe.wait_ge(s["diagonals"], b + 1)
                    for c in range(2):
                        last = nc.tensor.matmul(BK[n][c][:, :], ONES[:], DG[n][:, 4 * c:4 * c + 4, :], start=True,
                                                stop=True)
                    last.then_inc(s["score_rows"], 1)

                def gather(n, b):
                    pe.wait_ge(s["one_hot"], b + 1)
                    for i in range(NT):
                        nc.tensor.matmul(BK[n][2][:, 0:D], PM[n][:, i, :], H[n][:, i, :], start=(i == 0),
                                         stop=(i == NT - 1))
                    for i in range(NT):
                        last = nc.tensor.transpose(BK[n][i // 4][:, (i % 4) * P:(i % 4 + 1) * P], PM[n][:, i, :],
                                                   ident[:])
                    last.then_inc(s["gathered"], 1)

                def transpose2(src, name, ready, bank, off):
                    def step(n, b):
                        wait_apart(pe, s[ready], b + 1)
                        for h in range(2):
                            last = nc.tensor.transpose(BK[n][bank][:, off + h * P:off + (h + 1) * P],
                                                       src[n][:, h * P:(h + 1) * P], ident[:])
                        last.then_inc(s[name], 1)
                    return step

                def qkv(n, b):
                    pe.wait_ge(s["u1T_out"], b + 1)
                    pe.wait_ge(s["pt"], b + 1)
                    for m in range(2):
                        for gr in range(G4):
                            for h in range(2):
                                nc.tensor.matmul(BK[n][m][:, gr * P:(gr + 1) * P],
                                                 WQK[:, h, m, gr].rearrange("p j d -> p (j d)"),
                                                 UT[n][:, h, :], start=(h == 0), stop=(h == 1))
                    for h in range(2):
                        last = nc.tensor.matmul(BK[n][2][:, D:2 * D], UT[n][:, h, :], WV[:, h, :], start=(h == 0),
                                                stop=(h == 1))
                    last.then_inc(s["qkv"], 1)

                def scores(n, b):
                    wait_apart(pe, s["qkT_out"], b + 1)
                    wait_apart(pe, s["v_out"], b + 1)
                    for r in range(4):
                        nc.tensor.matmul(BK[n][r][:, :], identb[:], NEG[:], start=True, stop=False)
                    for gr in range(G4):
                        for j in range(4):
                            r = slice(32 * j, 32 * j + 32)
                            last = nc.tensor.matmul(BK[n][j][:, gr * P:(gr + 1) * P], QKT[n][r, 0, gr, :],
                                                    QKT[n][r, 1, gr, :], start=False, stop=(gr == G4 - 1))
                    last.then_inc(s["scores"], 1)

                def exp_transposed(n, b):
                    pe.wait_ge(s["exp"], b + 1)
                    for h in range(NH):
                        last = nc.tensor.transpose(BK[n][h // 4][:, (h % 4) * P:(h % 4 + 1) * P], EX[n][:, h, :], ident[:])
                    last.then_inc(s["expT"], 1)

                def heads(n, b):
                    pe.wait_ge(s["expT_out_a"], b + 1)
                    pe.wait_ge(s["expT_out_v"], b + 1)
                    for h in range(NH):
                        last = nc.tensor.matmul(BK[n][0][:, h * (DK + 1):(h + 1) * (DK + 1)], ET[n][:, h, :],
                                                V[n][:, h, :], start=True, stop=True)
                    last.then_inc(s["heads"], 1)

                def attended(n, b):
                    pe.wait_ge(s["headsT_out"], b + 1)
                    for h in range(2):
                        last = nc.tensor.matmul(BK[n][2][:, 0:D], OT[n][:, h, :], WOUT[:, h, :], start=(h == 0),
                                                stop=(h == 1))
                    last.then_inc(s["attended"], 1)

                def hidden(n, b):
                    pe.wait_ge(s["u2T_out"], b + 1)
                    for m in range(NF):
                        for k, wk in enumerate((W1, W2)):
                            for h in range(2):
                                bank, off = (3 * k, m * P) if m < 4 else (1, k * 2 * P + (m - 4) * P)
                                last = nc.tensor.matmul(BK[n][bank][:, off:off + P], wk[:, h, m * P:(m + 1) * P],
                                                        UT[n][:, h, :], start=(h == 0), stop=(h == 1))
                    last.then_inc(s["hidden"], 1)

                def processed(n, b):
                    pe.wait_ge(s["gated"], b + 1)
                    for h in range(2):
                        nc.tensor.matmul(BK[n][2][:, 0:D], OT[n][:, h, :], WOUT[:, h, :], start=(h == 0), stop=False)
                    for m in range(NF):
                        last = nc.tensor.matmul(BK[n][2][:, 0:D], GH[n][:, m * P:(m + 1) * P], W3[:, m, :], start=False,
                                                stop=(m == NF - 1))
                    last.then_inc(s["processed"], 1)

                def scattered(n, b):
                    pe.wait_ge(s["delta"], b + 1)
                    for i in range(NT):
                        o = BK[n][i // 2][:, (i % 2) * D:(i % 2 + 1) * D]
                        nc.tensor.matmul(o, PT[n][:, i, :], U[n][:], start=True, stop=False)
                        last = nc.tensor.matmul(o, ident[:], H[n][:, i, :], start=False, stop=True)
                    last.then_inc(s["scattered"], 1)

                with pe.Fori(0, B // 2) as j:
                    for step in (score_rows, gather, transpose2(U, "u1T", "u1", 3, 0), qkv, scores, exp_transposed, heads,
                                 transpose2(U, "headsT", "heads_out", 1, 0), attended,
                                 transpose2(U, "u2T", "u2", 1, D), hidden, processed, scattered):
                        both(step, j)

            @block.scalar
            def _(act):
                act.wait_ge(s["constants"], 7)

                def z(n, b):
                    act.wait_ge(s["mean"], b + 1)
                    for i in range(NT):
                        last = nc.scalar.activation(H[n][:, i, :], X[:, b * NT + i, :], ACT.Identity,
                                                    bias=RL[n][:, 3, i:i + 1], scale=RL[n][:, 1, i:i + 1])
                    last.then_inc(s["z"], 1)

                def selected(n, b):
                    act.wait_ge(s["gathered"], b + 1)
                    nc.scalar.activation(SEL[n][:], BK[n][2][:, 0:D], ACT.Copy)
                    nc.scalar.activation(JUNK[n][:, 0, 0:D], BK[n][2][:, 0:D], ACT.Square,
                                         accum_out=SM[n][:, 0, 0:1]).then_inc(s["sum1"], 1)
                    for c in range(2):
                        last = nc.scalar.activation(PT[n][:, 4 * c:4 * c + 4, :],
                                                    BK[n][c][:, :].rearrange("p (a b) -> p a b", a=4), ACT.Copy)
                    last.then_inc(s["pt"], 1)

                def copy_ut(ready, name, bank, off, to=UT):
                    def step(n, b):
                        act.wait_ge(s[ready], b + 1)
                        nc.scalar.activation(to[n][:], BK[n][bank][:, off:off + D].rearrange("p (h t) -> p h t", h=2),
                                             ACT.Copy).then_inc(s[name], 1)
                    return step

                def qk_out(n, b):
                    act.wait_ge(s["qkv"], b + 1)
                    for m in range(2):
                        last = nc.scalar.activation(QKT[n][:, m], BK[n][m][:, :].rearrange("p (a b) -> p a b", a=4), ACT.Copy)
                    last.then_inc(s["qkT_out"], 1)

                def exp(n, b):
                    act.wait_ge(s["max"], b + 1)
                    for h in range(NH):
                        last = nc.scalar.activation(EX[n][:, h, :], BK[n][h % 4][:, (h // 4) * P:(h // 4 + 1) * P], ACT.Exp,
                                                    bias=MX[n][:, 1, h:h + 1], scale=DK ** -0.5)
                    last.then_inc(s["exp"], 1)

                def exp_t_out(n, b):
                    act.wait_ge(s["expT"], b + 1)
                    for c in range(2):
                        last = nc.scalar.activation(ET[n][:, 4 * c:4 * c + 4, :],
                                                    BK[n][c][:, :].rearrange("p (a b) -> p a b", a=4), ACT.Copy)
                    last.then_inc(s["expT_out_a"], 1)

                def square2(n, b):
                    act.wait_ge(s["xa"], b + 1)
                    nc.scalar.activation(JUNK[n][:, 1, 0:D], XA[n][:], ACT.Square,
                                         accum_out=SM[n][:, 1, 0:1]).then_inc(s["sum2"], 1)

                def tanh(n, b):
                    act.wait_ge(s["hidden"], b + 1)
                    nc.scalar.activation(TH[n][:, 0:4 * P], BK[n][0][:, :], ACT.Tanh, scale=0.5)
                    nc.scalar.activation(TH[n][:, 4 * P:], BK[n][1][:, 0:(NF - 4) * P], ACT.Tanh,
                                         scale=0.5).then_inc(s["tanh"], 1)

                def delta(n, b):
                    act.wait_ge(s["processed"], b + 1)
                    nc.scalar.activation(U[n][:], BK[n][2][:, 0:D], ACT.Copy).then_inc(s["delta"], 1)

                with act.Fori(0, B // 2) as j:
                    for step in (z, selected, copy_ut("u1T", "u1T_out", 3, 0), qk_out, exp, exp_t_out,
                                 copy_ut("headsT", "headsT_out", 1, 0, OT), square2, copy_ut("u2T", "u2T_out", 1, D),
                                 tanh, delta):
                        both(step, j)

            @block.vector
            def _(dve):
                nc.vector.tensor_copy(identb[:], ident[:]).then_inc(s["constants"], 1)
                for n in range(2):
                    nc.vector.memset(CNT[n][:], 0.0).then_inc(s["free"], 1)
                dve.wait_ge(s["constants"], 7)

                def mean(n, b):
                    link = Linker(dve, c_ln, b, 4 + RSQRT_LINKS)
                    dve.wait_ge(s["free"], b + 1)
                    for i in range(NT):
                        last = nc.vector.bn_stats(ST[n][:, i, :], X[:, b * NT + i, :])
                    last.then_inc(c_ln, 1)
                    link.k += 1
                    wait_apart(dve, c_ln, link.before + link.k)
                    for i in range(NT):
                        last = nc.vector.bn_aggr(MV[n][:, i, :], ST[n][:, i, :])
                    link(last)
                    link(nc.vector.tensor_scalar(RL[n][:, 0, :], MV[n][:, :, 1], 1e-5, None, ALU.add))
                    rsqrt(dve, nc, link, RL[n][:, 0, :], RL[n][:, 1, :], RL[n][:, 2, :])
                    link(nc.vector.scalar_tensor_tensor(out=RL[n][:, 3, :], in0=MV[n][:, :, 0], scalar=-1.0,
                                                        in1=RL[n][:, 1, :], op0=ALU.mult, op1=ALU.mult))
                    nc.vector.tensor_copy(RL[n][:, 2, 0:1], RL[n][:, 3, 0:1]).then_inc(s["mean"], 1)
                    link.done()

                def rows_of(n, v):
                    return ROWS[n][:, v, :].unsqueeze(1).to_broadcast([P, NT, D])

                def h(n, b):
                    link = Linker(dve, c_h, b, 3)
                    dve.wait_ge(s["z"], b + 1)
                    dve.wait_ge(s["rows%d" % n], 16 * (b - n) // 2 + 16 if isinstance(b, int) else 8 * (b - n) + 16)
                    link(nc.vector.tensor_tensor(H[n][:], H[n][:], rows_of(n, 1), ALU.mult))
                    link(nc.vector.tensor_tensor(H[n][:], H[n][:], rows_of(n, 0), ALU.add))
                    for i in range(NT):
                        last = nc.vector.scalar_tensor_tensor(out=JUNK[n][:].rearrange("p a b -> p (a b)")[:, i * D:(i + 1) * D], in0=H[n][:, i, :], scalar=1.0,
                                                              in1=WR[:], op0=ALU.mult, op1=ALU.mult,
                                                              accum_out=SCR[n][:, i:i + 1])
                    link(last)
                    nc.vector.tensor_tensor(DG[n][:], ident[:].unsqueeze(1).to_broadcast([P, NT, P]),
                                            bcast(SCR[n][:], P), ALU.mult).then_inc(s["diagonals"], 1)
                    link.done()

                def junk(n, i):
                    if i >= 6:
                        return JUNK[n][:, i - 6, :]
                    r = (EX, ET)[i // 3][n][:].rearrange("p h k -> p (h k)").bitcast(BF16)
                    return r[:, (i % 3) * 9 * P:(i % 3 + 1) * 9 * P]

                def rank(n, b):
                    link = Linker(dve, c_rank, b, 2)
                    dve.wait_ge(s["score_rows"], b + 1)
                    for i in range(NT):
                        sc, at = SCR[n][:, i:i + 1], 0
                        for c in range(2):
                            lo, hi = c * 4, c * 4 + 4
                            if i < hi:
                                a = max(i, lo)
                                at += (hi - a) * P
                                last = nc.vector.tensor_scalar(junk(n, i)[:, at - (hi - a) * P:at], BK[n][c][:, (a - lo) * P:], sc, 0.0,
                                                               ALU.is_gt, ALU.add, accum_out=CNT[n][:, i, c:c + 1])
                            if i > lo:
                                a = min(i, hi)
                                at += (a - lo) * P
                                last = nc.vector.tensor_scalar(junk(n, i)[:, at - (a - lo) * P:at], BK[n][c][:, 0:(a - lo) * P], sc, 0.0,
                                                               ALU.is_ge, ALU.add, accum_out=CNT[n][:, i, 2 + c:3 + c])
                        last = nc.vector.scalar_tensor_tensor(out=junk(n, i)[:, at:at + P],
                                                              in0=BK[n][i // 4][:, (i % 4) * P:(i % 4 + 1) * P], scalar=sc,
                                                              in1=LOW[:], op0=ALU.is_equal, op1=ALU.mult,
                                                              accum_out=CNT[n][:, i, 4:5])
                    link(last)
                    link(nc.vector.tensor_reduce(RANK[n][:], CNT[n][:], AX.X, ALU.add))
                    link.done()
                    nc.vector.tensor_tensor(PM[n][:], RANKS[:].unsqueeze(1).to_broadcast([P, NT, P]),
                                            bcast(RANK[n][:], P), ALU.is_equal).then_inc(s["one_hot"], 1)

                def normed(src_of, ready, name, which, chain):
                    def step(n, b):
                        link = Linker(dve, chain, b, 1 + RSQRT_LINKS)
                        dve.wait_ge(s[ready], b + 1)
                        link(nc.vector.tensor_scalar(SM[n][:, which, 1:2], SM[n][:, which, 0:1], 1.0 / D, 1e-6, ALU.mult,
                                                     ALU.add))
                        rsqrt(dve, nc, link, SM[n][:, which, 1:2], SM[n][:, which, 2:3], SM[n][:, which, 3:4])
                        nc.vector.tensor_scalar(U[n][:], src_of[n][:], SM[n][:, which, 2:3], None, ALU.mult).then_inc(s[name], 1)
                        link.done()
                    return step

                def v_out(n, b):
                    dve.wait_ge(s["qkv"], b + 1)
                    nc.vector.tensor_copy(V[n][:, :, 0:DK],
                                          BK[n][2][:, D:2 * D].rearrange("p (h d) -> p h d", d=DK)).then_inc(s["v_out"], 1)

                def row_max(n, b):
                    link = Linker(dve, c_max, b, 1)
                    dve.wait_ge(s["scores"], b + 1)
                    for r in range(4):
                        last = nc.vector.tensor_reduce(MX[n][:, 0, r::4],
                                                       BK[n][r][:, :].rearrange("p (a b) -> p a b", a=4), AX.X, ALU.max)
                    link(last)
                    nc.vector.tensor_scalar(MX[n][:, 1, :], MX[n][:, 0, :], -(DK ** -0.5), None, ALU.mult).then_inc(s["max"], 1)
                    link.done()

                def exp_t_out(n, b):
                    dve.wait_ge(s["expT"], b + 1)
                    for c in range(2, 4):
                        last = nc.vector.tensor_copy(ET[n][:, 4 * c:4 * c + 4, :],
                                                     BK[n][c][:, :].rearrange("p (a b) -> p a b", a=4))
                    last.then_inc(s["expT_out_v"], 1)

                def heads_out(n, b):
                    link = Linker(dve, c_heads, b, 1)
                    dve.wait_ge(s["heads"], b + 1)
                    o = BK[n][0][:, 0:NH * (DK + 1)].rearrange("p (h e) -> p h e", e=DK + 1)
                    link(nc.vector.reciprocal(MX[n][:, 0, :], o[:, :, DK]))
                    nc.vector.tensor_tensor(U[n][:].rearrange("p (h d) -> p h d", d=DK), o[:, :, 0:DK],
                                            bcast(MX[n][:, 0, :], DK), ALU.mult).then_inc(s["heads_out"], 1)
                    link.done()

                def xa(n, b):
                    dve.wait_ge(s["attended"], b + 1)
                    nc.vector.tensor_tensor(XA[n][:], BK[n][2][:, 0:D], SEL[n][:], ALU.add).then_inc(s["xa"], 1)

                def gated(n, b):
                    link = Linker(dve, c_gate, b, 1)
                    dve.wait_ge(s["tanh"], b + 1)
                    k = (NF - 4) * P
                    nc.vector.scalar_tensor_tensor(out=TH[n][:, 0:4 * P], in0=TH[n][:, 0:4 * P], scalar=1.0,
                                                   in1=BK[n][0][:, :], op0=ALU.add, op1=ALU.mult)
                    link(nc.vector.scalar_tensor_tensor(out=TH[n][:, 4 * P:], in0=TH[n][:, 4 * P:], scalar=1.0,
                                                        in1=BK[n][1][:, 0:k], op0=ALU.add, op1=ALU.mult))
                    nc.vector.tensor_tensor(GH[n][:, 0:4 * P], TH[n][:, 0:4 * P], BK[n][3][:, :], ALU.mult)
                    nc.vector.tensor_tensor(GH[n][:, 4 * P:], TH[n][:, 4 * P:], BK[n][1][:, 2 * P:2 * P + k],
                                            ALU.mult).then_inc(s["gated"], 1)
                    link.done()

                def add_x(n, b):
                    link = Linker(dve, c_x, b, 1)
                    dve.wait_ge(s["scattered"], b + 1)
                    for m in range(4):
                        last = nc.vector.tensor_tensor(H[n][:, 2 * m:2 * m + 2, :],
                                                       BK[n][m][:, :].rearrange("p (a b) -> p a b", a=2),
                                                       ROWS[n][:, 2, :].unsqueeze(1).to_broadcast([P, 2, D]), ALU.mult)
                    link(last)
                    xb = X[:, bass.ds(b * NT, NT), :]
                    nc.vector.tensor_tensor(xb, xb, H[n][:], ALU.add).then_inc(s["free"], 1)
                    link.done()

                with dve.Fori(0, B // 2) as j:
                    for step in (mean, h, rank, normed(SEL, "sum1", "u1", 0, c_u1), v_out, row_max, exp_t_out, heads_out,
                                 xa, normed(XA, "sum2", "u2", 1, c_u2), gated, add_x):
                        both(step, j)


def time_mixing(nc, sem, g, w):
    with ExitStack() as st:
        def sb(name, shape, dtype=F32):
            return st.enter_context(nc.sbuf_tensor("t_" + name, shape, dtype))

        WT = sb("WT", [P, 3, 2, D])
        WO = sb("WO", [P, 2, D])
        COL = sb("COL", [P, 5, 2])
        with ExitStack() as tmp:
            WN = tmp.enter_context(nc.sbuf_tensor("t_WN", [P, 3, 2, D], F32))
            names = ("time_decay", "time_first", "time_mix_k", "time_mix_v", "time_mix_r")
            loads = [(COL[:, m, :], w[n].rearrange("(h p) -> p h", p=P)) for m, n in enumerate(names)]
            loads += [(WN[:, m], w[n].rearrange("(h p) c -> p h c", p=P)) for m, n in enumerate(("Wk", "Wv", "Wr"))]
            loads += [(WO[:], w["Wo"].rearrange("(h p) c -> p h c", p=P))]
            jobs = [(WN[:, m, o, h * P:(h + 1) * P], WT[:, m, h, o * P:(o + 1) * P], 1.0)
                    for m in range(3) for o in range(2) for h in range(2)]
            transpose_weights(nc, sem, g, "t_weights", jobs, loads)

        EW, EU = sb("EW", [P, 2]), sb("EU", [P, 2])
        S2 = range(2)
        WS, WOG = [sb(f"WS{s}", [P, 2, D]) for s in S2], [sb(f"WOG{s}", [P, 2, D]) for s in S2]
        ST, MV = [sb(f"ST{s}", [P, NT, 6]) for s in S2], [sb(f"MV{s}", [P, NT, 2]) for s in S2]
        RL = [sb(f"RL{s}", [P, 4, NT]) for s in S2]
        Z = [sb(f"Z{s}", [P, NT, D]) for s in S2]
        HT = [sb(f"HT{s}", [P, 2, T + 1]) for s in S2]
        XK = [sb(f"XK{s}", [P, 2, T + 1]) for s in S2]
        XV = [sb(f"XV{s}", [P, 2, T]) for s in S2]
        XR = [sb(f"XR{s}", [P, 2, T]) for s in S2]
        EK = [sb(f"EK{s}", [P, 2, T]) for s in S2]
        EKV = [sb(f"EKV{s}", [P, 2, T]) for s in S2]
        DIFF = [Z[s][:].rearrange("p (h i) c -> p h (i c)", h=2) for s in S2]
        TH = DIFF
        SA_, SB_ = HT, XK
        REC = XV
        Y = XR
        BK = [[st.enter_context(nc.psum_tensor(f"t_BK{s}{n}", [P, 512], F32)) for n in range(4)] for s in S2]
        X, ident, MOD = g["X"], g["ident"], g["MOD"]
        names = ["zero", "decay", "eu_ew", "half", "free", "wo_scaled", "woT", "woT_out", "mean", "z", "zT", "h",
                 "difference", "mixed", "k", "exp_k", "v", "exp_kv", "r", "tanh_r", "y", "projected"]
        s = {n: sem("t_" + n) for n in names}
        c_ln, c_scan = sem("t_chain_ln"), sem("t_chain_scan")

        def both(step, j):
            for n in range(2):
                step(n, 2 * j + n)

        with nc.Block() as block:
            @block.gpsimd
            def _(pool):
                for n in S2:
                    nc.gpsimd.memset(HT[n][:, :, 0], 0.0).then_inc(s["zero"], 1)
                    nc.gpsimd.memset(XK[n][:, :, 0], 0.0).then_inc(s["zero"], 1)

                def difference(n, b):
                    pool.wait_ge(s["h"], b + 1)
                    nc.gpsimd.tensor_tensor(DIFF[n], HT[n][:, :, 1:T + 1], HT[n][:, :, 0:T],
                                            ALU.subtract).then_inc(s["difference"], 1)

                with pool.Fori(0, B // 2) as j:
                    both(difference, j)

            @block.tensor
            def _(pe):
                def wo_t(n, b):
                    pe.wait_ge(s["wo_scaled"], b + 1)
                    for o in range(2):
                        for h in range(2):
                            last = nc.tensor.transpose(BK[n][0][:, h * D + o * P:h * D + (o + 1) * P],
                                                       WS[n][:, o, h * P:(h + 1) * P], ident[:])
                    last.then_inc(s["woT"], 1)

                def z_t(n, b):
                    pe.wait_ge(s["woT_out"], b + 1)
                    pe.wait_ge(s["z"], b + 1)
                    for h in range(2):
                        for i in range(NT):
                            last = nc.tensor.transpose(BK[n][2 * h + i // 4][:, (i % 4) * P:(i % 4 + 1) * P],
                                                       Z[n][:, i, h * P:(h + 1) * P], ident[:])
                    last.then_inc(s["zT"], 1)

                def project(m, x, off, name, before):
                    def step(n, b):
                        pe.wait_ge(s["mixed"], b + 1)
                        if before:
                            pe.wait_ge(s[before], b + 1)
                        for o in range(2):
                            for c in range(2):
                                for h in range(2):
                                    last = nc.tensor.matmul(BK[n][2 * o + c][:, :], WT[:, m, h, o * P:(o + 1) * P],
                                                            x[n][:, h, off + c * 512:off + (c + 1) * 512],
                                                            start=(h == 0), stop=(h == 1))
                        last.then_inc(s[name], 1)
                    return step

                def project_out(n, b):
                    pe.wait_ge(s["y"], b + 1)
                    for i in range(NT):
                        for h in range(2):
                            last = nc.tensor.matmul(BK[n][i // 2][:, (i % 2) * D:(i % 2 + 1) * D],
                                                    Y[n][:, h, i * P:(i + 1) * P], WOG[n][:, h, :],
                                                    start=(h == 0), stop=(h == 1))
                    last.then_inc(s["projected"], 1)

                with pe.Fori(0, B // 2) as j:
                    for step in (wo_t, z_t, project(0, XK, 1, "k", None), project(1, XV, 0, "v", "exp_k"),
                                 project(2, XR, 0, "r", "exp_kv"), project_out):
                        both(step, j)

            @block.scalar
            def _(act):
                nc.scalar.activation(EU[:], COL[:, 1, :], ACT.Exp)
                nc.scalar.activation(EW[:], COL[:, 0, :], ACT.Exp).then_inc(s["decay"], 1)
                act.wait_ge(s["decay"], 1)
                nc.scalar.activation(EW[:], EW[:], ACT.Exp, scale=-1.0).then_inc(s["eu_ew"], 1)
                nc.scalar.activation(WO[:], WO[:], ACT.Copy, scale=0.5).then_inc(s["half"], 1)
                act.wait_ge(s["half"], 1)
                act.wait_ge(s["zero"], 4)

                def scale_wo(n, b):
                    act.wait_ge(s["free"], b + 1)
                    for h in range(2):
                        last = nc.scalar.activation(WS[n][:, h, :], WO[:, h, :], ACT.Identity,
                                                    scale=MOD[:, 1, 2 * GA + h, bass.ds(b, 1)])
                    last.then_inc(s["wo_scaled"], 1)

                def wo_out(n, b):
                    act.wait_ge(s["woT"], b + 1)
                    nc.scalar.activation(WOG[n][:], BK[n][0][:, :].rearrange("p (h c) -> p h c", h=2),
                                         ACT.Copy).then_inc(s["woT_out"], 1)

                def z(n, b):
                    act.wait_ge(s["mean"], b + 1)
                    for i in range(NT):
                        last = nc.scalar.activation(Z[n][:, i, :], X[:, b * NT + i, :], ACT.Identity,
                                                    bias=RL[n][:, 3, i:i + 1], scale=RL[n][:, 1, i:i + 1])
                    last.then_inc(s["z"], 1)

                def h_t(n, b):
                    act.wait_ge(s["zT"], b + 1)
                    for h in range(2):
                        for c in range(2):
                            last = nc.scalar.activation(HT[n][:, h, 1 + c * 512:1 + (c + 1) * 512], BK[n][2 * h + c][:, :],
                                                        ACT.Identity, bias=MOD[:, 1, 2 * SA + h, bass.ds(b, 1)],
                                                        scale=MOD[:, 1, 2 * CA + h, bass.ds(b, 1)])
                    last.then_inc(s["h"], 1)

                def unary(out, func, scale, ready, name):
                    def step(n, b):
                        act.wait_ge(s[ready], b + 1)
                        for o in range(2):
                            for c in range(2):
                                last = nc.scalar.activation(out[n][:, o, c * 512:(c + 1) * 512], BK[n][2 * o + c][:, :],
                                                            func, scale=scale)
                        last.then_inc(s[name], 1)
                    return step

                with act.Fori(0, B // 2) as j:
                    for step in (scale_wo, wo_out, z, h_t, unary(EK, ACT.Exp, 1.0, "k", "exp_k"),
                                 unary(TH, ACT.Tanh, 0.5, "r", "tanh_r")):
                        both(step, j)

            @block.vector
            def _(dve):
                for n in S2:
                    nc.vector.memset(RL[n][:], 0.0).then_inc(s["free"], 1)
                dve.wait_ge(s["eu_ew"], 1)
                dve.wait_ge(s["zero"], 4)

                def mean(n, b):
                    link = Linker(dve, c_ln, b, 4 + RSQRT_LINKS)
                    dve.wait_ge(s["free"], b + 1)
                    for i in range(NT):
                        last = nc.vector.bn_stats(ST[n][:, i, :], X[:, b * NT + i, :])
                    last.then_inc(c_ln, 1)
                    link.k += 1
                    wait_apart(dve, c_ln, link.before + link.k)
                    for i in range(NT):
                        last = nc.vector.bn_aggr(MV[n][:, i, :], ST[n][:, i, :])
                    link(last)
                    link(nc.vector.tensor_scalar(RL[n][:, 0, :], MV[n][:, :, 1], 1e-5, None, ALU.add))
                    rsqrt(dve, nc, link, RL[n][:, 0, :], RL[n][:, 1, :], RL[n][:, 2, :])
                    link(nc.vector.scalar_tensor_tensor(out=RL[n][:, 3, :], in0=MV[n][:, :, 0], scalar=-1.0,
                                                        in1=RL[n][:, 1, :], op0=ALU.mult, op1=ALU.mult))
                    nc.vector.tensor_copy(RL[n][:, 2, 0:1], RL[n][:, 3, 0:1]).then_inc(s["mean"], 1)
                    link.done()

                def mix(n, b):
                    dve.wait_ge(s["difference"], b + 1)
                    for m, (x, off) in enumerate(((XK, 1), (XV, 0), (XR, 0))):
                        for h in range(2):
                            last = nc.vector.scalar_tensor_tensor(
                                out=x[n][:, h, off:off + T], in0=DIFF[n][:, h, :], scalar=COL[:, 2 + m, h:h + 1],
                                in1=HT[n][:, h, 0:T], op0=ALU.mult, op1=ALU.add)
                    last.then_inc(s["mixed"], 1)

                def exp_kv(n, b):
                    dve.wait_ge(s["exp_k"], b + 1)
                    dve.wait_ge(s["v"], b + 1)
                    for o in range(2):
                        for c in range(2):
                            cols = slice(c * 512, (c + 1) * 512)
                            last = nc.vector.tensor_tensor(EKV[n][:, o, cols], EK[n][:, o, cols], BK[n][2 * o + c][:, :], ALU.mult)
                    last.then_inc(s["exp_kv"], 1)

                def scan(n, b):
                    link = Linker(dve, c_scan, b, 4)
                    dve.wait_ge(s["exp_kv"], b + 1)
                    for state, x in ((SA_, EKV), (SB_, EK)):
                        for h in range(2):
                            last = nc.vector.tensor_tensor_scan(state[n][:, h, 1:T + 1], EW[:, h:h + 1].to_broadcast([P, T]),
                                                                x[n][:, h, :], 0.0, ALU.mult, ALU.add)
                    link(last)
                    for state, x in ((SB_, EK), (SA_, EKV)):
                        for h in range(2):
                            last = nc.vector.scalar_tensor_tensor(out=x[n][:, h, :], in0=x[n][:, h, :], scalar=EU[:, h:h + 1],
                                                                  in1=state[n][:, h, 0:T], op0=ALU.mult, op1=ALU.add)
                    link(last)
                    link(nc.vector.reciprocal(REC[n][:], EK[n][:]))
                    link(nc.vector.tensor_tensor(EK[n][:], EKV[n][:], REC[n][:], ALU.mult))
                    dve.wait_ge(s["tanh_r"], b + 1)
                    nc.vector.scalar_tensor_tensor(out=Y[n][:], in0=TH[n], scalar=1.0, in1=EK[n][:], op0=ALU.add,
                                                   op1=ALU.mult).then_inc(s["y"], 1)
                    link.done()

                def add_x(n, b):
                    dve.wait_ge(s["projected"], b + 1)
                    for m in range(4):
                        xt = X[:, bass.ds(b * NT + 2 * m, 2), :]
                        last = nc.vector.tensor_tensor(xt, BK[n][m][:, :].rearrange("p (a b) -> p a b", a=2), xt, ALU.add)
                    last.then_inc(s["free"], 1)

                with dve.Fori(0, B // 2) as j:
                    for step in (mean, mix, exp_kv, scan, add_x):
                        both(step, j)


def expert_layer(nc, sem, g, w, out):
    with ExitStack() as st:
        def sb(name, shape, dtype=F32):
            return st.enter_context(nc.sbuf_tensor("e_" + name, shape, dtype))

        S2 = range(2)
        NTT = B * NT
        GN, GW = sb("GN", [NE, D]), sb("GW", [P, 2, NE])
        ONES, PREF = sb("ONES", [P, P]), sb("PREF", [P, NE])
        ST, MV = [sb(f"ST{s}", [P, NT, 6]) for s in S2], [sb(f"MV{s}", [P, NT, 2]) for s in S2]
        RL = [sb(f"RL{s}", [P, 4, NT]) for s in S2]
        Z = [sb(f"Z{s}", [P, NT, D]) for s in S2]
        HT = [sb(f"HT{s}", [P, 2, T]) for s in S2]
        PROB, EQ, TOP = (sb(n, [P, NTT, NE]) for n in ("PROB", "EQ", "TOP"))
        TOP2, COMB = sb("TOP2", [P, NTT, NE]), sb("COMB", [P, NTT, NE])
        RED = sb("RED", [P, NTT])
        CNT, KEEP, ANY = sb("CNT", [P, NE]), sb("KEEP", [P, NE]), sb("ANY", [P, 1])
        FLAG = sb("FLAG", [P, 1], I32)
        W1, W2 = sb("W1", [P, 2, D]), sb("W2", [P, 2, D])
        B1, B2 = sb("B1", [P, 2]), sb("B2", [P, D])
        U, YB, ACC = sb("U", [P, 2, T]), sb("YB", [P, NT, D]), sb("ACC", [P, NT, D])
        GROW = sb("GROW", [P, D])
        BK = [[st.enter_context(nc.psum_tensor(f"e_BK{s}{n}", [P, 512], F32)) for n in range(4)] for s in S2]
        X, ident, MOD = g["X"], g["ident"], g["MOD"]
        s = {n: sem("e_" + n) for n in ("stored", "constants", "gate_loaded", "gateT", "gateT_out", "free", "mean",
                                        "z", "zT", "h", "logits", "shifted", "exp", "counted", "counts", "flag")}
        f = {n: sem("e_full_" + n) for n in ("free", "mean", "z", "zT", "h", "row", "weights", "hidden", "relu", "outputs",
                                             "expert_done", "cleared", "gated", "stored")}
        c_ln, c_top, c_expert = (sem("e_chain_" + n) for n in ("ln", "top", "expert"))
        xo = out.rearrange("b (i p) c -> p (b i) c", p=P)

        def both(step, j):
            for n in range(2):
                step(n, 2 * j + n)

        def z_t(pe, n, b, sm):
            pe.wait_ge(sm["z"], b + 1)
            for h in range(2):
                for i in range(NT):
                    last = nc.tensor.transpose(BK[n][2 * h + i // 4][:, (i % 4) * P:(i % 4 + 1) * P],
                                               Z[n][:, i, h * P:(h + 1) * P], ident[:])
            last.then_inc(sm["zT"], 1)

        def z_rows(act, n, b, sm):
            act.wait_ge(sm["mean"], b + 1)
            for i in range(NT):
                last = nc.scalar.activation(Z[n][:, i, :], X[:, bass.ds(b * NT + i, 1), :].rearrange("p a c -> p (a c)"),
                                            ACT.Identity, bias=RL[n][:, 3, i:i + 1], scale=RL[n][:, 1, i:i + 1])
            last.then_inc(sm["z"], 1)

        def h_t(act, n, b, sm):
            act.wait_ge(sm["zT"], b + 1)
            for h in range(2):
                for c in range(2):
                    last = nc.scalar.activation(HT[n][:, h, c * 512:(c + 1) * 512], BK[n][2 * h + c][:, :], ACT.Identity,
                                                bias=MOD[:, 1, 2 * SB + h, bass.ds(b, 1)],
                                                scale=MOD[:, 1, 2 * CB + h, bass.ds(b, 1)])
            last.then_inc(sm["h"], 1)

        def mean(dve, n, b, sm, links_before):
            link = Linker(dve, c_ln, b + links_before, 4 + RSQRT_LINKS)
            dve.wait_ge(sm["free"], b + 1)
            for i in range(NT):
                last = nc.vector.bn_stats(ST[n][:, i, :], X[:, b * NT + i, :])
            last.then_inc(c_ln, 1)
            link.k += 1
            wait_apart(dve, c_ln, link.before + link.k)
            for i in range(NT):
                last = nc.vector.bn_aggr(MV[n][:, i, :], ST[n][:, i, :])
            link(last)
            link(nc.vector.tensor_scalar(RL[n][:, 0, :], MV[n][:, :, 1], 1e-5, None, ALU.add))
            rsqrt(dve, nc, link, RL[n][:, 0, :], RL[n][:, 1, :], RL[n][:, 2, :])
            link(nc.vector.scalar_tensor_tensor(out=RL[n][:, 3, :], in0=MV[n][:, :, 0], scalar=-1.0,
                                                in1=RL[n][:, 1, :], op0=ALU.mult, op1=ALU.mult))
            nc.vector.tensor_copy(RL[n][:, 2, 0:1], RL[n][:, 3, 0:1]).then_inc(sm["mean"], 1)
            link.done()

        with nc.Block() as block:
            @block.sync
            def _(sp):
                sp.dma_start(GN[:], w["gate_w"]).then_inc(s["gate_loaded"], 16)
                sp.dma_start(xo, X[:]).then_inc(s["stored"], 16)
                sp.wait_ge(s["flag"], 1)
                kept = sp.value_load(FLAG[0:1, 0:1], min_val=0, max_val=1)
                with sp.If(kept > 0):
                    with sp.Fori(0, B) as b:
                        sp.wait_ge(f["free"], b + 1)
                        sp.dma_start(GROW[:].rearrange("p (h c) -> p h c", h=2),
                                     g["mod_dram"][1, 2 * GB:2 * GB + 2, bass.ds(b, 1), :].rearrange(
                                         "v b c -> b v c").to_broadcast([P, 2, P])).then_inc(f["row"], 16)
                        with sp.Fori(0, NE) as e:
                            sp.wait_ge(f["expert_done"], b * NE + e + 1)
                            ex = bass.ds(e, 1)
                            sp.dma_start(W1[:], w["W1"][ex].rearrange("e (h p) c -> p (e h) c", p=P)).then_inc(f["weights"], 16)
                            sp.dma_start(W2[:], w["W2"][ex].rearrange("e (h p) c -> p (e h) c", p=P)).then_inc(f["weights"], 16)
                            sp.dma_start(B1[:], w["b1"][ex].rearrange("e (h p) -> p (e h)", p=P),
                                         allow_slow_non_contiguous=True).then_inc(f["weights"], 16)
                            sp.dma_start(B2[:], w["b2"][ex].to_broadcast([P, D])).then_inc(f["weights"], 16)
                    sp.wait_ge(f["free"], B + 1)
                    sp.dma_start(xo, X[:]).then_inc(f["stored"], 16)
                    sp.wait_ge(f["stored"], 16)
                sp.wait_ge(s["stored"], 16)

            @block.gpsimd
            def _(pool):
                nc.gpsimd.memset(ONES[:], 1.0).then_inc(s["constants"], 1)
                nc.gpsimd.iota(PREF[:], pattern=[[-1, NE]], base=NE, channel_multiplier=0,
                               allow_small_or_imprecise_dtypes=True).then_inc(s["constants"], 1)

            @block.tensor
            def _(pe):
                pe.wait_ge(s["gate_loaded"], 16)
                for h in range(2):
                    last = nc.tensor.transpose(BK[0][0][:, h * NE:(h + 1) * NE], GN[:, h * P:(h + 1) * P], ident[0:NE, 0:NE])
                last.then_inc(s["gateT"], 1)
                pe.wait_ge(s["gateT_out"], 1)

                def logits(n, b):
                    pe.wait_ge(s["h"], b + 1)
                    for i in range(NT):
                        for h in range(2):
                            last = nc.tensor.matmul(BK[n][0][:, i * NE:(i + 1) * NE], HT[n][:, h, i * P:(i + 1) * P],
                                                    GW[:, h, :], start=(h == 0), stop=(h == 1))
                    last.then_inc(s["logits"], 1)

                with pe.Fori(0, B // 2) as j:
                    both(lambda n, b: z_t(pe, n, b, s), j)
                    both(logits, j)
                pe.wait_ge(s["counted"], 1)
                nc.tensor.matmul(BK[0][0][:, 0:NE], ONES[:], CNT[:], start=True, stop=True).then_inc(s["counts"], 1)
                pe.wait_ge(s["flag"], 1)
                kept = pe.value_load(FLAG[0:1, 0:1], min_val=0, max_val=1)
                with pe.If(kept > 0):
                    with pe.Fori(0, B) as b:
                        z_t(pe, 0, b, f)
                        wait_apart(pe, f["h"], b + 1)
                        with pe.Fori(0, NE) as e:
                            pe.wait_ge(f["weights"], 64 * (b * NE + e) + 64)
                            for o in range(2):
                                for c in range(2):
                                    for h in range(2):
                                        last = nc.tensor.matmul(BK[0][2 * o + c][:, :], W1[:, h, o * P:(o + 1) * P],
                                                                HT[0][:, h, c * 512:(c + 1) * 512], start=(h == 0), stop=(h == 1))
                            last.then_inc(f["hidden"], 1)
                            pe.wait_ge(f["relu"], b * NE + e + 1)
                            for i in range(NT):
                                for h in range(2):
                                    last = nc.tensor.matmul(BK[1][i // 2][:, (i % 2) * D:(i % 2 + 1) * D],
                                                            U[:, h, i * P:(i + 1) * P], W2[:, h, :], start=(h == 0), stop=(h == 1))
                            last.then_inc(f["outputs"], 1)

            @block.scalar
            def _(act):
                with act.Fori(0, B // 2) as j:
                    both(lambda n, b: z_rows(act, n, b, s), j)
                    both(lambda n, b: h_t(act, n, b, s), j)
                act.wait_ge(s["shifted"], 1)
                nc.scalar.activation(PROB[:], PROB[:], ACT.Exp).then_inc(s["exp"], 1)
                act.wait_ge(s["flag"], 1)
                kept = act.value_load(FLAG[0:1, 0:1], min_val=0, max_val=1)
                with act.If(kept > 0):
                    with act.Fori(0, B) as b:
                        z_rows(act, 0, b, f)
                        h_t(act, 0, b, f)
                        with act.Fori(0, NE) as e:
                            act.wait_ge(f["hidden"], b * NE + e + 1)
                            for o in range(2):
                                for c in range(2):
                                    last = nc.scalar.activation(U[:, o, c * 512:(c + 1) * 512], BK[0][2 * o + c][:, :],
                                                                ACT.Relu, bias=B1[:, o:o + 1])
                            last.then_inc(f["relu"], 1)

            @block.vector
            def _(dve):
                for n in S2:
                    nc.vector.memset(RL[n][:], 0.0).then_inc(s["free"], 1)
                dve.wait_ge(s["gateT"], 1)
                nc.vector.tensor_copy(GW[:], BK[0][0][:, 0:2 * NE].rearrange("p (h e) -> p h e", h=2)).then_inc(s["gateT_out"], 1)

                def logits_out(n, b):
                    dve.wait_ge(s["logits"], b + 1)
                    nc.vector.tensor_copy(PROB[:, bass.ds(b * NT, NT), :],
                                          BK[n][0][:, 0:NT * NE].rearrange("p (i e) -> p i e", e=NE)).then_inc(s["free"], 1)

                with dve.Fori(0, B // 2) as j:
                    both(lambda n, b: mean(dve, n, b, s, 0), j)
                    both(logits_out, j)

                link = Linker(dve, c_top, 0, 20)
                dve.wait_ge(s["free"], 2 + B)
                link(nc.vector.tensor_reduce(RED[:], PROB[:], AX.X, ALU.max))
                nc.vector.tensor_tensor(PROB[:], PROB[:], bcast(RED[:], NE), ALU.subtract).then_inc(s["shifted"], 1)
                dve.wait_ge(s["exp"], 1)
                link(nc.vector.tensor_reduce(RED[:], PROB[:], AX.X, ALU.add))
                link(nc.vector.reciprocal(RED[:], RED[:]))
                link(nc.vector.tensor_tensor(PROB[:], PROB[:], bcast(RED[:], NE), ALU.mult))
                dve.wait_ge(s["constants"], 2)
                pref = PREF[:].unsqueeze(1).to_broadcast([P, NTT, NE])
                for src, top in ((PROB, TOP), (COMB, TOP2)):
                    if src is COMB:
                        link(nc.vector.scalar_tensor_tensor(out=COMB[:], in0=TOP[:], scalar=-2.0, in1=PROB[:],
                                                            op0=ALU.mult, op1=ALU.add))
                    link(nc.vector.tensor_reduce(RED[:], src[:], AX.X, ALU.max))
                    link(nc.vector.tensor_tensor(EQ[:], src[:], bcast(RED[:], NE), ALU.is_equal))
                    link(nc.vector.tensor_tensor(EQ[:], EQ[:], pref, ALU.mult))
                    link(nc.vector.tensor_reduce(RED[:], EQ[:], AX.X, ALU.max))
                    link(nc.vector.tensor_tensor(top[:], EQ[:], bcast(RED[:], NE), ALU.is_equal))
                link(nc.vector.tensor_tensor(TOP[:], TOP[:], TOP2[:], ALU.add))
                nc.vector.tensor_reduce(CNT[:], TOP[:].rearrange("p t e -> p e t"), AX.X, ALU.add).then_inc(s["counted"], 1)
                dve.wait_ge(s["counts"], 1)
                link(nc.vector.tensor_scalar(KEEP[:], BK[0][0][:, 0:NE], float(EXPERT_CAP), None, ALU.is_le))
                link(nc.vector.tensor_reduce(ANY[:], KEEP[:], AX.X, ALU.max))
                nc.vector.tensor_copy(FLAG[:], ANY[:]).then_inc(s["flag"], 1)
                dve.wait_ge(s["flag"], 1)
                kept = dve.value_load(FLAG[0:1, 0:1], min_val=0, max_val=1)
                with dve.If(kept > 0):
                    link(nc.vector.tensor_tensor(COMB[:], PROB[:], TOP[:], ALU.mult))
                    link(nc.vector.tensor_tensor(COMB[:], COMB[:], KEEP[:].unsqueeze(1).to_broadcast([P, NTT, NE]), ALU.mult))
                    link.done()
                    nc.vector.memset(ST[0][:], 0.0).then_inc(f["free"], 1)
                    nc.vector.memset(ST[1][:], 0.0).then_inc(f["expert_done"], 1)
                    dve.wait_ge(s["stored"], 16)
                    with dve.Fori(0, B) as b:
                        mean(dve, 0, b, f, B)
                        nc.vector.memset(ACC[:], 0.0).then_inc(f["cleared"], 1)
                        with dve.Fori(0, NE) as e:
                            k = b * NE + e
                            dve.wait_ge(f["cleared"], b + 1)
                            dve.wait_ge(f["expert_done"], k + 1)
                            dve.wait_ge(f["weights"], 64 * k + 64)
                            dve.wait_ge(f["outputs"], k + 1)
                            for m in range(4):
                                last = nc.vector.tensor_tensor(YB[:, 2 * m:2 * m + 2, :],
                                                               BK[1][m][:, :].rearrange("p (a b) -> p a b", a=2),
                                                               B2[:].unsqueeze(1).to_broadcast([P, 2, D]), ALU.add)
                            last.then_inc(c_expert, 1)
                            dve.wait_ge(c_expert, k + 1)
                            for i in range(NT):
                                wt = COMB[:, bass.ds(b * NT + i, 1), bass.ds(e, 1)].rearrange("p a c -> p (a c)")
                                last = nc.vector.scalar_tensor_tensor(out=ACC[:, i, :], in0=YB[:, i, :], scalar=wt,
                                                                      in1=ACC[:, i, :], op0=ALU.mult, op1=ALU.add)
                            last.then_inc(f["expert_done"], 1)
                        dve.wait_ge(f["expert_done"], b * NE + NE + 1)
                        dve.wait_ge(f["row"], 16 * b + 16)
                        nc.vector.tensor_tensor(ACC[:], ACC[:], GROW[:].unsqueeze(1).to_broadcast([P, NT, D]),
                                                ALU.mult).then_inc(f["gated"], 1)
                        dve.wait_ge(f["gated"], b + 1)
                        xb = X[:, bass.ds(b * NT, NT), :]
                        nc.vector.tensor_tensor(xb, xb, ACC[:], ALU.add).then_inc(f["free"], 1)


def program(nc, a, out):
    with ExitStack() as st:
        def sem(name):
            return st.enter_context(nc.semaphore(name))

        def sb(name, shape):
            return st.enter_context(nc.sbuf_tensor(name, shape, F32))

        g = {"X": sb("X", [P, B * NT, D]), "MOD": sb("MOD", [P, 2, 12, B]), "ident": sb("ident", [P, P]),
             "ident16": st.enter_context(nc.sbuf_tensor("ident16", [P, P], F16)),
             "mod_dram": nc.dram_tensor("mod_dram", [2, 12, B, P], F32).ap()}
        modulation(nc, sem, g, [a["L0_c"], a["L1_c"]], [a["L0_wmod"], a["L1_wmod"]])
        softcap_attention(nc, sem, g, a["L0_attn_x"], a["L0_attn_w_q"], a["L0_attn_w_k"], a["L0_attn_w_v"],
                          a["L0_attn_w_o"])
        routed_block(nc, sem, g, {n: a["L0_ffn_" + n] for n in ("w_router", "W_qkv", "W_out", "g1", "g2", "W1", "W2", "W3")})
        time_mixing(nc, sem, g, {n: a["L1_attn_" + n] for n in ("time_decay", "time_first", "time_mix_k", "time_mix_v",
                                                                "time_mix_r", "Wk", "Wv", "Wr", "Wo")})
        expert_layer(nc, sem, g, {n: a["L1_ffn_" + n] for n in ("gate_w", "W1", "b1", "W2", "b2")}, out)


_INS = ["L0_attn_x", "L0_attn_w_q", "L0_attn_w_k", "L0_attn_w_v", "L0_attn_w_o", "L0_ffn_w_router", "L0_ffn_W_qkv",
        "L0_ffn_W_out", "L0_ffn_g1", "L0_ffn_g2", "L0_ffn_W1", "L0_ffn_W2", "L0_ffn_W3", "L0_c", "L0_wmod",
        "L1_attn_time_decay", "L1_attn_time_first", "L1_attn_time_mix_k", "L1_attn_time_mix_v", "L1_attn_time_mix_r",
        "L1_attn_Wk", "L1_attn_Wv", "L1_attn_Wr", "L1_attn_Wo", "L1_ffn_gate_w", "L1_ffn_W1", "L1_ffn_b1",
        "L1_ffn_W2", "L1_ffn_b2", "L1_c", "L1_wmod"]


def kernel(**inputs):
    import numpy as _np
    import concourse.bacc as _bacc
    from concourse import mybir as _mybir
    from concourse.bass_utils import run_bass_kernel_spmd as _run

    nc = _bacc.Bacc("TRN2", target_bir_lowering=False, num_devices=1)
    arrays, args = {}, {}
    for name in _INS:
        a = _np.ascontiguousarray(inputs[name])
        arrays[f"in_{name}_dram"] = a
        args[name] = nc.dram_tensor(f"in_{name}_dram", a.shape, _mybir.dt.from_np(a.dtype), kind="ExternalInput").ap()
    out = nc.dram_tensor("out_0_dram", [B, T, D], _mybir.dt.float32, kind="ExternalOutput").ap()
    program(nc, args, out)
    r = _run(nc, [arrays], core_ids=[0])
    return r.results[0]["out_0_dram"]
```

```python
import concourse.bass as bass
from concourse import mybir
from contextlib import ExitStack, contextmanager

F32 = mybir.dt.float32
F16 = mybir.dt.float16
BF16 = mybir.dt.bfloat16
I32 = mybir.dt.int32
ALU = mybir.AluOpType
ACT = mybir.ActivationFunctionType
AX = mybir.AxisListType

P = 128
B, T, D = 8, 1024, 256
NT = T // P
NH, DK = 16, 16
CAP = T // 8
DFF = 682
NE = 8
EXPERT_CAP = int(1.25 * B * T / NE)
RSQRT_MAGIC = 1597463007.0
SA, CA, GA, SB, CB, GB = range(6)


def rsqrt(dve, nc, link, x, y, t):
    link(nc.vector.tensor_scalar(y.bitcast(I32), x.bitcast(I32), -0.5, RSQRT_MAGIC, ALU.mult, ALU.add))
    for _ in range(3):
        link(nc.vector.scalar_tensor_tensor(out=t, in0=x, scalar=-0.5, in1=y, op0=ALU.mult, op1=ALU.mult))
        link(nc.vector.tensor_tensor(t, t, y, ALU.mult))
        link(nc.vector.scalar_tensor_tensor(out=y, in0=t, scalar=1.5, in1=y, op0=ALU.add, op1=ALU.mult))


RSQRT_LINKS = 10


def wait_apart(eng, sem, value):
    eng.wait_ge(sem, value)
    if not isinstance(value, int):
        eng.nop(nofuse=True)


def bcast(ap, n):
    return ap.unsqueeze(len(ap.shape)).to_broadcast(list(ap.shape) + [n])


class Linker:

    def __init__(self, eng, sem, batch, steps):
        self.eng, self.sem, self.before, self.steps, self.k = eng, sem, batch * steps, steps, 0

    def __call__(self, ins):
        ins.then_inc(self.sem, 1)
        self.k += 1
        self.eng.wait_ge(self.sem, self.before + self.k)

    def done(self):
        assert self.k == self.steps, (self.k, self.steps)


def modulation(nc, sem, g, cs, wmods):
    with ExitStack() as st:
        c_nat = st.enter_context(nc.sbuf_tensor("c_nat", [B, 2, D], F32))
        c_tanh = st.enter_context(nc.sbuf_tensor("c_tanh", [B, 2, D], F32))
        c_silu = st.enter_context(nc.sbuf_tensor("c_silu", [B, 2, D], F32))
        cT = st.enter_context(nc.sbuf_tensor("cT", [P, 2, 2, B], F32))
        wmod = st.enter_context(nc.sbuf_tensor("wmod", [P, 2, 2, 6 * D], F32))
        gate = st.enter_context(nc.sbuf_tensor("gate", [P, 2, 2, 2, 2, B], F32))
        ps_c = st.enter_context(nc.psum_tensor("ps_c", [P, 2, 2, B], F32))
        ps_m = st.enter_context(nc.psum_tensor("ps_m", [P, 2, 12, B], F32))
        mod_rows = st.enter_context(nc.sbuf_tensor("mod_rows", [12 * B, 2, P], F32))
        ps_r = st.enter_context(nc.psum_tensor("ps_r", [12 * B, 2, P], F32))
        s_ld, s_wm = sem("mod_c_loaded"), sem("mod_w_loaded")
        s_done, s_rt, s_rows, s_st = sem("mod_done"), sem("mod_rows_transposed"), sem("mod_rows"), sem("mod_stored")
        s_id, s_th, s_silu, s_ct, s_cte, s_mm = (sem("mod_" + n) for n in
            ("identity", "tanh", "silu", "c_transposed", "cT", "product"))
        s_dve = sem("mod_dve_chain")
        ident, MOD = g["ident"], g["MOD"]
        with nc.Block() as block:
            @block.sync
            def _(sp):
                for l in range(2):
                    sp.dma_start(c_nat[:, l, :], cs[l]).then_inc(s_ld, 16)
                for l in range(2):
                    sp.dma_start(wmod[:, l, :, :], wmods[l].rearrange("(h p) n -> p h n", p=P)).then_inc(s_wm, 16)
                sp.wait_ge(s_rows, 1)
                for l in range(2):
                    sp.dma_start(g["mod_dram"][l].rearrange("v b c -> (v b) c"), mod_rows[:, l, :]).then_inc(s_st, 16)
                sp.wait_ge(s_st, 32)

            @block.gpsimd
            def _(pool):
                nc.gpsimd.memset(ident[:], 0.0).then_inc(s_id, 1)
                pool.wait_ge(s_id, 1)
                nc.gpsimd.affine_select(out=ident[:], in_=ident[:], compare_op=ALU.not_equal, fill=1.0, base=0,
                                        pattern=[[-1, P]], channel_multiplier=1).then_inc(s_id, 1)

            @block.scalar
            def _(act):
                act.wait_ge(s_ld, 32)
                nc.scalar.activation(c_tanh[:], c_nat[:], ACT.Tanh, scale=0.5).then_inc(s_th, 1)

            @block.vector
            def _(dve):
                link = Linker(dve, s_dve, 0, 5)
                dve.wait_ge(s_th, 1)
                dve.wait_ge(s_id, 2)
                link(nc.vector.scalar_tensor_tensor(out=c_silu[:], in0=c_tanh[:], scalar=1.0, in1=c_nat[:],
                                                    op0=ALU.add, op1=ALU.mult))
                nc.vector.tensor_scalar(c_silu[:], c_silu[:], 0.5, None, ALU.mult).then_inc(s_silu, 1)
                dve.wait_ge(s_ct, 1)
                nc.vector.tensor_copy(cT[:], ps_c[:]).then_inc(s_cte, 1)
                dve.wait_ge(s_mm, 1)
                link(nc.vector.tensor_copy(MOD[:], ps_m[:]))
                v = MOD[:].rearrange("p l (a b h) n -> p l a b h n", a=2, b=3)
                for l in range(2):
                    for a in range(2):
                        nc.vector.tensor_scalar(gate[:, 0, l, a], v[:, l, a, 2], 0.0, 2.0, ALU.is_ge, ALU.mult)
                        last = nc.vector.scalar_tensor_tensor(out=gate[:, 1, l, a], in0=v[:, l, a, 2], scalar=-1.0,
                                                              in1=v[:, l, a, 2], op0=ALU.mult, op1=ALU.max)
                link(last)
                link(nc.vector.tensor_scalar(gate[:, 1], gate[:, 1], 0.25, None, ALU.max))
                for l in range(2):
                    for a in range(2):
                        nc.vector.tensor_scalar(v[:, l, a, 1], v[:, l, a, 1], 1.0, None, ALU.add)
                        last = nc.vector.scalar_tensor_tensor(out=v[:, l, a, 2], in0=gate[:, 0, l, a], scalar=-1.0,
                                                              in1=gate[:, 1, l, a], op0=ALU.add, op1=ALU.mult)
                link(last)
                nc.vector.tensor_copy(g["ident16"][:], ident[:]).then_inc(s_done, 1)
                link.done()
                dve.wait_ge(s_rt, 1)
                nc.vector.tensor_copy(mod_rows[:], ps_r[:]).then_inc(s_rows, 1)

            @block.tensor
            def _(pe):
                pe.wait_ge(s_id, 2)
                pe.wait_ge(s_silu, 1)
                for l in range(2):
                    for h in range(2):
                        last = nc.tensor.transpose(ps_c[:, l, h, :], c_silu[:, l, h * P:(h + 1) * P], ident[0:B, 0:B])
                last.then_inc(s_ct, 1)
                pe.wait_ge(s_cte, 1)
                pe.wait_ge(s_wm, 32)
                for l in range(2):
                    for m in range(12):
                        for h in range(2):
                            last = nc.tensor.matmul(ps_m[:, l, m, :], wmod[:, l, h, m * P:(m + 1) * P], cT[:, l, h, :],
                                                    start=(h == 0), stop=(h == 1))
                last.then_inc(s_mm, 1)
                pe.wait_ge(s_done, 1)
                for l in range(2):
                    last = nc.tensor.transpose(ps_r[:, l, :], MOD[:, l].rearrange("p v b -> p (v b)"), ident[:])
                last.then_inc(s_rt, 1)


def softcap_attention(nc, sem, g, x, w_q, w_k, w_v, w_o):
    QC = 512
    NQC = T // QC
    UNITS = [(q, c, i) for q in range(4) for c in range(NQC) for i in range((c + 1) * QC // P)]
    NU = len(UNITS)
    NTP = 3
    assert NU % NTP == 0
    N_DIAG = 4 * NT
    EPS = 1.1920929e-07
    SPLIT_SCALE = 2.0 ** 12

    def span(c, i):
        n0 = max(i * P, c * QC)
        return n0, (c + 1) * QC - n0

    EXTRA = {u: [] for u in range(NU)}
    def put(unit, *entries):
        EXTRA[unit] += entries

    put(0, ("heads_out", 7))
    put(1, ("gated_wo", 0), ("gated_wo", 1))
    for n in range(4):
        put(4 + n // 2, ("yT", n))
        put(6 + n, ("project_out", n))
        put((12, 13, 16, 16)[n], ("qkT_half1", 2 * n), ("qkT_half1", 2 * n + 1))
        put(17 + n // 2, ("hT", n))
    for n, u in {0: 19, 1: 20, 3: 21, 4: 24, 2: 25, 5: 29, 6: 30, 7: 31, 9: 32, 10: 33, 8: 37, 11: 40}.items():
        put(u, ("qkv", n))
    for n in range(4):
        put(41 + n, ("qkT_half0", 2 * n), ("qkT_half0", 2 * n + 1))
    for m, u in enumerate((9, 14, 18, 29, 33, 38, 42)):
        put(u, ("heads_out", m))
    LN_AT = 1
    ORDER = [e for u in range(NU) for e in EXTRA[u]]

    def of_before(e):
        return e[0] in ("gated_wo", "yT", "project_out") or e == ("heads_out", 7)

    def of_next(e):
        return e[0] in ("hT", "qkv", "qkT_half0")

    BEFORES, NEXTS = list(filter(of_before, ORDER)), list(filter(of_next, ORDER))
    IN_LAST = [e for e in ORDER if not of_next(e)]
    assert ORDER[:len(BEFORES)] == BEFORES and len(ORDER) % 2 == 0

    def uses(stage, n, b):
        e = (stage, n)
        base = len(NEXTS) - len(BEFORES)
        fixed = isinstance(b, int)
        if of_next(e):
            at = NEXTS.index(e) + 1 if fixed and b == 0 else base + len(ORDER) * (b - 1) + ORDER.index(e) + 1
            odd = (NEXTS.index(e) if fixed and b == 0 else base + ORDER.index(e)) % 2
        elif of_before(e):
            cut = len(NEXTS) if fixed and b == B - 1 else 0
            at = base - cut + len(ORDER) * (b + 1) + ORDER.index(e) + 1
            odd = (base - cut + ORDER.index(e)) % 2
        else:
            order = IN_LAST if fixed and b == B - 1 else ORDER
            at = base + len(ORDER) * b + order.index(e) + 1
            odd = (base + order.index(e)) % 2
        return at, odd

    def batch_of(e, b, first, last):
        if of_before(e):
            return None if first else b - 1
        if of_next(e):
            return None if last else b + 1
        return b

    with ExitStack() as st:
        def sb(name, shape):
            return st.enter_context(nc.sbuf_tensor("a_" + name, shape, F32))

        def sb16(name, shape):
            return st.enter_context(nc.sbuf_tensor("a_" + name, shape, F16))

        KT = sb16("KT", [P, NH // 2, T])
        QT = sb16("QT", [P, NH // 2, T])
        QKS = sb16("QKS", [P, 2, NT, NH, 4, DK])
        VA = sb("VA", [P, NT, NH, DK + 1])
        VR = sb("VR", [P, NT, D // 2])
        Z = sb("Z", [P, NT, D])
        HT = sb("HT", [P, 2, T])
        QK = Z[:].rearrange("p (m i) c -> p m i c", m=2)
        TP = sb("TP", [P, NTP, 4, QC])
        OS = sb("OS", [P, 2, QC])
        Y = sb("Y", [P, NT, D])
        YT = HT
        WOG = sb("WOG", [P, 2, D])
        WS = Z[:, 0:2, :]
        WO = sb("WO", [P, 2, D])
        WQKV = sb("WQKV", [P, 2, 3 * D])
        STATS = sb("STATS", [P, NT, 6])
        MV = sb("MV", [P, NT, 2])
        LV, LR, LT = sb("LV", [P, NT]), sb("LR", [P, NT]), sb("LT", [P, NT])
        SS, RS, RT = (sb(n, [P, NT // 2 * 32]) for n in ("SS", "RS", "RT"))
        RC = sb("RC", [P, 2, 4, 4])
        SC = st.enter_context(nc.psum_tensor("SC", [P, 4, QC], F32))
        OB = [st.enter_context(nc.psum_tensor(f"OB{i}", [P, QC], F32)) for i in range(2)]
        AUX = [st.enter_context(nc.psum_tensor(f"AUX{i}", [P, 512], F32)) for i in range(2)]
        X, ident, MOD = g["X"], g["ident"], g["MOD"]
        ident16 = g["ident16"]

        WN = Z[:].rearrange("p (m h) c -> p m h c", h=2)

        def square_of(i):
            return QKS[:, 0, i].rearrange("p h s d -> p (h s d)").bitcast(F32)

        s_w, s_wo_ld, s_x = sem("a_w_loaded"), sem("a_wo_loaded"), sem("a_x_loaded")
        s_ones, s_wt, s_wte = sem("a_ones"), sem("a_w_transposed"), sem("a_wT")
        s_aux, s_auxf = sem("a_ring_filled"), sem("a_ring_emptied")
        s_z, s_sq, s_ssr, s_qkn = sem("a_z"), sem("a_qk_squared"), sem("a_squares_summed"), sem("a_qk_normed")
        s_va1, s_zero = sem("a_v_half1"), sem("a_strips_zero")
        s_sc, s_th, s_ex, s_mk, s_pv = (sem("a_" + n) for n in ("scores", "tanh", "exp", "masked", "pv"))
        s_os, s_ws = sem("a_strips_copied"), sem("a_wo_scaled")
        c_ln, c_norm, c_rc = sem("a_ln_chain"), sem("a_norm_chain"), sem("a_reciprocal_chain")

        with nc.Block() as block:
            @block.sync
            def _(sp):
                for m, w in enumerate((w_q, w_k, w_v)):
                    sp.dma_start(WN[:, m], w.rearrange("(h p) c -> p h c", p=P)).then_inc(s_w, 16)
                sp.dma_start(WO[:], w_o.rearrange("(h p) c -> p h c", p=P)).then_inc(s_wo_ld, 16)
                xv = x.rearrange("b (i p) c -> p (b i) c", p=P)
                sp.dma_start(X[:, 0:NT, :], xv[:, 0:NT, :]).then_inc(s_x, 16)
                with sp.Fori(1, B) as b:
                    sp.wait_ge(s_x, 16 * b)
                    sp.dma_start(X[:, bass.ds(b * NT, NT), :], xv[:, bass.ds(b * NT, NT), :]).then_inc(s_x, 16)

            @block.gpsimd
            def _(pool):
                nc.gpsimd.memset(VA[:, :, :, DK], 1.0).then_inc(s_ones, 1)

                def square(b, i):
                    pool.wait_ge(s_auxf, uses("qkv", 3 * (i // 2) + i % 2, b)[0])
                    nc.gpsimd.tensor_tensor(square_of(i).rearrange("p (m c) -> p m c", m=2), QK[:, :, i % 4],
                                            QK[:, :, i % 4], ALU.mult).then_inc(s_sq, 1)

                def v_copy(b):
                    wait_apart(pool, s_auxf, uses("qkv", 11, b)[0])
                    nc.gpsimd.tensor_copy(VA[:, :, NH // 2:, 0:DK],
                                          VR[:].rearrange("p i (h d) -> p i h d", d=DK)).then_inc(s_va1, 1)

                def units(b, first, last):
                    n_diag = 0
                    for u, (q, c, i) in enumerate(UNITS):
                        if i >= c * QC // P:
                            wait_apart(pool, s_ex, NU * b + u + 1)
                            n_diag += 1
                            t = TP[:, u % NTP, :, 0:P]
                            nc.gpsimd.affine_select(out=t, in_=t, compare_op=ALU.is_ge, fill=0.0, base=0,
                                                    pattern=[[0, 4], [1, P]], channel_multiplier=-1).then_inc(s_mk, 1)
                        for stage, n in EXTRA[u - 1] if u and not last else []:
                            if stage == "qkv" and n % 3 < 2:
                                square(b + 1, 2 * (n // 3) + n % 3)
                        if u == 10:
                            if not first:
                                pool.wait_ge(s_pv, NU * b)
                            v_copy(b)
                    assert n_diag == N_DIAG

                for i in range(NT):
                    square(0, i)
                units(0, True, False)
                with pool.Fori(1, B - 1) as b:
                    units(b, False, False)
                units(B - 1, False, True)

            @block.scalar
            def _(act):
                def tanh(b, u):
                    q, c, i = UNITS[u]
                    _, n = span(c, i)
                    act.wait_ge(s_sc, NU * b + u + 1)
                    if not (isinstance(b, int) and NU * b + u < NTP):
                        act.wait_ge(s_pv, NU * b + u - NTP + 1)
                    nc.scalar.activation(TP[:, u % NTP, :, 0:n], SC[:, :, 0:n], ACT.Tanh,
                                         scale=1.0 / (50.0 * DK ** 0.5 * SPLIT_SCALE ** 2)).then_inc(s_th, 1)

                def exp(b, u):
                    q, c, i = UNITS[u]
                    _, n = span(c, i)
                    act.wait_ge(s_th, NU * b + u + 1)
                    t = TP[:, u % NTP, :, 0:n]
                    nc.scalar.activation(t, t, ACT.Exp, scale=50.0).then_inc(s_ex, 1)

                def units(b, last):
                    for u in range(NU):
                        if u + 1 < NU:
                            tanh(b, u + 1)
                        elif not last:
                            tanh(b + 1, 0)
                        exp(b, u)

                tanh(0, 0)
                units(0, False)
                with act.Fori(1, B - 1) as b:
                    units(b, False)
                units(B - 1, True)

            @block.tensor
            def _(pe):
                pe.wait_ge(s_w, 48)
                for m in range(3):
                    if m >= 2:
                        pe.wait_ge(s_wte, m - 1)
                    for h in range(2):
                        for o in range(2):
                            last = nc.tensor.transpose(AUX[m % 2][:, h * D + o * P:h * D + o * P + P],
                                                       WN[:, m, o, h * P:h * P + P], ident[:])
                    last.then_inc(s_wt, 1)
                pe.wait_ge(s_wte, 3)

                def tiles_T(aux, src, g4, col):
                    for t in range(4):
                        last = nc.tensor.transpose(aux[:, t * P:(t + 1) * P], src[:, 4 * g4 + t, col:col + P], ident[:])
                    return last

                def extra(stage, n, b):
                    at, odd = uses(stage, n, b)
                    if not (isinstance(at, int) and at <= 2):
                        pe.wait_ge(s_auxf, at - 2)
                    aux = AUX[odd]
                    if stage == "hT":
                        pe.wait_ge(s_z, NT * b + 4 * (n // 2) + 4)
                        last = tiles_T(aux, Z, n // 2, P * (n % 2))
                    elif stage == "qkv":
                        p, what = n // 3, n % 3
                        if n == 0:
                            pe.wait_ge(s_auxf, uses("hT", 3, b)[0])
                        if what < 2:
                            i = 2 * p + what
                            for h in range(2):
                                last = nc.tensor.matmul(aux[:, :], HT[:, h, i * P:(i + 1) * P], WQKV[:, h, 0:2 * D],
                                                        start=(h == 0), stop=(h == 1))
                        else:
                            for i in range(2):
                                for h in range(2):
                                    last = nc.tensor.matmul(aux[:, i * D:(i + 1) * D],
                                                            HT[:, h, (2 * p + i) * P:(2 * p + i + 1) * P],
                                                            WQKV[:, h, 2 * D:3 * D], start=(h == 0), stop=(h == 1))
                    elif stage in ("qkT_half0", "qkT_half1"):
                        pe.wait_ge(s_qkn, 2 * b + 2)
                        aux16 = aux[:, :].bitcast(F16)
                        pair, kind = 4 * int(stage[-1]) + n // 2, 1 - n % 2
                        for i in range(NT):
                            src = QKS[:, kind, i, 2 * pair:2 * pair + 2].rearrange("p h s d -> p (h s d)")
                            last = nc.tensor.transpose(aux16[:, i * P:(i + 1) * P], src, ident16[:])
                    elif stage == "heads_out":
                        pe.wait_ge(s_os, 8 * b + n + 1)
                        for t in range(4):
                            last = nc.tensor.transpose(aux[:, t * P:(t + 1) * P], OS[:, n % 2, t * P:(t + 1) * P], ident[:])
                    elif stage == "gated_wo":
                        pe.wait_ge(s_ws, b + 1)
                        for h in range(2):
                            last = nc.tensor.transpose(aux[:, h * P:(h + 1) * P], WS[:, h, n * P:(n + 1) * P], ident[:])
                    elif stage == "yT":
                        pe.wait_ge(s_auxf, uses("heads_out", 7, b)[0])
                        last = tiles_T(aux, Y, n // 2, P * (n % 2))
                    elif stage == "project_out":
                        pe.wait_ge(s_auxf, uses("yT", 3, b)[0])
                        for t in range(2):
                            for h in range(2):
                                last = nc.tensor.matmul(aux[:, t * D:(t + 1) * D],
                                                        YT[:, h, (2 * n + t) * P:(2 * n + t + 1) * P], WOG[:, h, :],
                                                        start=(h == 0), stop=(h == 1))
                    last.then_inc(s_aux, 1)

                def scores(b, u):
                    q, c, i = UNITS[u]
                    n0, n = span(c, i)
                    if u == 0:
                        pe.wait_ge(s_auxf, uses("qkT_half0", 7, b)[0])
                    if u == NU // 2:
                        pe.wait_ge(s_auxf, uses("qkT_half1", 7, b)[0])
                    if not (isinstance(b, int) and NU * b + u == 0):
                        pe.wait_ge(s_th, NU * b + u)
                    for j in range(4):
                        pair, rows = 2 * q + j // 2, slice(64 * (j % 2), 64 * (j % 2) + 64)
                        last = nc.tensor.matmul(SC[:, j, 0:n], KT[rows, pair, i * P:(i + 1) * P],
                                                QT[rows, pair, n0:n0 + n], start=True, stop=True)
                    last.then_inc(s_sc, 1)

                def values(b, u, n_diag):
                    q, c, i = UNITS[u]
                    n0, n = span(c, i)
                    m = NQC * q + c
                    if u == 0:
                        pe.wait_ge(s_auxf, uses("qkv", 11, b)[0])
                        pe.wait_ge(s_ones, 1)
                        pe.wait_ge(s_zero, 1)
                    if u == NU // 2:
                        pe.wait_ge(s_va1, b + 1)
                    if i == 0 and not (isinstance(b, int) and 8 * b + m < 2):
                        pe.wait_ge(s_os, 8 * b + m - 1)

                    def columns(lo, hi):
                        for j in range(4):
                            at = n0 - c * QC
                            last = nc.tensor.matmul(OB[m % 2][32 * j:32 * j + DK + 1, at + lo:at + hi],
                                                    VA[:, i, 4 * q + j, :], TP[:, u % NTP, j, lo:hi],
                                                    start=(i == 0), stop=(i == (c + 1) * QC // P - 1))
                        return last

                    pe.wait_ge(s_ex, NU * b + u + 1)
                    masked = n
                    if i >= c * QC // P:
                        if i > 0 and n > P:
                            columns(P, n)
                            masked = P
                        n_diag += 1
                        pe.wait_ge(s_mk, N_DIAG * b + n_diag)
                    columns(0, masked).then_inc(s_pv, 1)
                    return n_diag

                def units(b, first, last):
                    n_diag = 0
                    for u in range(NU):
                        if u + 2 < NU:
                            scores(b, u + 2)
                        elif not last:
                            scores(b + 1, u + 2 - NU)
                        for e in EXTRA[u]:
                            bb = batch_of(e, b, first, last)
                            if bb is not None:
                                extra(*e, bb)
                        n_diag = values(b, u, n_diag)

                for e in NEXTS:
                    extra(*e, 0)
                scores(0, 0)
                scores(0, 1)
                units(0, True, False)
                with pe.Fori(1, B - 1) as b:
                    units(b, False, False)
                units(B - 1, False, True)
                for e in BEFORES:
                    extra(*e, B - 1)

            @block.vector
            def _(dve):
                for m in range(3):
                    dve.wait_ge(s_wt, m + 1)
                    nc.vector.tensor_copy(WQKV[:, :, m * D:(m + 1) * D],
                                          AUX[m % 2][:, :].rearrange("p (h o) -> p h o", h=2)).then_inc(s_wte, 1)
                dve.wait_ge(s_wo_ld, 16)
                nc.vector.memset(OB[0][:, :], 0.0)
                nc.vector.memset(OB[1][:, :], 0.0).then_inc(s_zero, 1)

                def layer_norm(b):
                    link = Linker(dve, c_ln, b, 3 + RSQRT_LINKS)
                    dve.wait_ge(s_x, 16 * b + 16)
                    for i in range(NT):
                        last = nc.vector.bn_stats(STATS[:, i, :], X[:, b * NT + i, :])
                    last.then_inc(c_ln, 1)
                    link.k += 1
                    wait_apart(dve, c_ln, link.before + link.k)
                    for i in range(NT):
                        last = nc.vector.bn_aggr(MV[:, i, :], STATS[:, i, :])
                    link(last)
                    link(nc.vector.tensor_scalar(LV[:], MV[:, :, 1], 1e-5, None, ALU.add))
                    rsqrt(dve, nc, link, LV[:], LR[:], LT[:])
                    link.done()
                    if not (isinstance(b, int) and b == 0):
                        dve.wait_ge(s_qkn, 2 * b)
                    for i in range(NT):
                        nc.vector.tensor_scalar(Z[:, i, :], X[:, b * NT + i, :], MV[:, i, 0:1], LR[:, i:i + 1],
                                                ALU.subtract, ALU.mult).then_inc(s_z, 1)

                def sum_squares(b, i):
                    dve.wait_ge(s_sq, NT * b + i + 1)
                    nc.vector.tensor_reduce(SS[:].rearrange("p (m i h) -> p m i h", m=2, i=4)[:, :, i % 4],
                                            square_of(i).rearrange("p (m h d) -> p m h d", m=2, d=DK), AX.X,
                                            ALU.add).then_inc(s_ssr, 1)

                def norm_qk(b, g4):
                    sum_squares(b, 4 * g4 + 3)
                    link = Linker(dve, c_norm, 2 * b + g4, 3 + RSQRT_LINKS)
                    dve.wait_ge(s_ssr, NT * b + 4 * g4 + 4)
                    link(nc.vector.tensor_scalar(SS[:], SS[:], 1.0 / DK / SPLIT_SCALE ** 2, EPS / SPLIT_SCALE ** 2,
                                                 ALU.mult, ALU.add))
                    rsqrt(dve, nc, link, SS[:], RS[:], RT[:])
                    qv = QK[:].rearrange("p m i (h d) -> p (m i h) d", d=DK)
                    link(nc.vector.tensor_tensor(qv, qv, bcast(RS[:], DK), ALU.mult))

                    def both(ap):
                        return ap.unsqueeze(2).to_broadcast([P, 4 * NH, 2, DK])

                    tiles = slice(4 * g4, 4 * g4 + 4)
                    q, k = (QK[:, m].rearrange("p i (h d) -> p (i h) d", d=DK) for m in range(2))
                    qs, ks = (QKS[:, m, tiles].rearrange("p i h s d -> p (i h) s d") for m in range(2))
                    nc.vector.tensor_copy(qs[:, :, 0:2], both(q))
                    link(nc.vector.tensor_copy(ks[:, :, 0::2], both(k)))
                    nc.vector.tensor_tensor(qs[:, :, 2:4], both(q), qs[:, :, 0:2], ALU.subtract)
                    nc.vector.tensor_tensor(ks[:, :, 1::2], both(k), ks[:, :, 0::2], ALU.subtract).then_inc(s_qkn, 1)
                    link.done()

                def scale_wo(b):
                    dve.wait_ge(s_qkn, 2 * B if isinstance(b, int) and b == B - 1 else 2 * b + 4)
                    for h in range(2):
                        last = nc.vector.tensor_scalar(WS[:, h, :], WO[:, h, :], MOD[:, 0, 2 * GA + h, bass.ds(b, 1)],
                                                       None, ALU.mult)
                    last.then_inc(s_ws, 1)

                def extra(stage, n, b):
                    zero = isinstance(b, int) and b == 0
                    at, odd = uses(stage, n, b)
                    aux = AUX[odd]
                    dve.wait_ge(s_aux, at)
                    if stage == "hT":
                        h, g4 = n % 2, n // 2
                        last = nc.vector.tensor_scalar(HT[:, h, g4 * 512:(g4 + 1) * 512], aux[:, :],
                                                       MOD[:, 0, 2 * CA + h, bass.ds(b, 1)],
                                                       MOD[:, 0, 2 * SA + h, bass.ds(b, 1)], ALU.mult, ALU.add)
                    elif stage == "qkv" and n % 3 < 2:
                        if n == 6:
                            dve.wait_ge(s_qkn, 2 * b + 1)
                        last = nc.vector.tensor_copy(QK[:, :, (2 * (n // 3) + n % 3) % 4],
                                                     aux[:, :].rearrange("p (m c) -> p m c", m=2))
                    elif stage == "qkv":
                        if not zero:
                            dve.wait_ge(s_va1, b)
                        if not zero and n == 2:
                            dve.wait_ge(s_pv, NU * (b - 1) + NU // 2)
                        tiles, v = slice(2 * (n // 3), 2 * (n // 3) + 2), aux[:, :].rearrange("p (i c) -> p i c", i=2)
                        nc.vector.tensor_copy(VA[:, tiles, 0:NH // 2, 0:DK],
                                              v[:, :, 0:P].rearrange("p i (h d) -> p i h d", d=DK))
                        last = nc.vector.tensor_copy(VR[:, tiles, :], v[:, :, P:])
                    elif stage in ("qkT_half0", "qkT_half1"):
                        half = int(stage[-1])
                        if n == 0 and not zero:
                            dve.wait_ge(s_sc, NU * (b - 1) + (NU if half else NU // 2))
                        last = nc.vector.tensor_copy((QT if n % 2 else KT)[:, 4 * half + n // 2, :], aux[:, :].bitcast(F16))
                    elif stage == "heads_out":
                        link = Linker(dve, c_rc, 8 * b + n, 1)
                        av = aux[:, :].rearrange("p (t j e) -> p t j e", t=4, j=4)
                        link(nc.vector.reciprocal(RC[:, n % 2], av[:, :, :, DK]))
                        yv = Y[:].rearrange("p i (q j d) -> p i q j d", q=4, d=DK)
                        last = nc.vector.tensor_tensor(yv[:, 4 * (n % 2):4 * (n % 2) + 4, n // 2], av[:, :, :, 0:DK],
                                                       bcast(RC[:, n % 2], DK), ALU.mult)
                    elif stage == "gated_wo":
                        last = nc.vector.tensor_copy(WOG[:, n, :], aux[:, 0:D])
                    elif stage == "yT":
                        last = nc.vector.tensor_copy(YT[:, n % 2, n // 2 * 512:n // 2 * 512 + 512], aux[:, :])
                    elif stage == "project_out":
                        xt = X[:, bass.ds(b * NT + 2 * n, 2), :]
                        last = nc.vector.tensor_tensor(xt, aux[:, :].rearrange("p (t c) -> p t c", t=2), xt, ALU.add)
                    last.then_inc(s_auxf, 1)
                    if stage == "qkv" and n % 3 < 2 and n % 6:
                        sum_squares(b, 2 * (n // 3) + n % 3 - 1)
                    if stage == "qkv" and n % 6 == 4:
                        norm_qk(b, n // 6)

                def units(b, first, last):
                    for u, (q, c, i) in enumerate(UNITS):
                        if i == (c + 1) * QC // P - 1:
                            m = NQC * q + c
                            dve.wait_ge(s_pv, NU * b + u + 1)
                            nc.vector.tensor_copy(OS[:, m % 2, :], OB[m % 2][:, :]).then_inc(s_os, 1)
                        for e in EXTRA[u]:
                            bb = batch_of(e, b, first, last)
                            if bb is not None:
                                extra(*e, bb)
                        if u == 0 and not first:
                            scale_wo(b - 1)
                        if u == LN_AT and not last:
                            layer_norm(b + 1)

                layer_norm(0)
                for e in NEXTS:
                    extra(*e, 0)
                units(0, True, False)
                with dve.Fori(1, B - 1) as b:
                    units(b, False, False)
                units(B - 1, False, True)
                scale_wo(B - 1)
                for e in BEFORES:
                    extra(*e, B - 1)


def staggered(eng, front, back, early=()):
    order = sorted([(at, 0, step) for at, step in early] + [(at, 1, step) for at, step in front] +
                   [(at, 2, step) for at, step in back], key=lambda e: e[:2])

    def beside(slot, b, first=False, last=False):
        for _, which, step in order:
            if which == 0 and not last:
                step(1 - slot, b + 1)
            elif which == 1:
                step(slot, b)
            elif which == 2 and not first:
                step(1 - slot, b - 1)

    for _, step in early:
        step(0, 0)
    beside(0, 0, first=True)
    with eng.Fori(0, B // 2 - 1) as j:
        beside(1, 2 * j + 1)
        beside(0, 2 * j + 2)
    beside(1, B - 1, last=True)
    for _, step in back:
        step(1, B - 1)


def transpose_weights(nc, sem, g, name, jobs, loads, zeroed=()):
    def place(n):
        return ring[n % 4][0:jobs[n][0].shape[1], 0:jobs[n][0].shape[0]]

    with ExitStack() as st:
        ring = [st.enter_context(nc.psum_tensor(f"{name}_ring{i}", [P, P], F32)) for i in range(4)]
        s_ld = sem(name + "_loaded")
        if zeroed:
            s_zero = sem(name + "_zeroed")
        s_t = sem(name + "_transposed")
        s_out = [sem(name + "_out_vector"), sem(name + "_out_scalar")]
        with nc.Block() as block:
            @block.sync
            def _(sp):
                for d, s in loads:
                    sp.dma_start(d, s, allow_slow_non_contiguous=(len(s.shape) == 2 and s.shape[1] == 2)).then_inc(s_ld, 16)

            @block.gpsimd
            def _(pool):
                for z in zeroed:
                    nc.gpsimd.memset(z, 0.0).then_inc(s_zero, 1)

            @block.tensor
            def _(pe):
                pe.wait_ge(s_ld, 16 * len(loads))
                for n, (src, dst, scale) in enumerate(jobs):
                    if n >= 4:
                        pe.wait_ge(s_out[n % 2], (n - 4) // 2 + 1)
                    nc.tensor.transpose(place(n), src, g["ident"][0:src.shape[0], 0:src.shape[0]]).then_inc(s_t, 1)

            @block.vector
            def _(dve):
                dve.wait_ge(s_ld, 16 * len(loads))
                if zeroed:
                    dve.wait_ge(s_zero, len(zeroed))
                for n, (src, dst, scale) in enumerate(jobs):
                    if n % 2 == 0:
                        dve.wait_ge(s_t, n + 1)
                        nc.vector.tensor_scalar(dst, _like(place(n), dst), scale, None,
                                                ALU.mult).then_inc(s_out[0], 1)

            @block.scalar
            def _(act):
                act.wait_ge(s_ld, 16 * len(loads))
                if zeroed:
                    act.wait_ge(s_zero, len(zeroed))
                for n, (src, dst, scale) in enumerate(jobs):
                    if n % 2:
                        act.wait_ge(s_t, n + 1)
                        nc.scalar.activation(dst, _like(place(n), dst), ACT.Copy if isinstance(scale, float)
                                             else ACT.Identity, scale=scale).then_inc(s_out[1], 1)


def _like(src, dst):
    if len(dst.shape) == 2:
        return src
    if len(dst.shape) == 3:
        return src.rearrange("p (a b) -> p a b", a=dst.shape[1])
    return src.rearrange("p (a b c) -> p a b c", a=dst.shape[1], b=dst.shape[2])


def routed_block(nc, sem, g, w):
    NF = -(-DFF // P)
    G4 = NH // 4
    with ExitStack() as st:
        def sb(name, shape, dtype=F32):
            return st.enter_context(nc.sbuf_tensor("r_" + name, shape, dtype))

        WQK = sb("WQK", [P, 2, 2, G4, 4, 2 * DK])
        WV = sb("WV", [P, 2, D])
        WOUT = sb("WOUT", [P, 2, D])
        W1 = sb("W1", [P, 2, NF * P])
        W2 = sb("W2", [P, 2, NF * P])
        W3 = sb("W3", [P, NF, D])
        WR = sb("WR", [P, D])
        with ExitStack() as tmp:
            def tb(name, shape):
                return tmp.enter_context(nc.sbuf_tensor("r_" + name, shape, F32))
            G = tb("G", [P, 2, 2])
            NQ, N1, N2 = tb("NQ", [P, 6, D]), tb("N1", [P, NF, D]), tb("N2", [P, NF, D])
            N3, NO = tb("N3", [P, 2, DFF]), tb("NO", [P, 2, D])
            full, rest = DFF // P, DFF % P
            loads = [(G[:, m, :], w["g%d" % (m + 1)].rearrange("(h p) -> p h", p=P)) for m in range(2)]
            loads += [(NQ[:], w["W_qkv"].rearrange("(m p) c -> p m c", p=P)),
                      (NO[:], w["W_out"].rearrange("(m p) c -> p m c", p=P)),
                      (N3[:], w["W3"].rearrange("(m p) c -> p m c", p=P)),
                      (WR[:], w["w_router"].unsqueeze(0).to_broadcast([P, D]))]
            for n, t in ((N1, "W1"), (N2, "W2")):
                loads += [(n[:, 0:full, :], w[t][0:full * P].rearrange("(m p) c -> p m c", p=P)),
                          (n[0:rest, full, :], w[t][full * P:DFF])]
            jobs = []
            for h in range(2):
                cols = slice(h * P, (h + 1) * P)
                for m in range(4):
                    dst = WQK[:, h, m // 2, 2 * (m % 2):2 * (m % 2) + 2, :, 0:DK]
                    jobs.append((NQ[:, m, cols], dst, G[:, 0, h:h + 1]))
                for m in range(2):
                    jobs.append((NQ[:, 4 + m, cols], WV[:, h, m * P:(m + 1) * P], G[:, 0, h:h + 1]))
                    jobs.append((NO[:, m, cols], WOUT[:, h, m * P:(m + 1) * P], 1.0))
                for m in range(NF):
                    rows = min(P, DFF - m * P)
                    for n, d in ((N1, W1), (N2, W2)):
                        jobs.append((n[0:rows, m, cols], d[:, h, m * P:m * P + rows], G[:, 1, h:h + 1]))
            for m in range(NF):
                rows = min(P, DFF - m * P)
                for c in range(2):
                    jobs.append((N3[:, c, m * P:m * P + rows], W3[0:rows, m, c * P:(c + 1) * P], 0.5))
            transpose_weights(nc, sem, g, "r_weights", jobs, loads, zeroed=(WQK[:], W1[:], W2[:], W3[:, full, :]))

        LOW = sb("LOW", [P, P])
        RANKS = sb("RANKS", [P, P])
        ONES = sb("ONES", [P, P])
        NEG = sb("NEG", [P, 4, P], BF16)
        identb = sb("identb", [P, P], BF16)
        ROWS = [sb(f"ROWS{s}", [P, 3, D]) for s in range(2)]
        H = [sb(f"H{s}", [P, NT, D]) for s in range(2)]
        JUNK = [sb(f"JUNK{s}", [P, 2, 9 * P], BF16) for s in range(2)]
        ST, MV = [sb(f"ST{s}", [P, NT, 6]) for s in range(2)], [sb(f"MV{s}", [P, NT, 2]) for s in range(2)]
        RL = [sb(f"RL{s}", [P, 4, NT]) for s in range(2)]
        SCR = [sb(f"SCR{s}", [P, NT]) for s in range(2)]
        CNT = [sb(f"CNT{s}", [P, NT, 5]) for s in range(2)]
        RANK = [sb(f"RANK{s}", [P, NT]) for s in range(2)]
        DG = [sb(f"DG{s}", [P, NT, P]) for s in range(2)]
        PM = [DG[s] for s in range(2)]
        PT = [sb(f"PT{s}", [P, NT, P]) for s in range(2)]
        SEL = [sb(f"SEL{s}", [P, D]) for s in range(2)]
        XA = [sb(f"XA{s}", [P, D]) for s in range(2)]
        U = [sb(f"U{s}", [P, D]) for s in range(2)]
        UT = [sb(f"UT{s}", [P, 2, P]) for s in range(2)]
        OT = [sb(f"OT{s}", [P, 2, P]) for s in range(2)]
        QKT = [sb(f"QKT{s}", [P, 2, G4, P]) for s in range(2)]
        V = [sb(f"V{s}", [P, NH, DK + 1]) for s in range(2)]
        EX = [sb(f"EX{s}", [P, NH, P]) for s in range(2)]
        ET = [sb(f"ET{s}", [P, NH, P]) for s in range(2)]
        TH = [EX[s][:].rearrange("p h k -> p (h k)")[:, 0:NF * P] for s in range(2)]
        GH = [ET[s][:].rearrange("p h k -> p (h k)")[:, 0:NF * P] for s in range(2)]
        MX = [sb(f"MX{s}", [P, 2, NH]) for s in range(2)]
        SM = [sb(f"SM{s}", [P, 2, 4]) for s in range(2)]
        BK = [[st.enter_context(nc.psum_tensor(f"r_BK{s}{n}", [P, 512], F32)) for n in range(4)] for s in range(2)]
        X, ident = g["X"], g["ident"]
        names = ["filled", "constants", "rows0", "rows1", "free", "mean", "z", "router", "diagonals", "counted", "score_rows", "one_hot", "gathered",
                 "pt", "sum1", "u1", "u1T", "u1T_out", "qkv", "qkT_out", "v_out", "scores", "max", "exp",
                 "expT", "expT_out_a", "expT_out_v", "heads", "heads_out", "headsT", "headsT_out", "attended", "xa",
                 "sum2", "u2", "u2T", "u2T_out", "hidden", "tanh", "gated", "processed", "delta", "scattered",
                 "gated_h", "x_h"]
        s = {n: sem("r_" + n) for n in names}
        c_ln, c_h, c_rank, c_u1, c_max, c_heads, c_u2, c_gate = (sem("r_chain_" + n) for n in
            ("ln", "h", "rank", "u1", "max", "heads", "u2", "gate"))
        rows_dram = g["mod_dram"]

        with nc.Block() as block:
            @block.sync
            def _(sp):
                with sp.Fori(0, B // 2) as j:
                    for n in range(2):
                        sp.wait_ge(s["free"], 2 * j + n + 1)
                        sp.dma_start(ROWS[n][:].rearrange("p v (h c) -> p (v h) c", h=2),
                                     rows_dram[0, 2 * SB:2 * GB + 2, bass.ds(2 * j + n, 1), :].rearrange(
                                         "v b c -> b v c").to_broadcast([P, 6, P])).then_inc(s["rows%d" % n], 16)

            @block.gpsimd
            def _(pool):
                c = s["constants"]
                nc.gpsimd.memset(LOW[:], 1.0).then_inc(s["filled"], 1)
                nc.gpsimd.memset(NEG[:], 0.0).then_inc(s["filled"], 1)
                pool.wait_ge(s["filled"], 2)
                nc.gpsimd.affine_select(out=LOW[:], in_=LOW[:], compare_op=ALU.is_gt, fill=0.0, base=0,
                                        pattern=[[-1, P]], channel_multiplier=1).then_inc(c, 1)
                nc.gpsimd.affine_select(out=NEG[:], in_=NEG[:], compare_op=ALU.is_ge, fill=-1e30, base=0,
                                        pattern=[[0, 4], [-1, P]], channel_multiplier=1).then_inc(c, 1)
                nc.gpsimd.iota(RANKS[:], pattern=[[1, P]], base=0, channel_multiplier=0,
                               allow_small_or_imprecise_dtypes=True).then_inc(c, 1)
                nc.gpsimd.memset(ONES[:], 1.0).then_inc(c, 1)
                for n in range(2):
                    nc.gpsimd.memset(V[n][:, :, DK], 1.0).then_inc(c, 1)

                def gated_h(n, b):
                    wait_apart(pool, s["gathered"], b + 1)
                    wait_apart(pool, s["rows%d" % n], 8 * (b - n) + 16)
                    nc.gpsimd.tensor_tensor(H[n][:], H[n][:], ROWS[n][:, 2, :].unsqueeze(1).to_broadcast([P, NT, D]),
                                            ALU.mult).then_inc(s["gated_h"], 1)

                def x_plus_h(n, b):
                    wait_apart(pool, s["gated_h"], b + 1)
                    xb = X[:, bass.ds(b * NT, NT), :]
                    nc.gpsimd.tensor_tensor(xb, xb, H[n][:], ALU.add).then_inc(s["x_h"], 1)

                staggered(pool, [(.7, gated_h), (.8, x_plus_h)], [])

            @block.tensor
            def _(pe):
                pe.wait_ge(s["constants"], 7)

                def score_rows(n, b):
                    pe.wait_ge(s["diagonals"], b + 1)
                    for c in range(2):
                        last = nc.tensor.matmul(BK[n][c][:, :], ONES[:], DG[n][:, 4 * c:4 * c + 4, :], start=True,
                                                stop=True)
                    last.then_inc(s["score_rows"], 1)

                def gather(n, b):
                    pe.wait_ge(s["one_hot"], b + 1)
                    for i in range(NT):
                        nc.tensor.matmul(BK[n][2][:, 0:D], PM[n][:, i, :], H[n][:, i, :], start=(i == 0),
                                         stop=(i == NT - 1))
                    for i in range(NT):
                        last = nc.tensor.transpose(BK[n][i // 4][:, (i % 4) * P:(i % 4 + 1) * P], PM[n][:, i, :],
                                                   ident[:])
                    last.then_inc(s["gathered"], 1)

                def transpose2(src, name, ready, bank, off):
                    def step(n, b):
                        wait_apart(pe, s[ready], b + 1)
                        for h in range(2):
                            last = nc.tensor.transpose(BK[n][bank][:, off + h * P:off + (h + 1) * P],
                                                       src[n][:, h * P:(h + 1) * P], ident[:])
                        last.then_inc(s[name], 1)
                    return step

                def qkv(n, b):
                    pe.wait_ge(s["u1T_out"], b + 1)
                    pe.wait_ge(s["pt"], b + 1)
                    for m in range(2):
                        for gr in range(G4):
                            for h in range(2):
                                nc.tensor.matmul(BK[n][m][:, gr * P:(gr + 1) * P],
                                                 WQK[:, h, m, gr].rearrange("p j d -> p (j d)"),
                                                 UT[n][:, h, :], start=(h == 0), stop=(h == 1))
                    for h in range(2):
                        last = nc.tensor.matmul(BK[n][2][:, D:2 * D], UT[n][:, h, :], WV[:, h, :], start=(h == 0),
                                                stop=(h == 1))
                    last.then_inc(s["qkv"], 1)

                def scores(n, b):
                    wait_apart(pe, s["qkT_out"], b + 1)
                    wait_apart(pe, s["v_out"], b + 1)
                    for r in range(4):
                        nc.tensor.matmul(BK[n][r][:, :], identb[:], NEG[:], start=True, stop=False)
                        rows = slice(32 * r, 32 * r + 32)
                        for gr in range(G4):
                            last = nc.tensor.matmul(BK[n][r][:, gr * P:(gr + 1) * P], QKT[n][rows, 0, gr, :],
                                                    QKT[n][rows, 1, gr, :], start=False, stop=(gr == G4 - 1))
                        last.then_inc(s["scores"], 1)

                def exp_transposed(n, b):
                    for r in range(4):
                        pe.wait_ge(s["exp"], 4 * b + r + 1)
                        for gr in range(G4):
                            last = nc.tensor.transpose(BK[n][r][:, gr * P:(gr + 1) * P], EX[n][:, 4 * gr + r, :], ident[:])
                        last.then_inc(s["expT"], 1)

                def heads(n, b):
                    pe.wait_ge(s["expT_out_a"], b + 1)
                    pe.wait_ge(s["expT_out_v"], b + 1)
                    for h in range(NH):
                        last = nc.tensor.matmul(BK[n][0][:, h * (DK + 1):(h + 1) * (DK + 1)], ET[n][:, h, :],
                                                V[n][:, h, :], start=True, stop=True)
                    last.then_inc(s["heads"], 1)

                def attended(n, b):
                    pe.wait_ge(s["headsT_out"], b + 1)
                    for h in range(2):
                        last = nc.tensor.matmul(BK[n][2][:, 0:D], OT[n][:, h, :], WOUT[:, h, :], start=(h == 0),
                                                stop=(h == 1))
                    last.then_inc(s["attended"], 1)

                def hidden(n, b):
                    pe.wait_ge(s["u2T_out"], b + 1)
                    for m in range(NF):
                        for k, wk in enumerate((W1, W2)):
                            for h in range(2):
                                bank, off = (3 * k, m * P) if m < 4 else (1, k * 2 * P + (m - 4) * P)
                                last = nc.tensor.matmul(BK[n][bank][:, off:off + P], wk[:, h, m * P:(m + 1) * P],
                                                        UT[n][:, h, :], start=(h == 0), stop=(h == 1))
                    last.then_inc(s["hidden"], 1)

                def processed(n, b):
                    pe.wait_ge(s["gated"], b + 1)
                    for h in range(2):
                        nc.tensor.matmul(BK[n][2][:, 0:D], OT[n][:, h, :], WOUT[:, h, :], start=(h == 0), stop=False)
                    for m in range(NF):
                        last = nc.tensor.matmul(BK[n][2][:, 0:D], GH[n][:, m * P:(m + 1) * P], W3[:, m, :], start=False,
                                                stop=(m == NF - 1))
                    last.then_inc(s["processed"], 1)

                def scattered(n, b):
                    pe.wait_ge(s["delta"], b + 1)
                    for i in range(NT):
                        o = BK[n][i // 2][:, (i % 2) * D:(i % 2 + 1) * D]
                        last = nc.tensor.matmul(o, PT[n][:, i, :], U[n][:], start=True, stop=True)
                    last.then_inc(s["scattered"], 1)

                staggered(pe, [(.27, score_rows), (.62, gather), (.69, transpose2(U, "u1T", "u1", 3, 0)), (.74, qkv)],
                          [(.03, scores), (.2, exp_transposed),
                           (.26, heads), (.38, transpose2(U, "headsT", "heads_out", 1, 0)), (.43, attended),
                           (.54, transpose2(U, "u2T", "u2", 1, D)), (.6, hidden), (.65, processed), (.71, scattered)])

            @block.scalar
            def _(act):
                act.wait_ge(s["constants"], 7)

                def z(n, b):
                    act.wait_ge(s["free"], b + 1)
                    act.wait_ge(s["mean"], b + 1)
                    for i in range(NT):
                        last = nc.scalar.activation(H[n][:, i, :], X[:, b * NT + i, :], ACT.Identity,
                                                    bias=RL[n][:, 3, i:i + 1], scale=RL[n][:, 1, i:i + 1])
                    last.then_inc(s["z"], 1)

                def selected(n, b):
                    act.wait_ge(s["gathered"], b + 1)
                    nc.scalar.activation(SEL[n][:], BK[n][2][:, 0:D], ACT.Copy)
                    nc.scalar.activation(JUNK[n][:, 0, 0:D], BK[n][2][:, 0:D], ACT.Square,
                                         accum_out=SM[n][:, 0, 0:1]).then_inc(s["sum1"], 1)
                    for c in range(2):
                        last = nc.scalar.activation(PT[n][:, 4 * c:4 * c + 4, :],
                                                    BK[n][c][:, :].rearrange("p (a b) -> p a b", a=4), ACT.Copy)
                    last.then_inc(s["pt"], 1)

                def copy_ut(ready, name, bank, off, to=UT):
                    def step(n, b):
                        act.wait_ge(s[ready], b + 1)
                        nc.scalar.activation(to[n][:], BK[n][bank][:, off:off + D].rearrange("p (h t) -> p h t", h=2),
                                             ACT.Copy).then_inc(s[name], 1)
                    return step

                def qk_out(n, b):
                    act.wait_ge(s["qkv"], b + 1)
                    for m in range(2):
                        last = nc.scalar.activation(QKT[n][:, m], BK[n][m][:, :].rearrange("p (a b) -> p a b", a=4), ACT.Copy)
                    last.then_inc(s["qkT_out"], 1)

                def exp(n, b):
                    for r in range(4):
                        act.wait_ge(s["max"], 4 * b + r + 1)
                        for gr in range(G4):
                            h = 4 * gr + r
                            last = nc.scalar.activation(EX[n][:, h, :], BK[n][r][:, gr * P:(gr + 1) * P], ACT.Exp,
                                                        bias=MX[n][:, 1, h:h + 1], scale=DK ** -0.5)
                        last.then_inc(s["exp"], 1)

                def exp_t_out(n, b):
                    for c in range(2):
                        act.wait_ge(s["expT"], 4 * b + c + 1)
                        last = nc.scalar.activation(ET[n][:, c::4, :],
                                                    BK[n][c][:, :].rearrange("p (a b) -> p a b", a=4), ACT.Copy)
                    last.then_inc(s["expT_out_a"], 1)

                def square2(n, b):
                    act.wait_ge(s["xa"], b + 1)
                    nc.scalar.activation(JUNK[n][:, 1, 0:D], XA[n][:], ACT.Square,
                                         accum_out=SM[n][:, 1, 0:1]).then_inc(s["sum2"], 1)

                def tanh(n, b):
                    act.wait_ge(s["hidden"], b + 1)
                    nc.scalar.activation(TH[n][:, 0:4 * P], BK[n][0][:, :], ACT.Tanh, scale=0.5)
                    nc.scalar.activation(TH[n][:, 4 * P:], BK[n][1][:, 0:(NF - 4) * P], ACT.Tanh,
                                         scale=0.5).then_inc(s["tanh"], 1)

                staggered(act, [(.06, z), (.66, selected), (.7, copy_ut("u1T", "u1T_out", 3, 0)), (.78, qk_out)],
                          [(.12, exp), (.22, exp_t_out), (.4, copy_ut("headsT", "headsT_out", 1, 0, OT)), (.48, square2),
                           (.56, copy_ut("u2T", "u2T_out", 1, D)), (.61, tanh)])

            @block.vector
            def _(dve):
                nc.vector.tensor_copy(identb[:], ident[:]).then_inc(s["constants"], 1)
                for n in range(2):
                    nc.vector.memset(CNT[n][:], 0.0).then_inc(s["free"], 1)
                dve.wait_ge(s["constants"], 7)

                def mean(n, b):
                    link = Linker(dve, c_ln, b, 4 + RSQRT_LINKS)
                    if not (isinstance(b, int) and b < 2):
                        dve.wait_ge(s["z"], b - 1)
                    for i in range(NT):
                        last = nc.vector.bn_stats(ST[n][:, i, :], X[:, b * NT + i, :])
                    last.then_inc(c_ln, 1)
                    link.k += 1
                    wait_apart(dve, c_ln, link.before + link.k)
                    for i in range(NT):
                        last = nc.vector.bn_aggr(MV[n][:, i, :], ST[n][:, i, :])
                    link(last)
                    link(nc.vector.tensor_scalar(RL[n][:, 0, :], MV[n][:, :, 1], 1e-5, None, ALU.add))
                    rsqrt(dve, nc, link, RL[n][:, 0, :], RL[n][:, 1, :], RL[n][:, 2, :])
                    link(nc.vector.scalar_tensor_tensor(out=RL[n][:, 3, :], in0=MV[n][:, :, 0], scalar=-1.0,
                                                        in1=RL[n][:, 1, :], op0=ALU.mult, op1=ALU.mult))
                    nc.vector.tensor_copy(RL[n][:, 2, 0:1], RL[n][:, 3, 0:1]).then_inc(s["mean"], 1)
                    link.done()

                def rows_of(n, v):
                    return ROWS[n][:, v, :].unsqueeze(1).to_broadcast([P, 2, D])

                def h_part(k):
                    def step(n, b):
                        link = Linker(dve, c_h, 4 * b + k, 2)
                        tiles = H[n][:, 2 * k:2 * k + 2, :]
                        if k == 0:
                            dve.wait_ge(s["z"], b + 1)
                            dve.wait_ge(s["rows%d" % n], 8 * (b - n) + 16)
                        link(nc.vector.tensor_tensor(tiles, tiles, rows_of(n, 1), ALU.mult))
                        link(nc.vector.tensor_tensor(tiles, tiles, rows_of(n, 0), ALU.add))
                        for i in range(2 * k, 2 * k + 2):
                            last = nc.vector.scalar_tensor_tensor(
                                out=JUNK[n][:].rearrange("p a b -> p (a b)")[:, i * D:(i + 1) * D], in0=H[n][:, i, :],
                                scalar=1.0, in1=WR[:], op0=ALU.mult, op1=ALU.mult, accum_out=SCR[n][:, i:i + 1])
                        last.then_inc(s["router"], 1)
                        link.done()
                        if k == 3:
                            dve.wait_ge(s["router"], 4 * b + 4)
                            nc.vector.tensor_tensor(DG[n][:], ident[:].unsqueeze(1).to_broadcast([P, NT, P]),
                                                    bcast(SCR[n][:], P), ALU.mult).then_inc(s["diagonals"], 1)
                    return step

                def junk(n, i):
                    if i >= 6:
                        return JUNK[n][:, i - 6, :]
                    r = (EX, ET)[i // 3][n][:].rearrange("p h k -> p (h k)").bitcast(BF16)
                    return r[:, (i % 3) * 9 * P:(i % 3 + 1) * 9 * P]

                def rank_part(i):
                    def step(n, b):
                        if i == 0:
                            dve.wait_ge(s["score_rows"], b + 1)
                        sc, at = SCR[n][:, i:i + 1], 0
                        for c in range(2):
                            lo, hi = c * 4, c * 4 + 4
                            if i < hi:
                                a = max(i, lo)
                                at += (hi - a) * P
                                nc.vector.tensor_scalar(junk(n, i)[:, at - (hi - a) * P:at], BK[n][c][:, (a - lo) * P:], sc,
                                                        0.0, ALU.is_gt, ALU.add, accum_out=CNT[n][:, i, c:c + 1])
                            if i > lo:
                                a = min(i, hi)
                                at += (a - lo) * P
                                nc.vector.tensor_scalar(junk(n, i)[:, at - (a - lo) * P:at], BK[n][c][:, 0:(a - lo) * P], sc,
                                                        0.0, ALU.is_ge, ALU.add, accum_out=CNT[n][:, i, 2 + c:3 + c])
                        nc.vector.scalar_tensor_tensor(out=junk(n, i)[:, at:at + P],
                                                       in0=BK[n][i // 4][:, (i % 4) * P:(i % 4 + 1) * P], scalar=sc,
                                                       in1=LOW[:], op0=ALU.is_equal, op1=ALU.mult,
                                                       accum_out=CNT[n][:, i, 4:5]).then_inc(s["counted"], 1)
                    return step

                def one_hot(n, b):
                    link = Linker(dve, c_rank, b, 1)
                    dve.wait_ge(s["counted"], NT * b + NT)
                    link(nc.vector.tensor_reduce(RANK[n][:], CNT[n][:], AX.X, ALU.add))
                    link.done()
                    nc.vector.tensor_tensor(PM[n][:], RANKS[:].unsqueeze(1).to_broadcast([P, NT, P]),
                                            bcast(RANK[n][:], P), ALU.is_equal).then_inc(s["one_hot"], 1)

                def normed(src_of, ready, name, which, chain):
                    def step(n, b):
                        link = Linker(dve, chain, b, 1 + RSQRT_LINKS)
                        dve.wait_ge(s[ready], b + 1)
                        link(nc.vector.tensor_scalar(SM[n][:, which, 1:2], SM[n][:, which, 0:1], 1.0 / D, 1e-6, ALU.mult,
                                                     ALU.add))
                        rsqrt(dve, nc, link, SM[n][:, which, 1:2], SM[n][:, which, 2:3], SM[n][:, which, 3:4])
                        nc.vector.tensor_scalar(U[n][:], src_of[n][:], SM[n][:, which, 2:3], None, ALU.mult).then_inc(s[name], 1)
                        link.done()
                    return step

                def v_out(n, b):
                    dve.wait_ge(s["qkv"], b + 1)
                    nc.vector.tensor_copy(V[n][:, :, 0:DK],
                                          BK[n][2][:, D:2 * D].rearrange("p (h d) -> p h d", d=DK)).then_inc(s["v_out"], 1)

                def row_max(n, b):
                    link = Linker(dve, c_max, b, 4)
                    for r in range(4):
                        dve.wait_ge(s["scores"], 4 * b + r + 1)
                        link(nc.vector.tensor_reduce(MX[n][:, 0, r::4],
                                                     BK[n][r][:, :].rearrange("p (a b) -> p a b", a=4), AX.X, ALU.max))
                        nc.vector.tensor_scalar(MX[n][:, 1, r::4], MX[n][:, 0, r::4], -(DK ** -0.5), None,
                                                ALU.mult).then_inc(s["max"], 1)
                    link.done()

                def exp_t_out(n, b):
                    for c in range(2, 4):
                        dve.wait_ge(s["expT"], 4 * b + c + 1)
                        last = nc.vector.tensor_copy(ET[n][:, c::4, :],
                                                     BK[n][c][:, :].rearrange("p (a b) -> p a b", a=4))
                    last.then_inc(s["expT_out_v"], 1)

                def heads_out(n, b):
                    link = Linker(dve, c_heads, b, 1)
                    dve.wait_ge(s["heads"], b + 1)
                    o = BK[n][0][:, 0:NH * (DK + 1)].rearrange("p (h e) -> p h e", e=DK + 1)
                    link(nc.vector.reciprocal(MX[n][:, 0, :], o[:, :, DK]))
                    nc.vector.tensor_tensor(U[n][:].rearrange("p (h d) -> p h d", d=DK), o[:, :, 0:DK],
                                            bcast(MX[n][:, 0, :], DK), ALU.mult).then_inc(s["heads_out"], 1)
                    link.done()

                def xa(n, b):
                    dve.wait_ge(s["attended"], b + 1)
                    nc.vector.tensor_tensor(XA[n][:], BK[n][2][:, 0:D], SEL[n][:], ALU.add).then_inc(s["xa"], 1)

                def gated(n, b):
                    link = Linker(dve, c_gate, b, 1)
                    dve.wait_ge(s["tanh"], b + 1)
                    k = (NF - 4) * P
                    nc.vector.scalar_tensor_tensor(out=TH[n][:, 0:4 * P], in0=TH[n][:, 0:4 * P], scalar=1.0,
                                                   in1=BK[n][0][:, :], op0=ALU.add, op1=ALU.mult)
                    link(nc.vector.scalar_tensor_tensor(out=TH[n][:, 4 * P:], in0=TH[n][:, 4 * P:], scalar=1.0,
                                                        in1=BK[n][1][:, 0:k], op0=ALU.add, op1=ALU.mult))
                    nc.vector.tensor_tensor(GH[n][:, 0:4 * P], TH[n][:, 0:4 * P], BK[n][3][:, :], ALU.mult)
                    nc.vector.tensor_tensor(GH[n][:, 4 * P:], TH[n][:, 4 * P:], BK[n][1][:, 2 * P:2 * P + k],
                                            ALU.mult).then_inc(s["gated"], 1)
                    link.done()

                def delta(n, b):
                    dve.wait_ge(s["processed"], b + 1)
                    nc.vector.tensor_tensor(U[n][:], BK[n][2][:, 0:D], ROWS[n][:, 2, :], ALU.mult).then_inc(s["delta"], 1)

                def add_x(n, b):
                    dve.wait_ge(s["x_h"], b + 1)
                    dve.wait_ge(s["scattered"], b + 1)
                    for m in range(4):
                        xt = X[:, bass.ds(b * NT + 2 * m, 2), :]
                        last = nc.vector.tensor_tensor(xt, BK[n][m][:, :].rearrange("p (a b) -> p a b", a=2), xt, ALU.add)
                    last.then_inc(s["free"], 1)

                staggered(dve, [(.13 + .036 * k, h_part(k)) for k in range(4)] +
                          [(.29 + .04 * i, rank_part(i)) for i in range(NT)] +
                          [(.59, one_hot), (.67, normed(SEL, "sum1", "u1", 0, c_u1)), (.78, v_out)],
                          [(.08, row_max), (.201, exp_t_out), (.35, heads_out), (.46, xa),
                           (.5, normed(XA, "sum2", "u2", 1, c_u2)), (.63, gated), (.68, delta), (.8, add_x)],
                          [(.75, mean)])


def time_mixing(nc, sem, g, w):
    with ExitStack() as st:
        def sb(name, shape, dtype=F32):
            return st.enter_context(nc.sbuf_tensor("t_" + name, shape, dtype))

        WT = sb("WT", [P, 3, 2, D])
        WO = sb("WO", [P, 2, D])
        COL = sb("COL", [P, 5, 2])
        with ExitStack() as tmp:
            WN = tmp.enter_context(nc.sbuf_tensor("t_WN", [P, 3, 2, D], F32))
            names = ("time_decay", "time_first", "time_mix_k", "time_mix_v", "time_mix_r")
            loads = [(COL[:, m, :], w[n].rearrange("(h p) -> p h", p=P)) for m, n in enumerate(names)]
            loads += [(WN[:, m], w[n].rearrange("(h p) c -> p h c", p=P)) for m, n in enumerate(("Wk", "Wv", "Wr"))]
            loads += [(WO[:], w["Wo"].rearrange("(h p) c -> p h c", p=P))]
            jobs = [(WN[:, m, o, h * P:(h + 1) * P], WT[:, m, h, o * P:(o + 1) * P], 1.0)
                    for m in range(3) for o in range(2) for h in range(2)]
            transpose_weights(nc, sem, g, "t_weights", jobs, loads)

        EW, EU = sb("EW", [P, 2]), sb("EU", [P, 2])
        S2 = range(2)
        WS, WOG = [sb(f"WS{s}", [P, 2, D]) for s in S2], [sb(f"WOG{s}", [P, 2, D]) for s in S2]
        ST, MV = [sb(f"ST{s}", [P, NT, 6]) for s in S2], [sb(f"MV{s}", [P, NT, 2]) for s in S2]
        RL = [sb(f"RL{s}", [P, 4, NT]) for s in S2]
        Z = [sb(f"Z{s}", [P, NT, D]) for s in S2]
        HT = [sb(f"HT{s}", [P, 2, T + 1]) for s in S2]
        XK = [sb(f"XK{s}", [P, 2, T + 1]) for s in S2]
        XV = [sb(f"XV{s}", [P, 2, T]) for s in S2]
        XR = [sb(f"XR{s}", [P, 2, T]) for s in S2]
        EK = [sb(f"EK{s}", [P, 2, T]) for s in S2]
        EKV = [sb(f"EKV{s}", [P, 2, T]) for s in S2]
        DIFF = [Z[s][:].rearrange("p (h i) c -> p h (i c)", h=2) for s in S2]
        TH = DIFF
        SA_, SB_ = HT, XK
        REC = XV
        Y = XR
        BK = [[st.enter_context(nc.psum_tensor(f"t_BK{s}{n}", [P, 512], F32)) for n in range(4)] for s in S2]
        X, ident, MOD = g["X"], g["ident"], g["MOD"]
        names = ["zero", "decay", "eu_ew", "half", "free", "wo_scaled", "woT", "woT_out", "mean", "z", "zT", "h",
                 "difference", "mixed", "k", "exp_k", "v", "exp_kv", "r", "tanh_r", "scanned_a", "scanned_b", "denominator",
                 "numerator", "reciprocal", "quotient", "y", "projected"]
        s = {n: sem("t_" + n) for n in names}
        c_ln = sem("t_chain_ln")

        with nc.Block() as block:
            @block.gpsimd
            def _(pool):
                for n in S2:
                    nc.gpsimd.memset(HT[n][:, :, 0], 0.0).then_inc(s["zero"], 1)
                    nc.gpsimd.memset(XK[n][:, :, 0], 0.0).then_inc(s["zero"], 1)

                def difference(n, b):
                    pool.wait_ge(s["h"], b + 1)
                    for h in range(2):
                        nc.gpsimd.tensor_tensor(DIFF[n][:, h, :], HT[n][:, h, 1:T + 1], HT[n][:, h, 0:T],
                                                ALU.subtract).then_inc(s["difference"], 1)

                staggered(pool, [(.4, difference)], [])

            @block.tensor
            def _(pe):
                def wo_t(n, b):
                    pe.wait_ge(s["wo_scaled"], b + 1)
                    for o in range(2):
                        for h in range(2):
                            last = nc.tensor.transpose(BK[n][0][:, h * D + o * P:h * D + (o + 1) * P],
                                                       WS[n][:, o, h * P:(h + 1) * P], ident[:])
                    last.then_inc(s["woT"], 1)

                def z_t(n, b):
                    pe.wait_ge(s["woT_out"], b + 1)
                    pe.wait_ge(s["z"], b + 1)
                    for h in range(2):
                        for i in range(NT):
                            last = nc.tensor.transpose(BK[n][2 * h + i // 4][:, (i % 4) * P:(i % 4 + 1) * P],
                                                       Z[n][:, i, h * P:(h + 1) * P], ident[:])
                    last.then_inc(s["zT"], 1)

                def project(m, x, off, name, before):
                    def half(o):
                        def step(n, b):
                            pe.wait_ge(s["mixed"], 3 * b + m + 1)
                            if before:
                                pe.wait_ge(s[before], 2 * b + o + 1)
                            for c in range(2):
                                for h in range(2):
                                    last = nc.tensor.matmul(BK[n][2 * o + c][:, :], WT[:, m, h, o * P:(o + 1) * P],
                                                            x[n][:, h, off + c * 512:off + (c + 1) * 512],
                                                            start=(h == 0), stop=(h == 1))
                            last.then_inc(s[name], 1)
                        return step
                    return half

                def project_out(n, b):
                    pe.wait_ge(s["y"], 2 * b + 2)
                    for i in range(NT):
                        for h in range(2):
                            last = nc.tensor.matmul(BK[n][i // 2][:, (i % 2) * D:(i % 2 + 1) * D],
                                                    Y[n][:, h, i * P:(i + 1) * P], WOG[n][:, h, :],
                                                    start=(h == 0), stop=(h == 1))
                    last.then_inc(s["projected"], 1)

                k, v, r = project(0, XK, 1, "k", None), project(1, XV, 0, "v", "exp_k"), project(2, XR, 0, "r", "exp_kv")
                staggered(pe, [(.07, wo_t), (.2, z_t), (.64, k(0)), (.68, k(1)), (.84, v(0)), (.9, v(1))],
                          [(.04, r(0)), (.06, r(1)), (.8, project_out)])

            @block.scalar
            def _(act):
                nc.scalar.activation(EU[:], COL[:, 1, :], ACT.Exp)
                nc.scalar.activation(EW[:], COL[:, 0, :], ACT.Exp).then_inc(s["decay"], 1)
                act.wait_ge(s["decay"], 1)
                nc.scalar.activation(EW[:], EW[:], ACT.Exp, scale=-1.0).then_inc(s["eu_ew"], 1)
                nc.scalar.activation(WO[:], WO[:], ACT.Copy, scale=0.5).then_inc(s["half"], 1)
                act.wait_ge(s["half"], 1)
                act.wait_ge(s["zero"], 4)

                def scale_wo(n, b):
                    act.wait_ge(s["free"], b + 1)
                    for h in range(2):
                        last = nc.scalar.activation(WS[n][:, h, :], WO[:, h, :], ACT.Identity,
                                                    scale=MOD[:, 1, 2 * GA + h, bass.ds(b, 1)])
                    last.then_inc(s["wo_scaled"], 1)

                def wo_out(n, b):
                    act.wait_ge(s["woT"], b + 1)
                    nc.scalar.activation(WOG[n][:], BK[n][0][:, :].rearrange("p (h c) -> p h c", h=2),
                                         ACT.Copy).then_inc(s["woT_out"], 1)

                def z(n, b):
                    act.wait_ge(s["mean"], b + 1)
                    for i in range(NT):
                        last = nc.scalar.activation(Z[n][:, i, :], X[:, b * NT + i, :], ACT.Identity,
                                                    bias=RL[n][:, 3, i:i + 1], scale=RL[n][:, 1, i:i + 1])
                    last.then_inc(s["z"], 1)

                def h_t(n, b):
                    act.wait_ge(s["zT"], b + 1)
                    for h in range(2):
                        for c in range(2):
                            last = nc.scalar.activation(HT[n][:, h, 1 + c * 512:1 + (c + 1) * 512], BK[n][2 * h + c][:, :],
                                                        ACT.Identity, bias=MOD[:, 1, 2 * SA + h, bass.ds(b, 1)],
                                                        scale=MOD[:, 1, 2 * CA + h, bass.ds(b, 1)])
                    last.then_inc(s["h"], 1)

                def unary(out, func, scale, ready, name):
                    def half(o):
                        def step(n, b):
                            act.wait_ge(s[ready], 2 * b + o + 1)
                            for c in range(2):
                                last = nc.scalar.activation(out[n][:, o, c * 512:(c + 1) * 512], BK[n][2 * o + c][:, :],
                                                            func, scale=scale)
                            last.then_inc(s[name], 1)
                        return step
                    return half

                exp_k, tanh_r = unary(EK, ACT.Exp, 1.0, "k", "exp_k"), unary(TH, ACT.Tanh, 0.5, "r", "tanh_r")
                staggered(act, [(.05, scale_wo), (.08, wo_out), (.09, z), (.28, h_t), (.7, exp_k(0)), (.74, exp_k(1))],
                          [(.1, tanh_r(0)), (.12, tanh_r(1))])

            @block.vector
            def _(dve):
                for n in S2:
                    nc.vector.memset(RL[n][:], 0.0).then_inc(s["free"], 1)
                dve.wait_ge(s["eu_ew"], 1)
                dve.wait_ge(s["zero"], 4)

                def mean(n, b):
                    link = Linker(dve, c_ln, b, 4 + RSQRT_LINKS)
                    if not (isinstance(b, int) and b < 2):
                        dve.wait_ge(s["z"], b - 1)
                    for i in range(NT):
                        last = nc.vector.bn_stats(ST[n][:, i, :], X[:, b * NT + i, :])
                    last.then_inc(c_ln, 1)
                    link.k += 1
                    wait_apart(dve, c_ln, link.before + link.k)
                    for i in range(NT):
                        last = nc.vector.bn_aggr(MV[n][:, i, :], ST[n][:, i, :])
                    link(last)
                    link(nc.vector.tensor_scalar(RL[n][:, 0, :], MV[n][:, :, 1], 1e-5, None, ALU.add))
                    rsqrt(dve, nc, link, RL[n][:, 0, :], RL[n][:, 1, :], RL[n][:, 2, :])
                    link(nc.vector.scalar_tensor_tensor(out=RL[n][:, 3, :], in0=MV[n][:, :, 0], scalar=-1.0,
                                                        in1=RL[n][:, 1, :], op0=ALU.mult, op1=ALU.mult))
                    nc.vector.tensor_copy(RL[n][:, 2, 0:1], RL[n][:, 3, 0:1]).then_inc(s["mean"], 1)
                    link.done()

                def mix(m, x, off):
                    def step(n, b):
                        for h in range(2):
                            dve.wait_ge(s["difference"], 2 * b + h + 1)
                            last = nc.vector.scalar_tensor_tensor(
                                out=x[n][:, h, off:off + T], in0=DIFF[n][:, h, :], scalar=COL[:, 2 + m, h:h + 1],
                                in1=HT[n][:, h, 0:T], op0=ALU.mult, op1=ALU.add)
                        last.then_inc(s["mixed"], 1)
                    return step

                def exp_kv(o):
                    def step(n, b):
                        dve.wait_ge(s["exp_k"], 2 * b + o + 1)
                        dve.wait_ge(s["v"], 2 * b + o + 1)
                        for c in range(2):
                            cols = slice(c * 512, (c + 1) * 512)
                            last = nc.vector.tensor_tensor(EKV[n][:, o, cols], EK[n][:, o, cols], BK[n][2 * o + c][:, :], ALU.mult)
                        last.then_inc(s["exp_kv"], 1)
                    return step

                def scan(o, state, x, name):
                    def step(n, b):
                        dve.wait_ge(s["exp_kv"], 2 * b + o + 1)
                        nc.vector.tensor_tensor_scan(state[n][:, o, 1:T + 1], EW[:, o:o + 1].to_broadcast([P, T]),
                                                     x[n][:, o, :], 0.0, ALU.mult, ALU.add).then_inc(s[name], 1)
                    return step

                def with_bonus(o, state, x, name, scanned):
                    def step(n, b):
                        dve.wait_ge(s[scanned], 2 * b + o + 1)
                        nc.vector.scalar_tensor_tensor(out=x[n][:, o, :], in0=x[n][:, o, :], scalar=EU[:, o:o + 1],
                                                       in1=state[n][:, o, 0:T], op0=ALU.mult, op1=ALU.add).then_inc(s[name], 1)
                    return step

                def reciprocal(o):
                    def step(n, b):
                        dve.wait_ge(s["denominator"], 2 * b + o + 1)
                        nc.vector.reciprocal(REC[n][:, o, :], EK[n][:, o, :]).then_inc(s["reciprocal"], 1)
                    return step

                def quotient(o):
                    def step(n, b):
                        dve.wait_ge(s["numerator"], 2 * b + o + 1)
                        dve.wait_ge(s["reciprocal"], 2 * b + o + 1)
                        nc.vector.tensor_tensor(EK[n][:, o, :], EKV[n][:, o, :], REC[n][:, o, :],
                                                ALU.mult).then_inc(s["quotient"], 1)
                    return step

                def y(o):
                    def step(n, b):
                        dve.wait_ge(s["quotient"], 2 * b + o + 1)
                        dve.wait_ge(s["tanh_r"], 2 * b + 2)
                        nc.vector.scalar_tensor_tensor(out=Y[n][:, o, :], in0=TH[n][:, o, :], scalar=1.0, in1=EK[n][:, o, :],
                                                       op0=ALU.add, op1=ALU.mult).then_inc(s["y"], 1)
                    return step

                def add_x(n, b):
                    dve.wait_ge(s["projected"], b + 1)
                    for m in range(4):
                        xt = X[:, bass.ds(b * NT + 2 * m, 2), :]
                        last = nc.vector.tensor_tensor(xt, BK[n][m][:, :].rearrange("p (a b) -> p a b", a=2), xt, ALU.add)
                    last.then_inc(s["free"], 1)

                chain = [(.01, exp_kv(0)), (.03, exp_kv(1))]
                for o in range(2):
                    for n, step in enumerate((scan(o, SB_, EK, "scanned_b"), scan(o, SA_, EKV, "scanned_a"),
                                              with_bonus(o, SB_, EK, "denominator", "scanned_b"),
                                              with_bonus(o, SA_, EKV, "numerator", "scanned_a"), reciprocal(o), quotient(o),
                                              y(o))):
                        chain.append((.14 + .24 * o + .03 * n, step))
                staggered(dve, [(.5, mix(0, XK, 1)), (.55, mix(1, XV, 0)), (.6, mix(2, XR, 0))],
                          chain + [(.92, add_x)], [(.65, mean)])


def expert_layer(nc, sem, g, w, out):
    with ExitStack() as st:
        def sb(name, shape, dtype=F32):
            return st.enter_context(nc.sbuf_tensor("e_" + name, shape, dtype))

        S2 = range(2)
        NTT = B * NT
        GN, GW = sb("GN", [NE, D]), sb("GW", [P, 2, NE])
        ONES, PREF = sb("ONES", [P, P]), sb("PREF", [P, NE])
        ST, MV = [sb(f"ST{s}", [P, NT, 6]) for s in S2], [sb(f"MV{s}", [P, NT, 2]) for s in S2]
        RL = [sb(f"RL{s}", [P, 4, NT]) for s in S2]
        Z = [sb(f"Z{s}", [P, NT, D]) for s in S2]
        HT = [sb(f"HT{s}", [P, 2, T]) for s in S2]
        PROB, EQ, TOP = (sb(n, [P, NTT, NE]) for n in ("PROB", "EQ", "TOP"))
        TOP2, COMB = sb("TOP2", [P, NTT, NE]), sb("COMB", [P, NTT, NE])
        RED = sb("RED", [P, NTT])
        CNT, KEEP, ANY = sb("CNT", [P, NE]), sb("KEEP", [P, NE]), sb("ANY", [P, 1])
        FLAG = sb("FLAG", [P, 1], I32)
        W1, W2 = sb("W1", [P, 2, D]), sb("W2", [P, 2, D])
        B1, B2 = sb("B1", [P, 2]), sb("B2", [P, D])
        U, YB, ACC = sb("U", [P, 2, T]), sb("YB", [P, NT, D]), sb("ACC", [P, NT, D])
        GROW = sb("GROW", [P, D])
        BK = [[st.enter_context(nc.psum_tensor(f"e_BK{s}{n}", [P, 512], F32)) for n in range(4)] for s in S2]
        X, ident, MOD = g["X"], g["ident"], g["MOD"]
        s = {n: sem("e_" + n) for n in ("stored", "constants", "gate_loaded", "gateT", "gateT_out", "free", "mean", "z_low",
                                        "z", "zT", "h", "logits", "shifted", "exp", "counted", "counts", "flag")}
        f = {n: sem("e_full_" + n) for n in ("free", "mean", "z", "zT", "h", "row", "weights", "hidden", "relu", "outputs",
                                             "expert_done", "cleared", "gated", "stored")}
        c_ln, c_top, c_expert = (sem("e_chain_" + n) for n in ("ln", "top", "expert"))
        xo = out.rearrange("b (i p) c -> p (b i) c", p=P)

        def z_t(pe, n, b, sm):
            pe.wait_ge(sm["z"], b + 1)
            if sm is s:
                pe.wait_ge(s["z_low"], b + 1)
            for h in range(2):
                for i in range(NT):
                    last = nc.tensor.transpose(BK[n][2 * h + i // 4][:, (i % 4) * P:(i % 4 + 1) * P],
                                               Z[n][:, i, h * P:(h + 1) * P], ident[:])
            last.then_inc(sm["zT"], 1)

        def z_rows(act, n, b, sm):
            act.wait_ge(sm["mean"], b + 1)
            if sm is s:
                act.wait_ge(s["free"], b + 1)
            for i in range(NT // 2 if sm is s else 0, NT):
                last = nc.scalar.activation(Z[n][:, i, :], X[:, bass.ds(b * NT + i, 1), :].rearrange("p a c -> p (a c)"),
                                            ACT.Identity, bias=RL[n][:, 3, i:i + 1], scale=RL[n][:, 1, i:i + 1])
            last.then_inc(sm["z"], 1)

        def h_t(act, n, b, sm):
            act.wait_ge(sm["zT"], b + 1)
            for h in range(2):
                for c in range(2):
                    last = nc.scalar.activation(HT[n][:, h, c * 512:(c + 1) * 512], BK[n][2 * h + c][:, :], ACT.Identity,
                                                bias=MOD[:, 1, 2 * SB + h, bass.ds(b, 1)],
                                                scale=MOD[:, 1, 2 * CB + h, bass.ds(b, 1)])
            last.then_inc(sm["h"], 1)

        def mean(dve, n, b, sm, links_before):
            link = Linker(dve, c_ln, b + links_before, 4 + RSQRT_LINKS)
            if sm is not s:
                dve.wait_ge(sm["free"], b + 1)
            elif not (isinstance(b, int) and b < 2):
                dve.wait_ge(s["z"], b - 1)
                dve.wait_ge(s["z_low"], b - 1)
            for i in range(NT):
                last = nc.vector.bn_stats(ST[n][:, i, :], X[:, b * NT + i, :])
            last.then_inc(c_ln, 1)
            link.k += 1
            wait_apart(dve, c_ln, link.before + link.k)
            for i in range(NT):
                last = nc.vector.bn_aggr(MV[n][:, i, :], ST[n][:, i, :])
            link(last)
            link(nc.vector.tensor_scalar(RL[n][:, 0, :], MV[n][:, :, 1], 1e-5, None, ALU.add))
            rsqrt(dve, nc, link, RL[n][:, 0, :], RL[n][:, 1, :], RL[n][:, 2, :])
            link(nc.vector.scalar_tensor_tensor(out=RL[n][:, 3, :], in0=MV[n][:, :, 0], scalar=-1.0,
                                                in1=RL[n][:, 1, :], op0=ALU.mult, op1=ALU.mult))
            nc.vector.tensor_copy(RL[n][:, 2, 0:1], RL[n][:, 3, 0:1]).then_inc(sm["mean"], 1)
            link.done()

        with nc.Block() as block:
            @block.sync
            def _(sp):
                sp.dma_start(GN[:], w["gate_w"]).then_inc(s["gate_loaded"], 16)
                sp.dma_start(xo, X[:]).then_inc(s["stored"], 16)
                sp.wait_ge(s["flag"], 1)
                kept = sp.value_load(FLAG[0:1, 0:1], min_val=0, max_val=1)
                with sp.If(kept > 0):
                    with sp.Fori(0, B) as b:
                        sp.wait_ge(f["free"], b + 1)
                        sp.dma_start(GROW[:].rearrange("p (h c) -> p h c", h=2),
                                     g["mod_dram"][1, 2 * GB:2 * GB + 2, bass.ds(b, 1), :].rearrange(
                                         "v b c -> b v c").to_broadcast([P, 2, P])).then_inc(f["row"], 16)
                        with sp.Fori(0, NE) as e:
                            sp.wait_ge(f["expert_done"], b * NE + e + 1)
                            ex = bass.ds(e, 1)
                            sp.dma_start(W1[:], w["W1"][ex].rearrange("e (h p) c -> p (e h) c", p=P)).then_inc(f["weights"], 16)
                            sp.dma_start(W2[:], w["W2"][ex].rearrange("e (h p) c -> p (e h) c", p=P)).then_inc(f["weights"], 16)
                            sp.dma_start(B1[:], w["b1"][ex].rearrange("e (h p) -> p (e h)", p=P),
                                         allow_slow_non_contiguous=True).then_inc(f["weights"], 16)
                            sp.dma_start(B2[:], w["b2"][ex].to_broadcast([P, D])).then_inc(f["weights"], 16)
                    sp.wait_ge(f["free"], B + 1)
                    sp.dma_start(xo, X[:]).then_inc(f["stored"], 16)
                    sp.wait_ge(f["stored"], 16)
                sp.wait_ge(s["stored"], 16)

            @block.gpsimd
            def _(pool):
                nc.gpsimd.memset(ONES[:], 1.0).then_inc(s["constants"], 1)
                nc.gpsimd.iota(PREF[:], pattern=[[-1, NE]], base=NE, channel_multiplier=0,
                               allow_small_or_imprecise_dtypes=True).then_inc(s["constants"], 1)

            @block.tensor
            def _(pe):
                pe.wait_ge(s["gate_loaded"], 16)
                for h in range(2):
                    last = nc.tensor.transpose(BK[0][0][:, h * NE:(h + 1) * NE], GN[:, h * P:(h + 1) * P], ident[0:NE, 0:NE])
                last.then_inc(s["gateT"], 1)
                pe.wait_ge(s["gateT_out"], 1)

                def logits(n, b):
                    pe.wait_ge(s["h"], b + 1)
                    for i in range(NT):
                        for h in range(2):
                            last = nc.tensor.matmul(BK[n][0][:, i * NE:(i + 1) * NE], HT[n][:, h, i * P:(i + 1) * P],
                                                    GW[:, h, :], start=(h == 0), stop=(h == 1))
                    last.then_inc(s["logits"], 1)

                staggered(pe, [(.3, lambda n, b: z_t(pe, n, b, s))], [(.5, logits)])
                pe.wait_ge(s["counted"], 1)
                nc.tensor.matmul(BK[0][0][:, 0:NE], ONES[:], CNT[:], start=True, stop=True).then_inc(s["counts"], 1)
                pe.wait_ge(s["flag"], 1)
                kept = pe.value_load(FLAG[0:1, 0:1], min_val=0, max_val=1)
                with pe.If(kept > 0):
                    with pe.Fori(0, B) as b:
                        z_t(pe, 0, b, f)
                        wait_apart(pe, f["h"], b + 1)
                        with pe.Fori(0, NE) as e:
                            pe.wait_ge(f["weights"], 64 * (b * NE + e) + 64)
                            for o in range(2):
                                for c in range(2):
                                    for h in range(2):
                                        last = nc.tensor.matmul(BK[0][2 * o + c][:, :], W1[:, h, o * P:(o + 1) * P],
                                                                HT[0][:, h, c * 512:(c + 1) * 512], start=(h == 0), stop=(h == 1))
                            last.then_inc(f["hidden"], 1)
                            pe.wait_ge(f["relu"], b * NE + e + 1)
                            for i in range(NT):
                                for h in range(2):
                                    last = nc.tensor.matmul(BK[1][i // 2][:, (i % 2) * D:(i % 2 + 1) * D],
                                                            U[:, h, i * P:(i + 1) * P], W2[:, h, :], start=(h == 0), stop=(h == 1))
                            last.then_inc(f["outputs"], 1)

            @block.scalar
            def _(act):
                staggered(act, [(.05, lambda n, b: z_rows(act, n, b, s)), (.6, lambda n, b: h_t(act, n, b, s))], [])
                act.wait_ge(s["shifted"], 1)
                nc.scalar.activation(PROB[:], PROB[:], ACT.Exp).then_inc(s["exp"], 1)
                act.wait_ge(s["flag"], 1)
                kept = act.value_load(FLAG[0:1, 0:1], min_val=0, max_val=1)
                with act.If(kept > 0):
                    with act.Fori(0, B) as b:
                        z_rows(act, 0, b, f)
                        h_t(act, 0, b, f)
                        with act.Fori(0, NE) as e:
                            act.wait_ge(f["hidden"], b * NE + e + 1)
                            for o in range(2):
                                for c in range(2):
                                    last = nc.scalar.activation(U[:, o, c * 512:(c + 1) * 512], BK[0][2 * o + c][:, :],
                                                                ACT.Relu, bias=B1[:, o:o + 1])
                            last.then_inc(f["relu"], 1)

            @block.vector
            def _(dve):
                for n in S2:
                    nc.vector.memset(RL[n][:], 0.0).then_inc(s["free"], 1)
                dve.wait_ge(s["gateT"], 1)
                nc.vector.tensor_copy(GW[:], BK[0][0][:, 0:2 * NE].rearrange("p (h e) -> p h e", h=2)).then_inc(s["gateT_out"], 1)

                def z_low(n, b):
                    dve.wait_ge(s["free"], b + 1)
                    dve.wait_ge(s["mean"], b + 1)
                    for i in range(NT // 2):
                        last = nc.vector.tensor_scalar(Z[n][:, i, :], X[:, b * NT + i, :], MV[n][:, i, 0:1],
                                                       RL[n][:, 1, i:i + 1], ALU.subtract, ALU.mult)
                    last.then_inc(s["z_low"], 1)

                def logits_out(n, b):
                    dve.wait_ge(s["logits"], b + 1)
                    nc.vector.tensor_copy(PROB[:, bass.ds(b * NT, NT), :],
                                          BK[n][0][:, 0:NT * NE].rearrange("p (i e) -> p i e", e=NE)).then_inc(s["free"], 1)

                staggered(dve, [(.05, z_low)], [(.8, logits_out)], [(.2, lambda n, b: mean(dve, n, b, s, 0))])

                link = Linker(dve, c_top, 0, 20)
                dve.wait_ge(s["free"], 2 + B)
                link(nc.vector.tensor_reduce(RED[:], PROB[:], AX.X, ALU.max))
                nc.vector.tensor_tensor(PROB[:], PROB[:], bcast(RED[:], NE), ALU.subtract).then_inc(s["shifted"], 1)
                dve.wait_ge(s["exp"], 1)
                link(nc.vector.tensor_reduce(RED[:], PROB[:], AX.X, ALU.add))
                link(nc.vector.reciprocal(RED[:], RED[:]))
                link(nc.vector.tensor_tensor(PROB[:], PROB[:], bcast(RED[:], NE), ALU.mult))
                dve.wait_ge(s["constants"], 2)
                pref = PREF[:].unsqueeze(1).to_broadcast([P, NTT, NE])
                for src, top in ((PROB, TOP), (COMB, TOP2)):
                    if src is COMB:
                        link(nc.vector.scalar_tensor_tensor(out=COMB[:], in0=TOP[:], scalar=-2.0, in1=PROB[:],
                                                            op0=ALU.mult, op1=ALU.add))
                    link(nc.vector.tensor_reduce(RED[:], src[:], AX.X, ALU.max))
                    link(nc.vector.tensor_tensor(EQ[:], src[:], bcast(RED[:], NE), ALU.is_equal))
                    link(nc.vector.tensor_tensor(EQ[:], EQ[:], pref, ALU.mult))
                    link(nc.vector.tensor_reduce(RED[:], EQ[:], AX.X, ALU.max))
                    link(nc.vector.tensor_tensor(top[:], EQ[:], bcast(RED[:], NE), ALU.is_equal))
                link(nc.vector.tensor_tensor(TOP[:], TOP[:], TOP2[:], ALU.add))
                nc.vector.tensor_reduce(CNT[:], TOP[:].rearrange("p t e -> p e t"), AX.X, ALU.add).then_inc(s["counted"], 1)
                dve.wait_ge(s["counts"], 1)
                link(nc.vector.tensor_scalar(KEEP[:], BK[0][0][:, 0:NE], float(EXPERT_CAP), None, ALU.is_le))
                link(nc.vector.tensor_reduce(ANY[:], KEEP[:], AX.X, ALU.max))
                nc.vector.tensor_copy(FLAG[:], ANY[:]).then_inc(s["flag"], 1)
                dve.wait_ge(s["flag"], 1)
                kept = dve.value_load(FLAG[0:1, 0:1], min_val=0, max_val=1)
                with dve.If(kept > 0):
                    link(nc.vector.tensor_tensor(COMB[:], PROB[:], TOP[:], ALU.mult))
                    link(nc.vector.tensor_tensor(COMB[:], COMB[:], KEEP[:].unsqueeze(1).to_broadcast([P, NTT, NE]), ALU.mult))
                    link.done()
                    nc.vector.memset(ST[0][:], 0.0).then_inc(f["free"], 1)
                    nc.vector.memset(ST[1][:], 0.0).then_inc(f["expert_done"], 1)
                    dve.wait_ge(s["stored"], 16)
                    with dve.Fori(0, B) as b:
                        mean(dve, 0, b, f, B)
                        nc.vector.memset(ACC[:], 0.0).then_inc(f["cleared"], 1)
                        with dve.Fori(0, NE) as e:
                            k = b * NE + e
                            dve.wait_ge(f["cleared"], b + 1)
                            dve.wait_ge(f["expert_done"], k + 1)
                            dve.wait_ge(f["weights"], 64 * k + 64)
                            dve.wait_ge(f["outputs"], k + 1)
                            for m in range(4):
                                last = nc.vector.tensor_tensor(YB[:, 2 * m:2 * m + 2, :],
                                                               BK[1][m][:, :].rearrange("p (a b) -> p a b", a=2),
                                                               B2[:].unsqueeze(1).to_broadcast([P, 2, D]), ALU.add)
                            last.then_inc(c_expert, 1)
                            dve.wait_ge(c_expert, k + 1)
                            for i in range(NT):
                                wt = COMB[:, bass.ds(b * NT + i, 1), bass.ds(e, 1)].rearrange("p a c -> p (a c)")
                                last = nc.vector.scalar_tensor_tensor(out=ACC[:, i, :], in0=YB[:, i, :], scalar=wt,
                                                                      in1=ACC[:, i, :], op0=ALU.mult, op1=ALU.add)
                            last.then_inc(f["expert_done"], 1)
                        dve.wait_ge(f["expert_done"], b * NE + NE + 1)
                        dve.wait_ge(f["row"], 16 * b + 16)
                        nc.vector.tensor_tensor(ACC[:], ACC[:], GROW[:].unsqueeze(1).to_broadcast([P, NT, D]),
                                                ALU.mult).then_inc(f["gated"], 1)
                        dve.wait_ge(f["gated"], b + 1)
                        xb = X[:, bass.ds(b * NT, NT), :]
                        nc.vector.tensor_tensor(xb, xb, ACC[:], ALU.add).then_inc(f["free"], 1)


@contextmanager
def phase(nc):
    with ExitStack() as st:
        made = []

        def sem(name):
            made.append(st.enter_context(nc.semaphore(name)))
            return made[-1]

        yield sem
        with nc.Block() as block:
            @block.sync
            def _(sp):
                for s in made:
                    sp.sem_clear(s)


def program(nc, a, out):
    with ExitStack() as st:
        def sb(name, shape):
            return st.enter_context(nc.sbuf_tensor(name, shape, F32))

        g = {"X": sb("X", [P, B * NT, D]), "MOD": sb("MOD", [P, 2, 12, B]), "ident": sb("ident", [P, P]),
             "ident16": st.enter_context(nc.sbuf_tensor("ident16", [P, P], F16)),
             "mod_dram": nc.dram_tensor("mod_dram", [2, 12, B, P], F32).ap()}
        with phase(nc) as sem:
            modulation(nc, sem, g, [a["L0_c"], a["L1_c"]], [a["L0_wmod"], a["L1_wmod"]])
            softcap_attention(nc, sem, g, a["L0_attn_x"], a["L0_attn_w_q"], a["L0_attn_w_k"], a["L0_attn_w_v"],
                              a["L0_attn_w_o"])
        with phase(nc) as sem:
            routed_block(nc, sem, g, {n: a["L0_ffn_" + n]
                                      for n in ("w_router", "W_qkv", "W_out", "g1", "g2", "W1", "W2", "W3")})
        with phase(nc) as sem:
            time_mixing(nc, sem, g, {n: a["L1_attn_" + n] for n in ("time_decay", "time_first", "time_mix_k", "time_mix_v",
                                                                    "time_mix_r", "Wk", "Wv", "Wr", "Wo")})
            expert_layer(nc, sem, g, {n: a["L1_ffn_" + n] for n in ("gate_w", "W1", "b1", "W2", "b2")}, out)


_INS = ["L0_attn_x", "L0_attn_w_q", "L0_attn_w_k", "L0_attn_w_v", "L0_attn_w_o", "L0_ffn_w_router", "L0_ffn_W_qkv",
        "L0_ffn_W_out", "L0_ffn_g1", "L0_ffn_g2", "L0_ffn_W1", "L0_ffn_W2", "L0_ffn_W3", "L0_c", "L0_wmod",
        "L1_attn_time_decay", "L1_attn_time_first", "L1_attn_time_mix_k", "L1_attn_time_mix_v", "L1_attn_time_mix_r",
        "L1_attn_Wk", "L1_attn_Wv", "L1_attn_Wr", "L1_attn_Wo", "L1_ffn_gate_w", "L1_ffn_W1", "L1_ffn_b1",
        "L1_ffn_W2", "L1_ffn_b2", "L1_c", "L1_wmod"]


def kernel(**inputs):
    import numpy as _np
    import concourse.bacc as _bacc
    from concourse import mybir as _mybir
    from concourse.bass_utils import run_bass_kernel_spmd as _run

    nc = _bacc.Bacc("TRN2", target_bir_lowering=False, num_devices=1)
    arrays, args = {}, {}
    for name in _INS:
        a = _np.ascontiguousarray(inputs[name])
        arrays[f"in_{name}_dram"] = a
        args[name] = nc.dram_tensor(f"in_{name}_dram", a.shape, _mybir.dt.from_np(a.dtype), kind="ExternalInput").ap()
    out = nc.dram_tensor("out_0_dram", [B, T, D], _mybir.dt.float32, kind="ExternalOutput").ap()
    program(nc, args, out)
    r = _run(nc, [arrays], core_ids=[0])
    return r.results[0]["out_0_dram"]
```
